# Optimizing a Trainium2 kernel written in Bass

```python
import numpy as np
import jax
import jax.numpy as jnp

def _softmax(x, axis=-1):
    return jax.nn.softmax(x, axis=axis)

def _gelu(x):
    return jax.nn.gelu(x, approximate=True)

def _silu(x):
    return jax.nn.silu(x)

def _sigmoid(x):
    return jax.nn.sigmoid(x)

def _layernorm(x, axis=-1, eps=1e-05):
    m = jnp.mean(x, axis=axis, keepdims=True)
    v = jnp.var(x, axis=axis, keepdims=True)
    return (x - m) / jnp.sqrt(v + eps)

def _scatter_add(tgt, idx, src, axis=0):
    return tgt.at[idx].add(src)

def _segment_sum(src, seg, n):
    return jax.ops.segment_sum(src, seg, n)
kernel_name = 'mk_adaln_ffn_d4_seqx_r8_7c2352'

def setup_inputs(seed: int=0):
    np.random.seed(seed)
    _w = jnp.asarray

    def _rec_inputs():
        import jax
        import jax.numpy as jnp
        _rk = jax.random.key(seed)
        x = -0.0003929 + 0.9999 * jax.random.normal(jax.random.fold_in(_rk, 1), (32, 32, 512), jnp.float32)
        _lenS = 32 - jax.random.randint(jax.random.fold_in(_rk, 7), (32,), 0, max(1, 32 // 4) + 1, jnp.int32)
        _lenS2 = 32 - jax.random.randint(jax.random.fold_in(_rk, 8), (32,), 0, max(1, 32 // 4) + 1, jnp.int32)
        itok_B_78_3631 = jax.random.randint(jax.random.fold_in(_rk, 11), (32,), 78, 454, jnp.int32)
        itok_B_0_15 = jax.random.randint(jax.random.fold_in(_rk, 12), (32,), 0, 16, jnp.int32)
        itok_B_3_7 = jax.random.randint(jax.random.fold_in(_rk, 13), (32,), 3, 8, jnp.int32)
        itok_Bx16_0_63 = jax.random.randint(jax.random.fold_in(_rk, 14), (32, 16), 0, 64, jnp.int32)
        itok_B_207_1644 = jax.random.randint(jax.random.fold_in(_rk, 15), (32,), 207, 1645, jnp.int32)
        return (x, itok_B_78_3631, itok_B_0_15, itok_B_3_7, itok_Bx16_0_63, itok_B_207_1644)
    x, itok_B_78_3631, itok_B_0_15, itok_B_3_7, itok_Bx16_0_63, itok_B_207_1644 = _rec_inputs()

    def _L0_cond_setup():
        import math
        import jax, jax.numpy as jnp
        import numpy as np
        B, H, N, L = (16, 32, 64, 512)
        DT_MIN, DT_MAX = (0.001, 0.1)

        def _get_kernel(log_dt, C, log_A_real, A_imag, length):
            dt = jnp.exp(log_dt)
            Cc = C[..., 0] + 1j * C[..., 1]
            A = -jnp.exp(log_A_real) + 1j * A_imag
            dtA = A * dt[:, None]
            Ct = Cc * (jnp.exp(dtA) - 1.0) / A
            P = dtA[:, :, None] * jnp.arange(length, dtype=jnp.float32)
            K = 2.0 * jnp.einsum('hn,hnl->hl', Ct, jnp.exp(P)).real
            return K
        key = jax.random.key(seed)
        ks = jax.random.split(key, 5)
        u = jax.random.normal(ks[0], (B, H, L), dtype=jnp.float32)
        log_dt = jax.random.uniform(ks[1], (H,), dtype=jnp.float32) * (math.log(DT_MAX) - math.log(DT_MIN)) + math.log(DT_MIN)
        C = jax.random.normal(ks[2], (H, N, 2), dtype=jnp.float32)
        log_A_real = jnp.log(0.5 * jnp.ones((H, N), dtype=jnp.float32))
        A_imag = math.pi * jnp.broadcast_to(jnp.arange(N, dtype=jnp.float32), (H, N))
        D = jax.random.normal(ks[3], (H,), dtype=jnp.float32)
        length = jax.random.randint(ks[4], (B,), 1, L + 1, dtype=jnp.int32)
        return {'u': u, 'log_dt': log_dt, 'C': C, 'log_A_real': log_A_real, 'A_imag': A_imag, 'D': D, 'length': length}
    _L0_cond_all = _L0_cond_setup()
    _L0_cond_in = {k: v for k, v in _L0_cond_all.items() if k in ('log_dt', 'C', 'log_A_real', 'A_imag', 'D')}
    del _L0_cond_all

    def _L0_ffn_setup():
        import jax, jax.numpy as jnp
        import numpy as np
        NUM_EXPERTS = 4
        HIDDEN = 512
        RANK = 8
        ALPHA = 8.0
        SCALE = ALPHA / RANK
        key = jax.random.key(seed)
        ks = jax.random.split(key, 6)
        B, T, H, E, R = (4, 512, HIDDEN, NUM_EXPERTS, RANK)
        x = jax.random.normal(ks[0], (B, T, H), dtype=jnp.float32)
        W_up = jax.random.normal(ks[1], (H, H), dtype=jnp.float32) / np.sqrt(H)
        gate_w = jax.random.normal(ks[2], (E, H), dtype=jnp.float32) / np.sqrt(H)
        expert_bias = jnp.zeros((E,), dtype=jnp.float32)
        lora_A = jax.random.normal(ks[3], (E, R, H), dtype=jnp.float32) / np.sqrt(H)
        lora_B = jax.random.normal(ks[4], (E, H, R), dtype=jnp.float32) * 0.01
        return {'x': x, 'W_up': W_up, 'gate_w': gate_w, 'expert_bias': expert_bias, 'lora_A': lora_A, 'lora_B': lora_B}
    _L0_ffn_all = _L0_ffn_setup()
    _L0_ffn_in = {k: v for k, v in _L0_ffn_all.items() if k in ('W_up', 'gate_w', 'expert_bias', 'lora_A', 'lora_B')}
    del _L0_ffn_all

    def _L1_cond_setup():
        import jax, jax.numpy as jnp
        import numpy as np
        B, C, T = (64, 32, 512)
        S, D = (16, 32)
        key = jax.random.key(seed)
        k1, k2, k3 = jax.random.split(key, 3)
        x = jax.random.normal(k1, (B, C, T), dtype=jnp.float32)
        condition = jax.random.randint(k2, (B,), 0, S, dtype=jnp.int64)
        bound = float(np.sqrt(6.0 / C))
        weights = jax.random.uniform(k3, (S, C, D), dtype=jnp.float32, minval=-bound, maxval=bound)
        return {'x': x, 'condition': condition, 'weights': weights}
    _L1_cond_all = _L1_cond_setup()
    _L1_cond_in = {k: v for k, v in _L1_cond_all.items() if k in ('weights',)}
    del _L1_cond_all

    def _L1_ffn_setup():
        import jax, jax.numpy as jnp
        import numpy as np
        NUM_EXPERTS = 8
        RANK = 32
        ALPHA = 16.0
        TOP_K = 2
        TEMPERATURE = 1.0
        GAMMA = 0.5
        SOFT_TOPK_TEMP = 0.5
        N_GRAM = 2
        EPS = 1e-06
        key = jax.random.key(seed)
        ks = jax.random.split(key, 6)
        d_in, d_out = (512, 512)
        Bsz, T = (4, 256)
        x = jax.random.normal(ks[0], (Bsz, T, d_in), dtype=jnp.float32)
        W = jax.random.normal(ks[1], (d_out, d_in), dtype=jnp.float32) / np.sqrt(d_in)
        b = jax.random.normal(ks[2], (d_out,), dtype=jnp.float32) * 0.01
        A = jax.random.normal(ks[3], (d_in, RANK), dtype=jnp.float32) / np.sqrt(d_in)
        Bmat = jax.random.normal(ks[4], (RANK, d_out), dtype=jnp.float32) * 0.01
        LiMEs = jax.random.normal(ks[5], (NUM_EXPERTS, RANK), dtype=jnp.float32) * 0.1
        return {'x': x, 'W': W, 'b': b, 'A': A, 'Bmat': Bmat, 'LiMEs': LiMEs}
    _L1_ffn_all = _L1_ffn_setup()
    _L1_ffn_in = {k: v for k, v in _L1_ffn_all.items() if k in ('W', 'b', 'A', 'Bmat', 'LiMEs')}
    del _L1_ffn_all

    def _L2_cond_setup():
        import jax, jax.numpy as jnp
        import numpy as np
        RANK = 16
        ALPHA = 16.0
        SCALING = ALPHA / RANK
        N_ADAPTERS = 8
        IN_F = 512
        OUT_F = 512
        BATCH = 4
        SEQ = 256
        key = jax.random.key(seed)
        kx, ka, kb, ki = jax.random.split(key, 4)
        x = jax.random.normal(kx, (BATCH, SEQ, IN_F), dtype=jnp.float32)
        A = jax.random.normal(ka, (N_ADAPTERS, OUT_F, RANK), dtype=jnp.float32) * 0.02
        B = jax.random.normal(kb, (N_ADAPTERS, RANK, IN_F), dtype=jnp.float32) * 0.02
        adapter_ids = jax.random.randint(ki, (BATCH,), 0, N_ADAPTERS, dtype=jnp.int32)
        return {'x': x, 'A': A, 'B': B, 'adapter_ids': adapter_ids}
    _L2_cond_all = _L2_cond_setup()
    _L2_cond_in = {k: v for k, v in _L2_cond_all.items() if k in ('A', 'B')}
    del _L2_cond_all

    def _L2_ffn_setup():
        import jax, jax.numpy as jnp
        import numpy as np
        B, S, D, O, E, R = (2, 512, 512, 512, 8, 16)
        TOP_K = 2
        SCALING = 32.0 / 16.0
        key = jax.random.key(seed)
        k = jax.random.split(key, 6)
        x = jax.random.normal(k[0], (B, S, D), dtype=jnp.float32)
        W_base = jax.random.normal(k[1], (O, D), dtype=jnp.float32) * 0.02
        b_base = jax.random.normal(k[2], (O,), dtype=jnp.float32) * 0.02
        W_router = jax.random.normal(k[3], (E, D), dtype=jnp.float32) * 0.01
        lora_A = jax.random.normal(k[4], (E, R, D), dtype=jnp.float32) * (1.0 / np.sqrt(D))
        lora_B = jax.random.normal(k[5], (E, O, R), dtype=jnp.float32) * 0.02
        return {'x': x, 'W_base': W_base, 'b_base': b_base, 'W_router': W_router, 'lora_A': lora_A, 'lora_B': lora_B}
    _L2_ffn_all = _L2_ffn_setup()
    _L2_ffn_in = {k: v for k, v in _L2_ffn_all.items() if k in ('W_base', 'b_base', 'W_router', 'lora_A', 'lora_B')}
    del _L2_ffn_all

    def _L3_cond_setup():
        import jax, jax.numpy as jnp
        import numpy as np
        B, S, HID = (4, 128, 512)
        D, HQ, HK = (128, 32, 8)
        PAGES, PSIZE, NPP = (64, 32, 16)
        THETA = 10000.0
        EPS = 1e-06
        SCALE = 1.0 / float(np.sqrt(D))

        def _rmsnorm(t, w):
            var = jnp.mean(t * t, axis=-1, keepdims=True)
            return t * jax.lax.rsqrt(var + EPS) * w

        def _rope(t, pos):
            inv_freq = 1.0 / THETA ** (jnp.arange(0, D, 2, dtype=jnp.float32) / D)
            freqs = pos[..., None].astype(jnp.float32) * inv_freq
            cos = jnp.cos(freqs)[:, :, None, :]
            sin = jnp.sin(freqs)[:, :, None, :]
            t1, t2 = (t[..., :D // 2], t[..., D // 2:])
            return jnp.concatenate([t1 * cos - t2 * sin, t2 * cos + t1 * sin], axis=-1)
        key = jax.random.key(seed)
        ks = jax.random.split(key, 10)
        x = jax.random.normal(ks[0], (B, S, HID), jnp.float32)
        Wq = jax.random.normal(ks[1], (HQ * D, HID), jnp.float32) * 0.02
        Wk = jax.random.normal(ks[2], (HK * D, HID), jnp.float32) * 0.02
        Wv = jax.random.normal(ks[3], (HK * D, HID), jnp.float32) * 0.02
        Wo = jax.random.normal(ks[4], (HID, HQ * D), jnp.float32) * 0.02
        q_norm_w = jax.random.uniform(ks[5], (D,), jnp.float32)
        k_norm_w = jax.random.uniform(ks[6], (D,), jnp.float32)
        k_cache = jax.random.normal(ks[7], (PAGES, PSIZE, HK, D), jnp.float32)
        v_cache = jax.random.normal(ks[8], (PAGES, PSIZE, HK, D), jnp.float32)
        block_table = jnp.arange(B * NPP, dtype=jnp.int32).reshape(B, NPP)
        cache_seqlens = jax.random.randint(ks[9], (B,), 0, 475).astype(jnp.int32)
        return dict(x=x, Wq=Wq, Wk=Wk, Wv=Wv, Wo=Wo, q_norm_w=q_norm_w, k_norm_w=k_norm_w, k_cache=k_cache, v_cache=v_cache, block_table=block_table, cache_seqlens=cache_seqlens)
    _L3_cond_all = _L3_cond_setup()
    _L3_cond_in = {k: v for k, v in _L3_cond_all.items() if k in ('Wq', 'Wk', 'Wv', 'Wo', 'q_norm_w', 'k_norm_w', 'k_cache', 'v_cache')}
    del _L3_cond_all

    def _L3_ffn_setup():
        import jax, jax.numpy as jnp
        import numpy as np
        BATCH, SEQ, D = (2, 256, 512)
        K, TOPK, RANK = (64, 16, 16)
        ALPHA = 32.0
        SCALING = ALPHA / RANK
        key = jax.random.key(seed)
        k1, k2, k3, k4 = jax.random.split(key, 4)
        x = jax.random.normal(k1, (BATCH, SEQ, D), dtype=jnp.float32)
        A = jax.random.normal(k2, (K, RANK, D), dtype=jnp.float32) * 0.02
        B = jax.random.normal(k3, (K, D, RANK), dtype=jnp.float32) * 0.02
        Wr = jax.random.normal(k4, (K, D), dtype=jnp.float32) * 0.02
        return {'x': x, 'A': A, 'B': B, 'Wr': Wr}
    _L3_ffn_all = _L3_ffn_setup()
    _L3_ffn_in = {k: v for k, v in _L3_ffn_all.items() if k in ('A', 'B', 'Wr')}
    del _L3_ffn_all
    return {'x': x, 'itok_B_78_3631': itok_B_78_3631, 'itok_B_0_15': itok_B_0_15, 'itok_B_3_7': itok_B_3_7, 'itok_Bx16_0_63': itok_Bx16_0_63, 'itok_B_207_1644': itok_B_207_1644, 'L0_cond_log_dt': _L0_cond_in['log_dt'], 'L0_cond_C': _L0_cond_in['C'], 'L0_cond_log_A_real': _L0_cond_in['log_A_real'], 'L0_cond_A_imag': _L0_cond_in['A_imag'], 'L0_cond_D': _L0_cond_in['D'], 'L0_ffn_W_up': _L0_ffn_in['W_up'], 'L0_ffn_gate_w': _L0_ffn_in['gate_w'], 'L0_ffn_expert_bias': _L0_ffn_in['expert_bias'], 'L0_ffn_lora_A': _L0_ffn_in['lora_A'], 'L0_ffn_lora_B': _L0_ffn_in['lora_B'], 'L1_cond_weights': _L1_cond_in['weights'], 'L1_ffn_W': _L1_ffn_in['W'], 'L1_ffn_b': _L1_ffn_in['b'], 'L1_ffn_A': _L1_ffn_in['A'], 'L1_ffn_Bmat': _L1_ffn_in['Bmat'], 'L1_ffn_LiMEs': _L1_ffn_in['LiMEs'], 'L2_cond_A': _L2_cond_in['A'], 'L2_cond_B': _L2_cond_in['B'], 'L2_ffn_W_base': _L2_ffn_in['W_base'], 'L2_ffn_b_base': _L2_ffn_in['b_base'], 'L2_ffn_W_router': _L2_ffn_in['W_router'], 'L2_ffn_lora_A': _L2_ffn_in['lora_A'], 'L2_ffn_lora_B': _L2_ffn_in['lora_B'], 'L3_cond_Wq': _L3_cond_in['Wq'], 'L3_cond_Wk': _L3_cond_in['Wk'], 'L3_cond_Wv': _L3_cond_in['Wv'], 'L3_cond_Wo': _L3_cond_in['Wo'], 'L3_cond_q_norm_w': _L3_cond_in['q_norm_w'], 'L3_cond_k_norm_w': _L3_cond_in['k_norm_w'], 'L3_cond_k_cache': _L3_cond_in['k_cache'], 'L3_cond_v_cache': _L3_cond_in['v_cache'], 'L3_ffn_A': _L3_ffn_in['A'], 'L3_ffn_B': _L3_ffn_in['B'], 'L3_ffn_Wr': _L3_ffn_in['Wr']}

def reference(x, itok_B_78_3631, itok_B_0_15, itok_B_3_7, itok_Bx16_0_63, itok_B_207_1644, L0_cond_log_dt, L0_cond_C, L0_cond_log_A_real, L0_cond_A_imag, L0_cond_D, L0_ffn_W_up, L0_ffn_gate_w, L0_ffn_expert_bias, L0_ffn_lora_A, L0_ffn_lora_B, L1_cond_weights, L1_ffn_W, L1_ffn_b, L1_ffn_A, L1_ffn_Bmat, L1_ffn_LiMEs, L2_cond_A, L2_cond_B, L2_ffn_W_base, L2_ffn_b_base, L2_ffn_W_router, L2_ffn_lora_A, L2_ffn_lora_B, L3_cond_Wq, L3_cond_Wk, L3_cond_Wv, L3_cond_Wo, L3_cond_q_norm_w, L3_cond_k_norm_w, L3_cond_k_cache, L3_cond_v_cache, L3_ffn_A, L3_ffn_B, L3_ffn_Wr):
    import jax
    import jax.numpy as jnp

    def _L0_cond_ref(u, log_dt, C, log_A_real, A_imag, D, length):
        import math
        import jax, jax.numpy as jnp
        import numpy as np
        B, H, N, L = (16, 32, 64, 512)
        DT_MIN, DT_MAX = (0.001, 0.1)

        def _get_kernel(log_dt, C, log_A_real, A_imag, length):
            dt = jnp.exp(log_dt)
            Cc = C[..., 0] + 1j * C[..., 1]
            A = -jnp.exp(log_A_real) + 1j * A_imag
            dtA = A * dt[:, None]
            Ct = Cc * (jnp.exp(dtA) - 1.0) / A
            P = dtA[:, :, None] * jnp.arange(length, dtype=jnp.float32)
            K = 2.0 * jnp.einsum('hn,hnl->hl', Ct, jnp.exp(P)).real
            return K
        Bq, Hq, Lq = u.shape
        K = _get_kernel(log_dt, C, log_A_real, A_imag, Lq)
        n = 2 * Lq
        kf = jnp.fft.rfft(K, n=n)
        uf = jnp.fft.rfft(u, n=n)
        y = jnp.fft.irfft(uf * kf[None], n=n)[..., :Lq]
        y = y + u * D[:, None]
        mask = (jnp.arange(Lq)[None, :] < length[:, None]).astype(u.dtype)
        return y * mask[:, None, :]

    def _L0_ffn_ref(x, W_up, gate_w, expert_bias, lora_A, lora_B):
        import jax, jax.numpy as jnp
        import numpy as np
        NUM_EXPERTS = 4
        HIDDEN = 512
        RANK = 8
        ALPHA = 8.0
        SCALE = ALPHA / RANK
        B, T, H = x.shape
        E = gate_w.shape[0]
        x_flat = x.reshape(-1, H)
        logits = x_flat @ gate_w.T + expert_bias
        top1 = jnp.argmax(logits, axis=-1)
        one_hot = jax.nn.one_hot(top1, E, dtype=x_flat.dtype)
        base_out = jnp.einsum('bth,oh->bto', x, W_up)
        z = jnp.einsum('nh,erh->ner', x_flat, lora_A)
        d = jnp.einsum('ner,ehr->neh', z, lora_B) * SCALE
        delta = jnp.einsum('neh,ne->nh', d, one_hot)
        return base_out + delta.reshape(B, T, H)

    def _L1_cond_ref(x, condition, weights):
        import jax, jax.numpy as jnp
        import numpy as np
        B, C, T = (64, 32, 512)
        S, D = (16, 32)
        W = weights[condition]
        return jnp.einsum('bct,bcd->bdt', x, W)

    def _L1_ffn_ref(x, W, b, A, Bmat, LiMEs):
        import jax, jax.numpy as jnp
        import numpy as np
        NUM_EXPERTS = 8
        RANK = 32
        ALPHA = 16.0
        TOP_K = 2
        TEMPERATURE = 1.0
        GAMMA = 0.5
        SOFT_TOPK_TEMP = 0.5
        N_GRAM = 2
        EPS = 1e-06
        Bsz, T, d_in = x.shape
        E = LiMEs.shape[0]
        scaling = ALPHA / RANK
        H = jnp.einsum('btd,od->bto', x, W) + b
        z = jnp.einsum('btd,dr->btr', x, A)
        anchors = jnp.arange(N_GRAM - 1, T, N_GRAM)
        H_slice = H[:, anchors, :E]
        delta_slice = jnp.einsum('bar,er->bae', z[:, anchors], LiMEs)
        H_scale = jnp.maximum(jnp.max(jnp.abs(H_slice)), EPS)
        d_scale = jnp.maximum(jnp.max(jnp.abs(delta_slice)), EPS)
        logits = ((1.0 - GAMMA) * (H_slice / H_scale) + GAMMA * (delta_slice / d_scale)) / TEMPERATURE
        probs = jax.nn.softmax(logits, axis=-1)
        topk_vals, _ = jax.lax.top_k(probs, TOP_K)
        thresh = topk_vals[..., -1:]
        mask = jax.nn.sigmoid((probs - thresh) / SOFT_TOPK_TEMP)
        weights = probs * mask
        weights = weights / (jnp.sum(weights, axis=-1, keepdims=True) + 1e-09)
        weights_full = jnp.repeat(weights, N_GRAM, axis=1)
        p_mix = jnp.einsum('bte,er->btr', weights_full, LiMEs)
        delta = jnp.einsum('btr,ro->bto', z * p_mix, Bmat) * scaling
        return H + delta

    def _L2_cond_ref(x, A, B, adapter_ids):
        import jax, jax.numpy as jnp
        import numpy as np
        RANK = 16
        ALPHA = 16.0
        SCALING = ALPHA / RANK
        N_ADAPTERS = 8
        IN_F = 512
        OUT_F = 512
        BATCH = 4
        SEQ = 256
        B_sel = B[adapter_ids]
        A_sel = A[adapter_ids]
        Bx = jnp.einsum('bni,bri->bnr', x, B_sel)
        out = jnp.einsum('bnr,bor->bno', Bx, A_sel)
        return out * SCALING

    def _L2_ffn_ref(x, W_base, b_base, W_router, lora_A, lora_B):
        import jax, jax.numpy as jnp
        import numpy as np
        B, S, D, O, E, R = (2, 512, 512, 512, 8, 16)
        TOP_K = 2
        SCALING = 32.0 / 16.0
        d = x.shape[-1]
        n_experts = W_router.shape[0]
        xf = x.reshape(-1, d)
        logits = xf @ W_router.T
        probs = jax.nn.softmax(logits, axis=-1)
        topk_p, topk_i = jax.lax.top_k(probs, TOP_K)
        topk_p = topk_p / jnp.sum(topk_p, axis=-1, keepdims=True)
        w = jnp.sum(jax.nn.one_hot(topk_i, n_experts, dtype=xf.dtype) * topk_p[..., None], axis=1)
        h = jnp.einsum('td,erd->ter', xf, lora_A)
        lora_out = jnp.einsum('ter,eor,te->to', h, lora_B, w) * SCALING
        base = x @ W_base.T + b_base
        return base + lora_out.reshape(x.shape[:-1] + (W_base.shape[0],))

    def _L3_cond_ref(x, Wq, Wk, Wv, Wo, q_norm_w, k_norm_w, k_cache, v_cache, block_table, cache_seqlens):
        import jax, jax.numpy as jnp
        import numpy as np
        B, S, HID = (4, 128, 512)
        D, HQ, HK = (128, 32, 8)
        PAGES, PSIZE, NPP = (64, 32, 16)
        THETA = 10000.0
        EPS = 1e-06
        SCALE = 1.0 / float(np.sqrt(D))

        def _rmsnorm(t, w):
            var = jnp.mean(t * t, axis=-1, keepdims=True)
            return t * jax.lax.rsqrt(var + EPS) * w

        def _rope(t, pos):
            inv_freq = 1.0 / THETA ** (jnp.arange(0, D, 2, dtype=jnp.float32) / D)
            freqs = pos[..., None].astype(jnp.float32) * inv_freq
            cos = jnp.cos(freqs)[:, :, None, :]
            sin = jnp.sin(freqs)[:, :, None, :]
            t1, t2 = (t[..., :D // 2], t[..., D // 2:])
            return jnp.concatenate([t1 * cos - t2 * sin, t2 * cos + t1 * sin], axis=-1)
        bsz, seqlen, _ = x.shape
        q = jnp.einsum('bsd,ed->bse', x, Wq).reshape(bsz, seqlen, HQ, D)
        k = jnp.einsum('bsd,ed->bse', x, Wk).reshape(bsz, seqlen, HK, D)
        v = jnp.einsum('bsd,ed->bse', x, Wv).reshape(bsz, seqlen, HK, D)
        q = _rmsnorm(q, q_norm_w)
        k = _rmsnorm(k, k_norm_w)
        pos = cache_seqlens[:, None] + jnp.arange(seqlen)[None, :]
        q = _rope(q, pos)
        k = _rope(k, pos)
        L = NPP * PSIZE
        kc = k_cache[block_table].reshape(bsz, L, HK, D)
        vc = v_cache[block_table].reshape(bsz, L, HK, D)
        k_all = jnp.concatenate([kc, k], axis=1)
        v_all = jnp.concatenate([vc, v], axis=1)
        valid_c = jnp.arange(L)[None, :] < cache_seqlens[:, None]
        valid = jnp.concatenate([valid_c, jnp.ones((bsz, seqlen), dtype=bool)], axis=1)
        rep = HQ // HK
        k_all = jnp.repeat(k_all, rep, axis=2)
        v_all = jnp.repeat(v_all, rep, axis=2)
        scores = jnp.einsum('bqhd,bkhd->bhqk', q, k_all) * SCALE
        scores = jnp.where(valid[:, None, None, :], scores, -1e+30)
        probs = jax.nn.softmax(scores, axis=-1)
        o = jnp.einsum('bhqk,bkhd->bqhd', probs, v_all)
        o = o.reshape(bsz, seqlen, HQ * D)
        return jnp.einsum('bse,de->bsd', o, Wo)

    def _L3_ffn_ref(x, A, B, Wr):
        import jax, jax.numpy as jnp
        import numpy as np
        BATCH, SEQ, D = (2, 256, 512)
        K, TOPK, RANK = (64, 16, 16)
        ALPHA = 32.0
        SCALING = ALPHA / RANK
        prefix = x.shape[:-1]
        xf = x.reshape(-1, x.shape[-1])
        N = xf.shape[0]
        scores = xf @ Wr.T
        top_vals, top_idx = jax.lax.top_k(scores, TOPK)
        gates = jax.nn.softmax(top_vals, axis=-1)
        G = jnp.zeros((N, K), xf.dtype).at[jnp.arange(N)[:, None], top_idx].set(gates)
        h = jnp.einsum('nd,krd->nkr', xf, A)
        out = jnp.einsum('nkr,kdr->nd', h * G[:, :, None], B)
        return (out * SCALING).reshape(*prefix, -1)
    x = x + _L0_ffn_ref(_L0_cond_ref(x, L0_cond_log_dt, L0_cond_C, L0_cond_log_A_real, L0_cond_A_imag, L0_cond_D, itok_B_78_3631), L0_ffn_W_up, L0_ffn_gate_w, L0_ffn_expert_bias, L0_ffn_lora_A, L0_ffn_lora_B)
    x = x + _L1_ffn_ref(_L1_cond_ref(x, itok_B_0_15, L1_cond_weights), L1_ffn_W, L1_ffn_b, L1_ffn_A, L1_ffn_Bmat, L1_ffn_LiMEs)
    x = x + _L2_ffn_ref(_L2_cond_ref(x, L2_cond_A, L2_cond_B, itok_B_3_7), L2_ffn_W_base, L2_ffn_b_base, L2_ffn_W_router, L2_ffn_lora_A, L2_ffn_lora_B)
    x = x + _L3_ffn_ref(_L3_cond_ref(x, L3_cond_Wq, L3_cond_Wk, L3_cond_Wv, L3_cond_Wo, L3_cond_q_norm_w, L3_cond_k_norm_w, L3_cond_k_cache, L3_cond_v_cache, itok_Bx16_0_63, itok_B_207_1644), L3_ffn_A, L3_ffn_B, L3_ffn_Wr)
    return x

_drawn_inputs = setup_inputs


def setup_inputs(seed=0):
    import zlib

    import numpy as np

    out = dict(_drawn_inputs(seed))
    spreads = {'L0_cond_log_A_real': (-0.6931471824645996, 0.2), 'L0_ffn_expert_bias': (0.0, 0.8)}
    factors = {'L0_ffn_gate_w': 3.273,
     'L0_ffn_lora_A': 2.805,
     'L0_ffn_lora_B': 2.829,
     'L1_ffn_b': 8.0,
     'L1_ffn_A': 8.0,
     'L1_ffn_Bmat': 8.0,
     'L1_ffn_LiMEs': 8.0,
     'L2_cond_A': 3.376,
     'L2_cond_B': 3.402,
     'L2_ffn_W_base': 3.453,
     'L2_ffn_b_base': 8.0,
     'L2_ffn_W_router': 8.0,
     'L2_ffn_lora_A': 8.0,
     'L2_ffn_lora_B': 8.0,
     'L3_cond_Wq': 8.0,
     'L3_cond_Wk': 8.0,
     'L3_cond_Wv': 8.0,
     'L3_cond_Wo': 8.0,
     'L3_cond_q_norm_w': 8.0,
     'L3_cond_k_norm_w': 8.0,
     'L3_cond_k_cache': 8.0,
     'L3_cond_v_cache': 8.0,
     'L3_ffn_A': 8.0,
     'L3_ffn_B': 8.0,
     'L3_ffn_Wr': 8.0}
    for name, (base, spread) in spreads.items():
        noise = np.random.default_rng([zlib.crc32(name.encode()), seed]).standard_normal(out[name].shape)
        drawn = base * np.exp(spread * noise) if base else spread * noise
        out[name] = jnp.asarray(drawn.astype(out[name].dtype))
    for name, factor in factors.items():
        out[name] = (out[name] * factor).astype(out[name].dtype)
    return out
```

```python
import math
from contextlib import ExitStack

import numpy as np
import concourse.bass as bass
from concourse import mybir

F32 = mybir.dt.float32
F32R = mybir.dt.float32r
I32 = mybir.dt.int32
U32 = mybir.dt.uint32
ALU = mybir.AluOpType
ACT = mybir.ActivationFunctionType
AX = mybir.AxisListType

P = 128
NB, NS, D = 32, 32, 512
TOK = NB * NS
TILES = TOK // P
KC = D // P
BPT = P // NS

MODES = 64
A_STEP, A_N, B_N = 32, 16, 32
KPAD = 640
E0, R0 = 4, 8
E1, R1 = 8, 32
AD2, RC2 = 8, 16
E2, R2 = 8, 16
HD, HQ, HK = 128, 32, 8
G = HQ // HK
PAGES, PS, NPP = 64, 32, 16
CL = NPP * PS
KL = CL + NS
E3, TOP3, R3 = 64, 16, 16
SCALE = 1.0 / math.sqrt(HD)
NEG = -1e30

MAGIC = 12582912.0
TWO_PI_1 = 6.28125
TWO_PI_2 = float(np.uint32(np.float32(2 * math.pi - 6.28125).view(np.uint32) & np.uint32(0xFFFFF000)).view(np.float32))
TWO_PI_3 = 2 * math.pi - TWO_PI_1 - TWO_PI_2
INV_2PI = 1.0 / (2 * math.pi)
PI_IN = float(np.nextafter(np.float32(math.pi), np.float32(0)))

CONST_PARTS = [("ident", P), ("iota8", 8), ("block4", BPT), ("cmod", 1), ("bvals", B_N), ("avals", A_N),
               ("phase", 1), ("phase2", 1), ("halfpi", 1), ("sign", 1), ("lpos", KC), ("adapter", 1), ("smod", 1),
               ("invf", HD // 2), ("sinsign", HD), ("iota512", CL), ("experts", E3), ("eps", 1)]
CONST_AT, _n = {}, 0
for _name, _len in CONST_PARTS:
    CONST_AT[_name] = (_n, _n + _len)
    _n += _len
CONST_N = _n


def constants():
    p = np.arange(P, dtype=np.float32)
    c = np.zeros((P, CONST_N), np.float32)

    def put(name, value):
        a, b = CONST_AT[name]
        c[:, a:b] = value

    put("ident", np.eye(P))
    put("iota8", np.arange(8)[None])
    put("block4", (p[:, None] // NS == np.arange(BPT)[None]))
    put("cmod", (p % NS)[:, None])
    put("bvals", np.arange(B_N)[None])
    put("avals", (A_STEP * np.arange(A_N))[None])
    put("phase", np.where(p < MODES, np.float32(math.pi / 2), 0)[:, None])
    put("phase2", np.where(p < MODES, np.float32(math.pi), np.float32(math.pi / 2))[:, None])
    put("halfpi", np.float32(math.pi / 2))
    put("sign", np.where(p < MODES, 1, -1)[:, None])
    put("lpos", p[:, None] + P * np.arange(KC)[None])
    put("adapter", (p // RC2)[:, None])
    put("smod", (p % NS)[:, None])
    put("invf", (np.float32(1) / np.float32(10000.0) ** (np.arange(0, HD, 2, dtype=np.float32) / np.float32(HD)))[None])
    put("sinsign", np.where(np.arange(HD) < HD // 2, -1, 1)[None])
    put("iota512", np.arange(CL)[None])
    put("eps", 1e-6)
    put("experts", np.arange(E3)[None])
    return c


class Link:

    def __init__(self, eng, sem, base=0):
        self.eng, self.sem, self.base, self.n = eng, sem, base, 0

    def __call__(self, ins, passed=None):
        self.n += 1
        ins.then_inc(self.sem, 1)
        if passed:
            lone_wait(self.eng, self.sem, self.base + self.n, passed)
        else:
            self.eng.wait_ge(self.sem, self.base + self.n)


def lone_wait(eng, sem, value, passed):
    eng.wait_ge(sem, value)
    eng.sem_inc(passed, 1)


def bc(ap, axis, n):
    shape = list(ap.shape)
    shape.insert(axis, n)
    return ap.unsqueeze(axis).broadcast_to(shape)


def reduce_angles(link, dve, theta, turns, phases):
    for (a, b), ph, in_turns in phases:
        if ph is None:
            link(dve.tensor_scalar(turns[:, a:b], theta[:, a:b], INV_2PI, None, ALU.mult))
        else:
            link(dve.tensor_scalar(turns[:, a:b], theta[:, a:b], ph, INV_2PI, ALU.add, ALU.mult))
    link(dve.tensor_scalar(turns, turns, MAGIC, None, ALU.add))
    link(dve.tensor_scalar(turns, turns, MAGIC, None, ALU.subtract))
    for part in (TWO_PI_1, TWO_PI_2, TWO_PI_3):
        link(dve.scalar_tensor_tensor(out=theta, in0=turns, scalar=-part, in1=theta, op0=ALU.mult, op1=ALU.add))
    for (a, b), ph, _ in phases:
        if ph is not None:
            link(dve.tensor_scalar(theta[:, a:b], theta[:, a:b], ph, None, ALU.add))
    link(dve.tensor_scalar(theta, theta, PI_IN, -PI_IN, ALU.min, ALU.max))


class Core:

    def __init__(self, nc, ctx, dram):
        self.nc, self.ctx, self.dram = nc, ctx, dram
        self.sems = []

    def sb(self, name, shape, dt=F32, ctx=None):
        return (ctx or self.ctx).enter_context(self.nc.sbuf_tensor(name, shape, dt))

    def sem(self, name):
        self.sems.append(self.nc.alloc_semaphore(name=name))
        return self.sems[-1]

    def end_phase(self, ctx):
        ctx.close()
        self.nc.clear_and_free_semaphores(self.sems)
        self.nc.all_engine_barrier()
        self.sems = []

    def c(self, name):
        a, b = CONST_AT[name]
        return self.cst[:, a:b]


def s4_phase(k):
    nc, dram = k.nc, k.dram
    ctx = ExitStack()
    sb = lambda name, shape, dt=F32: k.sb(name, shape, dt, ctx)
    NY, NX = NS * B_N, NS * A_N
    NT = NY + 2 * NX + 3 * NS
    s4in = sb("s4in", [P, 5, NS])
    drow = sb("drow", [1, NS])
    len_i = sb("len_i", [P, NB], I32)
    len_f = sb("len_f", [P, NB])
    lmask = sb("lmask", [P, KC, NB])
    xr = sb("xr", [P, KC, NS, NB])
    th = sb("th", [P, 2, NS])
    w1 = sb("w1", [P, 2, NS])
    w2 = sb("w2", [P, 2, NS])
    dm = sb("dm", [P, 2, NS])
    dta = sb("dta", [P, 2, NS])
    sm = sb("sm", [P, 12, NS])
    theta = sb("theta", [P, NT])
    turns = sb("turns", [P, NT])
    trig = sb("trig", [P, NT])
    mag = sb("mag", [P, NY + NX])
    ey = sb("ey", [P, NS, B_N])
    ex1 = sb("ex1", [P, NS, A_N])
    ex2 = sb("ex2", [P, NS, A_N])
    xx = sb("xx", [P, NS, A_N])
    ksb = sb("ksb", [A_N, NS * B_N])
    zeros = sb("zeros", [NS, P])
    RING = 4
    toep = sb("toep", [P, RING, D])
    kps = ctx.enter_context(nc.psum_tensor("kps", [A_N, 2, 512], F32))
    yps = ctx.enter_context(nc.psum_tensor("yps", [P, RING, 512], F32))
    const_in, s4_in, u_in, zero_made, kpad_out = (k.sem(n) for n in ("const_in", "s4_in", "u_in", "zero_made", "kpad_out"))
    s4_steps, tanh_done, half_ready, angle_ready, trig_done, expo_ready, mag_done = (
        k.sem(n) for n in ("s4_steps", "tanh_done", "half_ready", "angle_ready", "trig_done", "expo_ready", "mag_done"))
    xy_ready, kern_done, kern_kept = (k.sem(n) for n in ("xy_ready", "kern_done", "kern_kept"))
    toep_in = [k.sem(f"toep_in{s}") for s in range(RING)]
    conv_done, conv_kept = k.sem("conv_done"), k.sem("conv_kept")

    kpad = dram["kpad"]
    kpad_dst = kpad[:, P:].rearrange("h (a b) -> a h b", b=B_N)

    with nc.Block() as block:
        @block.sync
        def _(sp):
            sp.dma_start(s4in[:], dram["s4in"]).then_inc(s4_in, 16)
            sp.dma_start(k.cst[:], dram["cst"]).then_inc(const_in, 16)
            sp.dma_start(drow[:], dram["L0_cond_D"].unsqueeze(0)).then_inc(s4_in, 16)
            sp.dma_start(len_i[:], dram["len_b"]).then_inc(s4_in, 16)
            sp.dma_start(xr[:], dram["x_rev"]).then_inc(u_in, 16)
            sp.wait_ge(zero_made, 1)
            sp.dma_start(kpad[:, 0:P], zeros[:]).then_inc(kpad_out, 16)
            sp.wait_ge(kern_kept, 1)
            sp.dma_start(kpad_dst, ksb[:].rearrange("a (h b) -> a h b", b=B_N)).then_inc(kpad_out, 16)
            sp.wait_ge(kpad_out, 32)
            for s in range(RING):
                sp.dma_start(toep[:, s, :], dram["toeplitz"](s)).then_inc(toep_in[s], 16)
            with sp.Fori(1, NS // RING) as i:
                for s in range(RING):
                    sp.wait_ge(conv_done, i * RING + s - RING + 1)
                    sp.dma_start(toep[:, s, :], dram["toeplitz"](i * RING + s)).then_inc(toep_in[s], 16)

        @block.scalar
        def _(act):
            act.wait_ge(s4_in, 48)
            act.activation(th[:], s4in[:, 0:2, :], ACT.Tanh, scale=1.0 / 16).then_inc(tanh_done, 1)
            act.wait_ge(half_ready, 1)
            act.activation(sm[:, 0, :], dta[:, 0, :], ACT.Tanh, scale=0.5).then_inc(tanh_done, 1)
            act.wait_ge(expo_ready, 1)
            act.activation(mag[:], mag[:], ACT.Exp).then_inc(mag_done, 1)
            act.wait_ge(angle_ready, 1)
            act.activation(trig[:], theta[:], ACT.Sin).then_inc(trig_done, 1)

        @block.vector
        def _(dve):
            link = Link(dve, s4_steps)
            TS, TT, STT = dve.tensor_scalar, dve.tensor_tensor, dve.scalar_tensor_tensor
            TT_ = lambda out, a, b, op: link(TT(out, a, b, op))
            dve.memset(zeros[:], 0.0).then_inc(zero_made, 1)
            dve.wait_ge(tanh_done, 1)
            link(TS(w1[:], th[:], -1.0, 1.0, ALU.mult, ALU.add))
            link(dve.reciprocal(w2[:], w1[:]))
            link(STT(out=w1[:], in0=th[:], scalar=1.0, in1=w2[:], op0=ALU.add, op1=ALU.mult))
            TT_(w2[:], w1[:], w1[:], ALU.mult)
            TT_(w1[:], w2[:], w2[:], ALU.mult)
            TT_(dm[:], w1[:], w1[:], ALU.mult)
            dt, mre, im = dm[:, 0, :], dm[:, 1, :], s4in[:, 2, :]
            cr, ci = s4in[:, 3, :], s4in[:, 4, :]
            link(STT(out=dta[:, 0, :], in0=mre, scalar=-1.0, in1=dt, op0=ALU.mult, op1=ALU.mult))
            TT(dta[:, 1, :], im, dt, ALU.mult).then_inc(half_ready, 1)
            dve.wait_ge(const_in, 16)
            dve.wait_ge(half_ready, 1)
            magy = mag[:, 0:NY].rearrange("p (h b) -> p h b", b=B_N)
            magx = mag[:, NY:].rearrange("p (h a) -> p h a", a=A_N)
            bv, av = bc(k.c("bvals"), 1, NS), bc(k.c("avals"), 1, NS)
            link(TT(magy, bc(dta[:, 0, :], 2, B_N), bv, ALU.mult))
            TT(magx, bc(dta[:, 0, :], 2, A_N), av, ALU.mult).then_inc(expo_ready, 1)
            thy = theta[:, 0:NY].rearrange("p (h b) -> p h b", b=B_N)
            thx = [theta[:, NY + j * NX:NY + (j + 1) * NX].rearrange("p (h a) -> p h a", a=A_N) for j in range(2)]
            last = NY + 2 * NX
            link(TT(thy, bc(dta[:, 1, :], 2, B_N), bv, ALU.mult))
            for j in range(2):
                link(TT(thx[j], bc(dta[:, 1, :], 2, A_N), av, ALU.mult))
            link(dve.tensor_copy(theta[:, last:last + 2 * NS].rearrange("p (j h) -> p j h", j=2), bc(dta[:, 1, :], 1, 2)))
            link(TS(theta[:, last + 2 * NS:], dta[:, 1, :], 0.5, None, ALU.mult))
            reduce_angles(link, dve, theta[:], turns[:], [
                ((0, NY + NX), k.c("phase"), 0), ((NY + NX, last), k.c("phase2"), 0),
                ((last, last + NS), k.c("halfpi"), 0), ((last + NS, NT), None, 0)])
            dve.sem_inc(angle_ready, 1)
            dve.wait_ge(tanh_done, 2)
            S = lambda j: sm[:, j, :]
            link(TS(S(1), S(0), -1.0, 1.0, ALU.mult, ALU.add))
            link(dve.reciprocal(S(2), S(1)))
            link(STT(out=S(3), in0=S(0), scalar=2.0, in1=S(2), op0=ALU.mult, op1=ALU.mult))
            dve.wait_ge(trig_done, 1)
            cosb, sinb, sinh = (trig[:, last + j * NS:last + (j + 1) * NS] for j in range(3))
            link(STT(out=S(4), in0=sinh, scalar=-2.0, in1=sinh, op0=ALU.mult, op1=ALU.mult))
            TT_(S(5), S(3), cosb, ALU.mult)
            TT_(S(4), S(4), S(5), ALU.add)
            link(STT(out=S(5), in0=S(3), scalar=1.0, in1=sinb, op0=ALU.add, op1=ALU.mult))
            TT_(S(6), cr, S(4), ALU.mult)
            TT_(S(7), ci, S(5), ALU.mult)
            TT_(S(6), S(6), S(7), ALU.subtract)
            TT_(S(7), cr, S(5), ALU.mult)
            TT_(S(8), ci, S(4), ALU.mult)
            TT_(S(7), S(7), S(8), ALU.add)
            TT_(S(8), mre, mre, ALU.mult)
            TT_(S(9), im, im, ALU.mult)
            TT_(S(8), S(8), S(9), ALU.add)
            link(dve.reciprocal(S(9), S(8)))
            TT_(S(8), S(6), mre, ALU.mult)
            TT_(S(10), S(7), im, ALU.mult)
            TT_(S(8), S(10), S(8), ALU.subtract)
            TT_(S(10), S(7), mre, ALU.mult)
            TT_(S(11), S(6), im, ALU.mult)
            TT_(S(10), S(10), S(11), ALU.add)
            TT_(S(0), S(8), S(9), ALU.mult)
            link(STT(out=S(1), in0=S(10), scalar=-1.0, in1=S(9), op0=ALU.mult, op1=ALU.mult))
            dve.wait_ge(mag_done, 1)
            trigx = [trig[:, NY + j * NX:NY + (j + 1) * NX].rearrange("p (h a) -> p h a", a=A_N) for j in range(2)]
            link(STT(out=ey[:].rearrange("p h b -> p (h b)"), in0=trig[:, 0:NY], scalar=k.c("sign"),
                     in1=mag[:, 0:NY], op0=ALU.mult, op1=ALU.mult))
            TT_(ex1[:], trigx[0], magx, ALU.mult)
            TT_(ex2[:], trigx[1], magx, ALU.mult)
            TT_(ex1[:], ex1[:], bc(S(0), 2, A_N), ALU.mult)
            TT_(ex2[:], ex2[:], bc(S(1), 2, A_N), ALU.mult)
            TT(xx[:], ex1[:], ex2[:], ALU.add).then_inc(xy_ready, 1)
            link(dve.tensor_copy(len_f[:], len_i[:]))
            for c in range(KC):
                link(TS(lmask[:, c, :], len_f[:], k.c("lpos")[:, c:c + 1], None, ALU.is_gt))
            dve.wait_ge(kern_done, 1)
            link(TS(ksb[:].rearrange("a (j n) -> a j n", j=2), kps[:], 2.0, None, ALU.mult))
            tap = ksb[0:1, :].rearrange("a (h b) -> a h b", b=B_N)[:, :, 0]
            TT(tap, tap, drow[:], ALU.add).then_inc(kern_kept, 1)
            with dve.Fori(0, NS // RING) as i:
                for s in range(RING):
                    dve.wait_ge(conv_done, i * RING + s + 1)
                    out = k.y0T[:].rearrange("p c (b h) -> p c b h", h=NS)[:, :, :, bass.ds(i * RING + s, 1)]
                    TT(out.rearrange("p c b o -> p c (b o)"), yps[:, s, 0:KC * NB].rearrange("p (c b) -> p c b", b=NB),
                       lmask[:], ALU.mult).then_inc(conv_kept, 1)

        @block.tensor
        def _(pe):
            pe.wait_ge(xy_ready, 1)
            for h in range(NS):
                last = pe.matmul(kps[:, h // 16, (h % 16) * B_N:(h % 16 + 1) * B_N], xx[:, h, :], ey[:, h, :],
                                 start=True, stop=True)
            last.then_inc(kern_done, 1)
            pe.wait_ge(u_in, 16)

            def head(i, s):
                pe.wait_ge(toep_in[s], i * 16 + 16)
                for d in range(KC):
                    last = pe.matmul(yps[:, s, d * NB:KC * NB].rearrange("p (c b) -> p c b", b=NB),
                                     toep[:, s, d * P:(d + 1) * P],
                                     xr[:, 0:KC - d, bass.ds(i * RING + s, 1), :].rearrange("p c o b -> p c (o b)"),
                                     start=(d == 0), stop=(d == KC - 1))
                last.then_inc(conv_done, 1)

            for s in range(RING):
                head(0, s)
            with pe.Fori(1, NS // RING) as i:
                for s in range(RING):
                    pe.wait_ge(conv_kept, i * RING + s - RING + 1)
                    head(i, s)
    k.end_phase(ctx)


def peeled(eng, n, body):
    body(0, True)
    with eng.Fori(1, n) as i:
        body(i, False)


def mix_phase(k):
    nc, dram = k.nc, k.dram
    ctx = ExitStack()
    sb = lambda name, shape, dt=F32: k.sb(name, shape, dt, ctx)
    S2 = (0, 1)
    NGZ, NH1 = E0 + E0 * R0, E1 + R1
    xtok = sb("xtok", [P, TILES, D])
    wup = sb("wup", [P, KC, D])
    gzw = sb("gzw", [P, KC, NGZ])
    lb0 = sb("lb0", [E0 * R0, D])
    bias0 = sb("bias0", [P, E0])
    w1t = sb("w1t", [P, KC, D])
    a1h = sb("a1h", [P, KC, NH1])
    a1w = sb("a1w", [P, KC, R1])
    b1 = sb("b1", [P, D])
    lime = sb("lime", [P, E1, R1])
    cidx_i = sb("cidx_i", [P, TILES], I32)
    cidx_f = sb("cidx_f", [P, TILES])
    cidx = sb("cidx", [P, TILES], I32)
    wg = sb("wg", [P, TILES, NS])
    bd = sb("bd", [P, TILES, BPT, NS])
    ys = sb("ys", [P, 2, KC, P])
    lg = sb("lg", [P, 2, 8])
    mx = sb("mx", [P, 2, 8])
    ix = sb("ix", [P, 2, 8], U32)
    ixf = sb("ixf", [P, 2, 1])
    oh = sb("oh", [P, 2, E0])
    zm = sb("zm", [P, 2, E0 * R0])
    zmT = sb("zmT", [E0 * R0, 2, P])
    x1 = sb("x1", [P, 2, D])
    x1b = sb("x1b", [P, 2, D])
    y1T = sb("y1T", [P, 2, KC, P])
    y1d = sb("y1d", [P, 2, KC, P])
    ds1 = sb("ds1", [P, 2, E1, R1])
    pb = ctx.enter_context(nc.psum_tensor("pb", [P, 2, 512], F32))
    ps = ctx.enter_context(nc.psum_tensor("ps", [P, 2, 512], F32))
    pt = ctx.enter_context(nc.psum_tensor("pt", [P, 2, 512], F32))
    ph = ctx.enter_context(nc.psum_tensor("ph", [P, 2, 512], F32))
    idx_in, w0_in, w1_in, x_in, rows_in = (k.sem(n) for n in ("idx_in", "w0_in", "w1_in", "x_in", "rows_in"))
    idx_ready, bd_ready, ys_ready, proj0_done, zm_ready, zmT_done, zmT_kept, base0_done = (
        k.sem(n) for n in ("idx_ready", "bd_ready", "ys_ready", "proj0_done", "zm_ready", "zmT_done", "zmT_kept",
                           "base0_done"))
    x1_ready, y1T_done, y1T_kept, y1d_kept, x1b_ready, h_done, hx_kept, mix_steps = (
        k.sem(n) for n in ("x1_ready", "y1T_done", "y1T_kept", "y1d_kept", "x1b_ready", "h_done", "hx_kept",
                           "mix_steps"))

    passed = k.sem("passed_mix")
    with nc.Block() as block:
        @block.sync
        def _(sp):
            for dst, src, done in ((cidx_i, "cond_b", idx_in), (gzw, "gzw", w0_in), (bias0, "bias0", w0_in),
                                   (wup, "wup", w0_in), (lb0, "lb0", w0_in)):
                sp.dma_start(dst[:], dram[src]).then_inc(done, 16)
            sp.dma_start(xtok[:], dram["xtok"]).then_inc(x_in, 16)
            for dst, src in ((w1t, "w1t"), (a1h, "a1h"), (a1w, "a1w"), (b1, "b1"), (lime, "lime")):
                sp.dma_start(dst[:], dram[src]).then_inc(w1_in, 16)

        @block.gpsimd
        def _(pool):
            pool.wait_ge(idx_ready, 1)
            for t in range(TILES):
                pool.indirect_dma_start(wg[:, t, :], None, dram["l1w"],
                                        bass.IndirectOffsetOnAxis(cidx[:, t:t + 1], 0)).then_inc(rows_in, 16)

            def body(it, first):
                for s in S2:
                    at = it * 2 + s + 1
                    if not first:
                        pool.wait_ge(proj0_done, at - 2)
                    pool.tensor_copy(ys[:, s], k.y0T[:, :, bass.ds((it * 2 + s) * P, P)]).then_inc(ys_ready, 1)
                for s in S2:
                    at = it * 2 + s + 1
                    pool.wait_ge(x1_ready, at)
                    if first:
                        pool.wait_ge(w1_in, 80)
                    else:
                        pool.wait_ge(hx_kept, at - 2)
                    pool.tensor_tensor(x1b[:, s], x1[:, s], b1[:], ALU.add).then_inc(x1b_ready, 1)
            peeled(pool, TILES // 2, body)

        @block.tensor
        def _(pe):
            pe.wait_ge(w0_in, 64)

            def body(it, first):
                for s in S2:
                    at = it * 2 + s + 1
                    pe.wait_ge(ys_ready, at)
                    if not first:
                        pe.wait_ge(hx_kept, at - 2)
                    for c in range(KC):
                        pe.matmul(ps[:, s, 0:NGZ], ys[:, s, c, :], gzw[:, c, :], start=(c == 0), stop=(c == KC - 1))
                    for c in range(KC):
                        last = pe.matmul(pb[:, s, :], ys[:, s, c, :], wup[:, c, :], start=(c == 0), stop=False)
                    last.then_inc(proj0_done, 1)
                for s in S2:
                    pe.wait_ge(zm_ready, it * 2 + s + 1)
                    pe.transpose(ps[0:E0 * R0, s, 64:64 + P], zm[:, s, :], k.c("ident")).then_inc(zmT_done, 1)
                for s in S2:
                    pe.wait_ge(zmT_kept, it * 2 + s + 1)
                    pe.matmul(pb[:, s, :], zmT[:, s, :], lb0[:], start=False, stop=True).then_inc(base0_done, 1)
                if first:
                    pe.wait_ge(bd_ready, 1)
                for s in S2:
                    pe.wait_ge(x1_ready, it * 2 + s + 1)
                    mixer = bd[:].rearrange("p t b d -> p (t b d)")[:, bass.ds((it * 2 + s) * P, P)]
                    for c in range(KC):
                        last = pe.matmul(pt[:, s, c * P:(c + 1) * P], x1[:, s, c * P:(c + 1) * P], mixer,
                                         start=True, stop=True)
                    last.then_inc(y1T_done, 1)
                if first:
                    pe.wait_ge(w1_in, 80)
                for s in S2:
                    at = it * 2 + s + 1
                    pe.wait_ge(y1d_kept, at)
                    for c in range(KC):
                        pe.matmul(ps[:, s, 192:192 + NH1], y1d[:, s, c, :], a1h[:, c, :], start=(c == 0), stop=(c == KC - 1))
                    pe.wait_ge(y1T_kept, at)
                    for c in range(KC):
                        pe.matmul(ps[:, s, 256:256 + R1], y1T[:, s, c, :], a1w[:, c, :], start=(c == 0), stop=(c == KC - 1))
                    for c in range(KC):
                        last = pe.matmul(ph[:, s, :], y1T[:, s, c, :], w1t[:, c, :], start=(c == 0), stop=(c == KC - 1))
                    last.then_inc(h_done, 1)
            peeled(pe, TILES // 2, body)

        @block.scalar
        def _(act):
            def body(it, first):
                for s in S2:
                    act.wait_ge(zmT_done, it * 2 + s + 1)
                    act.copy(zmT[:, s, :], ps[0:E0 * R0, s, 64:64 + P]).then_inc(zmT_kept, 1)
                for s in S2:
                    act.wait_ge(y1T_done, it * 2 + s + 1)
                    act.copy(y1T[:, s].rearrange("p c t -> p (c t)"), pt[:, s, :]).then_inc(y1T_kept, 1)
            peeled(act, TILES // 2, body)

        @block.vector
        def _(dve):
            link = Link(dve, mix_steps)
            dve.wait_ge(idx_in, 16)
            link(dve.tensor_copy(cidx_f[:], cidx_i[:]))
            link(dve.tensor_scalar(cidx_f[:], cidx_f[:], float(NS), k.c("cmod"), ALU.mult, ALU.add))
            dve.tensor_copy(cidx[:], cidx_f[:]).then_inc(idx_ready, 1)
            link(dve.memset(lg[:], NEG))
            dve.wait_ge(rows_in, 16 * TILES)
            wide = lambda ap: ap.rearrange("p t (o d) -> p t o d", o=1).broadcast_to([P, TILES, BPT, NS])
            blk = bc(bc(k.c("block4"), 1, TILES), 3, NS)
            dve.tensor_tensor(bd[:], wide(wg[:]), blk, ALU.mult).then_inc(bd_ready, 1)
            dve.wait_ge(w0_in, 64)
            PER, pre = 12, link.n

            def body(it, first):
                link = Link(dve, mix_steps, pre + it * PER)
                for s in S2:
                    dve.wait_ge(proj0_done, it * 2 + s + 1)
                    link(dve.tensor_tensor(lg[:, s, 0:E0], ps[:, s, 0:E0], bias0[:], ALU.add), passed)
                    link(dve.max(mx[:, s, :], lg[:, s, :]), passed)
                    link(dve.max_index(ix[:, s, :], mx[:, s, :], lg[:, s, :]))
                    link(dve.tensor_copy(ixf[:, s, :], ix[:, s, 0:1]))
                    link(dve.tensor_scalar(oh[:, s, :], k.c("iota8")[:, 0:E0], ixf[:, s, :], None, ALU.is_equal))
                    dve.tensor_tensor(zm[:, s, :].rearrange("p (e r) -> p e r", e=E0),
                                      ps[:, s, E0:NGZ].rearrange("p (e r) -> p e r", e=E0),
                                      bc(oh[:, s, :], 2, R0), ALU.mult).then_inc(zm_ready, 1)
                if first:
                    dve.wait_ge(x_in, 16)
                for s in S2:
                    at = it * 2 + s + 1
                    dve.wait_ge(base0_done, at)
                    if not first:
                        dve.wait_ge(x1b_ready, at - 2)
                    dve.tensor_tensor(x1[:, s, :], pb[:, s, :], xtok[:].rearrange("p t d -> p (t d)")[:, bass.ds((it * 2 + s) * D, D)],
                                      ALU.add).then_inc(x1_ready, 1)
                for s in S2:
                    dve.wait_ge(y1T_kept, it * 2 + s + 1)
                    anchors = y1T[:, s].rearrange("p c (n two) -> p (c n) two", two=2)[:, :, 1]
                    dve.tensor_copy(y1d[:, s].rearrange("p c (n two) -> p (c n) two", two=2), bc(anchors, 2, 2))\
                        .then_inc(y1d_kept, 1)
                if first:
                    dve.wait_ge(w1_in, 80)
                for s in S2:
                    at = it * 2 + s + 1
                    t = it * 2 + s
                    dve.wait_ge(h_done, at)
                    row = lambda ap, n: ap[:, bass.ds(t * n, n)]
                    dve.tensor_copy(row(k.z1, R1), ps[:, s, 256:256 + R1])
                    dve.tensor_tensor(row(k.hs1, E1), ps[:, s, 192:192 + E1], b1[:, 0:E1], ALU.add)
                    link(dve.tensor_tensor(ds1[:, s], bc(ps[:, s, 192 + E1:192 + NH1], 1, E1), lime[:], ALU.mult))
                    dve.tensor_reduce(row(k.ds1, E1), ds1[:, s], AX.X, ALU.add)
                    dve.wait_ge(x1b_ready, at)
                    dve.tensor_tensor(row(k.hx, D), ph[:, s, :], x1b[:, s, :], ALU.add).then_inc(hx_kept, 1)
                assert link.n == PER
            peeled(dve, TILES // 2, body)
    k.end_phase(ctx)


def route_phase(k):
    nc, dram = k.nc, k.dram
    ctx = ExitStack()
    sb = lambda name, shape, dt=F32: k.sb(name, shape, dt, ctx)
    S2 = (0, 1)
    NRH = E2 + E2 * R2
    lime = sb("lime_re", [P, R1, E1])
    bmat = sb("bmat", [R1, D])
    b2t = sb("b2t", [P, KC, AD2 * RC2])
    a2 = sb("a2", [AD2 * RC2, D])
    ids_i = sb("ids_i", [P, TOK], I32)
    amask = sb("amask", [P, TOK])
    rw2 = sb("rw2", [P, KC, NRH])
    w2t = sb("w2t", [P, KC, D])
    lb2 = sb("lb2", [E2 * R2, D])
    bb2 = sb("bb2", [P, D])
    amx = sb("amx", [P, 2])
    gmx = sb("gmx", [P, 2])
    half = sb("half", [P, 2])
    lg = sb("lg1", [P, TILES, E1])
    l2 = sb("lg1b", [P, TILES, E1])
    pr = sb("pr1", [P, TILES, E1])
    sg = sb("sg1", [P, TILES, E1])
    m8 = sb("m8", [P, TILES, 8])
    st = sb("st1", [P, 2, TILES])
    mixed = sb("mixed", [P, TILES, R1, E1])
    zp = sb("zp", [P, TILES, R1])
    zs = sb("zs", [P, 2, R1])
    zpT = sb("zpT", [R1, 2, P])
    x2 = sb("x2", [P, 2, D])
    x2b = sb("x2b", [P, 2, D])
    x2T = sb("x2T", [P, 2, KC, P])
    bxm = sb("bxm", [P, 2, P])
    y2T = sb("y2T", [P, 2, KC, P])
    l8 = sb("l8", [P, 2, E2])
    mx = sb("mx2", [P, 2, 8])
    ix = sb("ix2", [P, 2, 8], U32)
    ixf = sb("ixf2", [P, 2, 2])
    nm = sb("nm2", [P, 2, 1])
    ex = sb("ex_2", [P, 2, E2])
    oh = sb("oh2", [P, 2, E2])
    em = sb("em2", [P, 2, E2])
    sr = sb("sr2", [P, 2, 2])
    hw = sb("hw2", [P, 2, E2 * R2])
    hwT = sb("hwT2", [E2 * R2, 2, P])
    x3 = sb("x3", [P, 2, D])
    pb = ctx.enter_context(nc.psum_tensor("pb2", [P, 2, 512], F32))
    ps = ctx.enter_context(nc.psum_tensor("ps2", [P, 2, 512], F32))
    pt = ctx.enter_context(nc.psum_tensor("pt2", [P, 2, 512], F32))
    ph = ctx.enter_context(nc.psum_tensor("ph2", [P, 2, 512], F32))
    r_in, w2_in, amx_ready, gmx_ready, lg_ready, ex1_done, pr_ready, sg1_done, amask_ready, route_steps, tile_steps = (
        k.sem(n) for n in ("r_in", "w2_in", "amx_ready", "gmx_ready", "lg_ready", "ex1_done", "pr_ready", "sg1_done",
                           "amask_ready", "route_steps", "tile_steps"))
    zs_ready, zpT_done, zpT_kept, delta_done, x2_ready, x2T_done, x2T_kept, bx_done, bxm_ready, y2T_done, y2T_kept = (
        k.sem(n) for n in ("zs_ready", "zpT_done", "zpT_kept", "delta_done", "x2_ready", "x2T_done", "x2T_kept",
                           "bx_done", "bxm_ready", "y2T_done", "y2T_kept"))
    x2b_ready, rh_done, nm_ready, ex2_done, hw_ready, hwT_done, hwT_kept, base2_done, x3_ready, x3T_done, x3h_kept, x3l_kept = (
        k.sem(n) for n in ("x2b_ready", "rh_done", "nm_ready", "ex2_done", "hw_ready", "hwT_done", "hwT_kept",
                           "base2_done", "x3_ready", "x3T_done", "x3h_kept", "x3l_kept"))
    x3_out = [k.sem("x3_out0"), k.sem("x3_out1")]
    x3res = dram["x3res"].rearrange("(t p) d -> t p d", p=P)

    passed = k.sem("passed_route")
    with nc.Block() as block:
        @block.sync
        def _(sp):
            for dst, src in ((lime, "lime_re"), (bmat, "bmat"), (ids_i, "ids_b"), (b2t, "b2t"), (a2, "a2")):
                sp.dma_start(dst[:], dram[src]).then_inc(r_in, 16)
            for dst, src in ((rw2, "rw2"), (w2t, "w2t"), (lb2, "lb2"), (bb2, "bb2")):
                sp.dma_start(dst[:], dram[src]).then_inc(w2_in, 16)

            def body(it, first):
                for s in S2:
                    sp.wait_ge(x3_ready, it * 2 + s + 1)
                    sp.dma_start(x3res[bass.ds(it * 2 + s, 1)].rearrange("o p d -> (o p) d"), x3[:, s, :])\
                        .then_inc(x3_out[s], 16)
            peeled(sp, TILES // 2, body)
            for s in S2:
                sp.wait_ge(x3_out[s], 16 * TILES // 2)

        @block.gpsimd
        def _(pool):
            pool.wait_ge(amx_ready, 1)
            pool.partition_all_reduce(gmx[:], amx[:], P, bass.bass_isa.ReduceOp.max).then_inc(gmx_ready, 1)
            pool.wait_ge(w2_in, 64)

            def body(it, first):
                for s in S2:
                    at = it * 2 + s + 1
                    pool.wait_ge(x2_ready, at)
                    if not first:
                        pool.wait_ge(x3_ready, at - 2)
                    pool.tensor_tensor(x2b[:, s], x2[:, s], bb2[:], ALU.add).then_inc(x2b_ready, 1)
            peeled(pool, TILES // 2, body)

        @block.tensor
        def _(pe):
            pe.wait_ge(r_in, 80)

            def body(it, first):
                for s in S2:
                    at = it * 2 + s + 1
                    pe.wait_ge(zs_ready, at)
                    pe.transpose(ps[0:R1, s, 0:P], zs[:, s, :], k.c("ident")).then_inc(zpT_done, 1)
                for s in S2:
                    pe.wait_ge(zpT_kept, it * 2 + s + 1)
                    pe.matmul(pb[:, s, :], zpT[:, s, :], bmat[:], start=True, stop=True).then_inc(delta_done, 1)
                for s in S2:
                    at = it * 2 + s + 1
                    pe.wait_ge(x2_ready, at)
                    if not first:
                        pe.wait_ge(x3l_kept, at - 2)
                    for c in range(KC):
                        last = pe.transpose(pt[:, s, c * P:(c + 1) * P], x2[:, s, c * P:(c + 1) * P], k.c("ident"))
                    last.then_inc(x2T_done, 1)
                for s in S2:
                    pe.wait_ge(x2T_kept, it * 2 + s + 1)
                    for c in range(KC):
                        last = pe.matmul(ps[:, s, P:2 * P], b2t[:, c, :], x2T[:, s, c, :], start=(c == 0), stop=(c == KC - 1))
                    last.then_inc(bx_done, 1)
                for s in S2:
                    pe.wait_ge(bxm_ready, it * 2 + s + 1)
                    for c in range(KC):
                        last = pe.matmul(ph[:, s, c * P:(c + 1) * P], a2[:, c * P:(c + 1) * P], bxm[:, s, :],
                                         start=True, stop=True)
                    last.then_inc(y2T_done, 1)
                if first:
                    pe.wait_ge(w2_in, 64)
                for s in S2:
                    pe.wait_ge(y2T_kept, it * 2 + s + 1)
                    for c in range(KC):
                        last = pe.matmul(ps[:, s, 256:256 + NRH], y2T[:, s, c, :], rw2[:, c, :], start=(c == 0), stop=(c == KC - 1))
                    last.then_inc(rh_done, 1)
                    for c in range(KC):
                        pe.matmul(pb[:, s, :], y2T[:, s, c, :], w2t[:, c, :], start=(c == 0), stop=False)
                for s in S2:
                    pe.wait_ge(hw_ready, it * 2 + s + 1)
                    pe.transpose(ps[:, s, 0:P], hw[:, s, :], k.c("ident")).then_inc(hwT_done, 1)
                for s in S2:
                    pe.wait_ge(hwT_kept, it * 2 + s + 1)
                    pe.matmul(pb[:, s, :], hwT[:, s, :], lb2[:], start=False, stop=True).then_inc(base2_done, 1)
                for s in S2:
                    pe.wait_ge(x3_ready, it * 2 + s + 1)
                    for c in range(KC):
                        last = pe.transpose(pt[:, s, c * P:(c + 1) * P], x3[:, s, c * P:(c + 1) * P], k.c("ident"))
                    last.then_inc(x3T_done, 1)
            peeled(pe, TILES // 2, body)

        @block.scalar
        def _(act):
            act.wait_ge(lg_ready, 1)
            act.activation(pr[:], l2[:], ACT.Exp).then_inc(ex1_done, 1)
            act.wait_ge(pr_ready, 1)
            act.activation(sg[:], sg[:], ACT.Exp, scale=-2.0).then_inc(sg1_done, 1)

            def body(it, first):
                for s in S2:
                    act.wait_ge(zpT_done, it * 2 + s + 1)
                    act.copy(zpT[:, s, :], ps[0:R1, s, 0:P]).then_inc(zpT_kept, 1)
                for s in S2:
                    act.wait_ge(x2T_done, it * 2 + s + 1)
                    act.copy(x2T[:, s].rearrange("p c t -> p (c t)"), pt[:, s, :]).then_inc(x2T_kept, 1)
                for s in S2:
                    act.wait_ge(y2T_done, it * 2 + s + 1)
                    act.copy(y2T[:, s].rearrange("p c t -> p (c t)"), ph[:, s, :]).then_inc(y2T_kept, 1)
                for s in S2:
                    act.wait_ge(nm_ready, it * 2 + s + 1)
                    act.activation(ex[:, s, :], l8[:, s, :], ACT.Exp, bias=nm[:, s, :]).then_inc(ex2_done, 1)
                for s in S2:
                    act.wait_ge(hwT_done, it * 2 + s + 1)
                    act.copy(hwT[:, s, :], ps[:, s, 0:P]).then_inc(hwT_kept, 1)
                for s in S2:
                    at = it * 2 + s + 1
                    act.wait_ge(x3T_done, at)
                    tile = k.x3h[:, :, bass.ds((it * 2 + s) * P, P)]
                    act.copy(tile, pt[:, s, :].rearrange("p (c t) -> p c t", c=KC)).then_inc(x3h_kept, 1)
            peeled(act, TILES // 2, body)

        @block.vector
        def _(dve):
            link = Link(dve, route_steps)
            TS, TT, STT = dve.tensor_scalar, dve.tensor_tensor, dve.scalar_tensor_tensor
            hs = k.hs1[:].rearrange("p (t e) -> p t e", e=E1)
            dl = k.ds1[:].rearrange("p (t e) -> p t e", e=E1)
            link(dve.tensor_reduce(amx[:, 0:1], k.hs1[:], AX.X, ALU.max, apply_absolute_value=True))
            dve.tensor_reduce(amx[:, 1:2], k.ds1[:], AX.X, ALU.max, apply_absolute_value=True).then_inc(amx_ready, 1)
            dve.wait_ge(gmx_ready, 1)
            link(TS(gmx[:], gmx[:], 1e-6, None, ALU.max))
            link(dve.reciprocal(half[:], gmx[:]))
            link(TS(half[:], half[:], 0.5, None, ALU.mult))
            link(TS(lg[:], hs, half[:, 0:1], None, ALU.mult))
            link(STT(out=lg[:], in0=dl, scalar=half[:, 1:2], in1=lg[:], op0=ALU.mult, op1=ALU.add))
            link(dve.tensor_reduce(st[:, 0, :], lg[:], AX.X, ALU.max))
            TT(l2[:], lg[:], bc(st[:, 0, :], 2, E1), ALU.subtract).then_inc(lg_ready, 1)
            dve.wait_ge(ex1_done, 1)
            link(dve.tensor_reduce(st[:, 1, :], pr[:], AX.X, ALU.add))
            link(dve.reciprocal(st[:, 0, :], st[:, 1, :]))
            link(TT(pr[:], pr[:], bc(st[:, 0, :], 2, E1), ALU.mult))
            for t in range(TILES):
                link(dve.max(m8[:, t, :], pr[:, t, :]))
            TT(sg[:], pr[:], bc(m8[:, :, 1], 2, E1), ALU.subtract).then_inc(pr_ready, 1)
            dve.wait_ge(sg1_done, 1)
            link(TS(sg[:], sg[:], 1.0, None, ALU.add))
            link(dve.reciprocal(l2[:], sg[:]))
            link(TT(pr[:], pr[:], l2[:], ALU.mult))
            link(dve.tensor_reduce(st[:, 1, :], pr[:], AX.X, ALU.add))
            link(TS(st[:, 1, :], st[:, 1, :], 1e-9, None, ALU.add))
            link(dve.reciprocal(st[:, 0, :], st[:, 1, :]))
            link(TT(pr[:], pr[:], bc(st[:, 0, :], 2, E1), ALU.mult))
            dve.wait_ge(r_in, 80)
            link(TT(mixed[:], pr[:].rearrange("p t (o e) -> p t o e", o=1).broadcast_to([P, TILES, R1, E1]),
                    bc(lime[:], 1, TILES), ALU.mult))
            link(dve.tensor_reduce(zp[:], mixed[:], AX.X, ALU.add))
            link(STT(out=zp[:], in0=zp[:], scalar=0.5, in1=k.z1[:].rearrange("p (t r) -> p t r", r=R1),
                     op0=ALU.mult, op1=ALU.mult))
            link(dve.tensor_copy(amask[:], ids_i[:]))
            link(TS(amask[:], amask[:], k.c("adapter"), None, ALU.is_equal))
            PER = 20

            def body(it, first):
                link = Link(dve, tile_steps, it * PER)
                for s in S2:
                    at = it * 2 + s + 1
                    dve.tensor_copy(zs[:, s, :], zp[:].rearrange("p t r -> p (t r)")[:, bass.ds((it * 2 + s) * R1, R1)])\
                        .then_inc(zs_ready, 1)
                for s in S2:
                    at = it * 2 + s + 1
                    dve.wait_ge(delta_done, at)
                    TT(x2[:, s, :], pb[:, s, :], k.hx[:, bass.ds((it * 2 + s) * D, D)], ALU.add).then_inc(x2_ready, 1)
                for s in S2:
                    dve.wait_ge(bx_done, it * 2 + s + 1)
                    TT(bxm[:, s, :], ps[:, s, P:2 * P], amask[:, bass.ds((it * 2 + s) * P, P)], ALU.mult).then_inc(bxm_ready, 1)
                if first:
                    dve.wait_ge(w2_in, 64)
                for s in S2:
                    at = it * 2 + s + 1
                    dve.wait_ge(rh_done, at)
                    link(dve.tensor_copy(l8[:, s, :], ps[:, s, 256:256 + E2]), passed)
                    link(dve.max(mx[:, s, :], l8[:, s, :]))
                    TS(nm[:, s, :], mx[:, s, 0:1], -1.0, None, ALU.mult).then_inc(nm_ready, 1)
                    link(dve.max_index(ix[:, s, :], mx[:, s, :], l8[:, s, :]))
                    link(dve.tensor_copy(ixf[:, s, :], ix[:, s, 0:2]))
                    link(TS(oh[:, s, :], k.c("iota8"), ixf[:, s, 0:1], None, ALU.is_equal))
                    link(STT(out=oh[:, s, :], in0=k.c("iota8"), scalar=ixf[:, s, 1:2], in1=oh[:, s, :],
                             op0=ALU.is_equal, op1=ALU.add))
                    dve.wait_ge(ex2_done, at)
                    link(TT(em[:, s, :], ex[:, s, :], oh[:, s, :], ALU.mult))
                    link(dve.tensor_reduce(sr[:, s, 0:1], em[:, s, :], AX.X, ALU.add))
                    link(dve.reciprocal(sr[:, s, 1:2], sr[:, s, 0:1]))
                    link(TS(em[:, s, :], em[:, s, :], sr[:, s, 1:2], 2.0, ALU.mult, ALU.mult))
                    TT(hw[:, s, :].rearrange("p (e r) -> p e r", e=E2),
                       ps[:, s, 256 + E2:256 + NRH].rearrange("p (e r) -> p e r", e=E2),
                       bc(em[:, s, :], 2, R2), ALU.mult).then_inc(hw_ready, 1)
                for s in S2:
                    at = it * 2 + s + 1
                    dve.wait_ge(base2_done, at)
                    dve.wait_ge(x2b_ready, at)
                    if not first:
                        dve.wait_ge(x3_out[s], it * 16)
                    TT(x3[:, s, :], pb[:, s, :], x2b[:, s, :], ALU.add).then_inc(x3_ready, 1)
                for s in S2:
                    at = it * 2 + s + 1
                    dve.wait_ge(x3h_kept, at)
                    tok = bass.ds((it * 2 + s) * P, P)
                    TT(k.x3l[:, :, tok], pt[:, s, :].rearrange("p (c t) -> p c t", c=KC),
                       k.x3h[:, :, tok].bitcast(F32), ALU.subtract).then_inc(x3l_kept, 1)
                assert link.n == PER, link.n
            peeled(dve, TILES // 2, body)
    k.end_phase(ctx)


def rope_phase(k):
    nc, dram = k.nc, k.dram
    ctx = ExitStack()
    sb = lambda name, shape, dt=F32: k.sb(name, shape, dt, ctx)
    HALF = HD // 2
    NA = TILES * HALF
    start_i = sb("start_i", [P, TILES], I32)
    pos = sb("pos", [P, TILES])
    nw = sb("nw", [P, 4, HD])
    ang = sb("ang", [P, 2 * NA])
    turns = sb("turns3", [P, 2 * NA])
    tab = sb("tab", [P, 4, TILES, HD])
    rope_in, ang_ready, trig3_done, tab_ready, tab_out, rope_steps = (
        k.sem(n) for n in ("rope_in", "ang_ready", "trig3_done", "tab_ready", "tab_out", "rope_steps"))
    with nc.Block() as block:
        @block.sync
        def _(sp):
            sp.dma_start(start_i[:], dram["start_b"]).then_inc(rope_in, 16)
            sp.dma_start(nw[:], dram["norm_w"]).then_inc(rope_in, 16)
            sp.wait_ge(tab_ready, 1)
            sp.dma_start(dram["ropetab"], tab[:].rearrange("p j t d -> p (j t d)")).then_inc(tab_out, 16)
            sp.wait_ge(tab_out, 16)

        @block.vector
        def _(dve):
            link = Link(dve, rope_steps)
            dve.wait_ge(rope_in, 32)
            link(dve.tensor_copy(pos[:], start_i[:]))
            link(dve.tensor_scalar(pos[:], pos[:], k.c("smod"), None, ALU.add))
            for j in range(2):
                link(dve.tensor_tensor(ang[:, j * NA:(j + 1) * NA].rearrange("p (t f) -> p t f", f=HALF),
                                       bc(pos[:], 2, HALF), bc(k.c("invf"), 1, TILES), ALU.mult))
            reduce_angles(link, dve, ang[:], turns[:], [((0, NA), k.c("halfpi"), 0), ((NA, 2 * NA), None, 0)])
            dve.sem_inc(ang_ready, 1)
            dve.wait_ge(trig3_done, 1)
            link(dve.tensor_scalar(ang[:, NA:], turns[:, NA:], -1.0, None, ALU.mult))
            cos = turns[:, 0:NA].rearrange("p (t f) -> p t f", f=HALF)
            sin = turns[:, NA:].rearrange("p (t f) -> p t f", f=HALF)
            neg = ang[:, NA:].rearrange("p (t f) -> p t f", f=HALF)
            for j, (lo, hi) in enumerate(((cos, cos), (neg, sin), (cos, cos), (neg, sin))):
                for part, src in ((slice(0, HALF), lo), (slice(HALF, HD), hi)):
                    link(dve.tensor_tensor(tab[:, j, :, part], src, bc(nw[:, j, part], 1, TILES), ALU.mult))
            dve.sem_inc(tab_ready, 1)

        @block.scalar
        def _(act):
            act.wait_ge(ang_ready, 1)
            act.activation(turns[:], ang[:], ACT.Sin).then_inc(trig3_done, 1)
    k.end_phase(ctx)


HH = HK // 2
UT = TILES
def project_phase(k, hh):
    nc, dram = k.nc, k.dram
    ctx = ExitStack()
    sb = lambda name, shape, dt=F32: k.sb(name, shape, dt, ctx)
    W4 = HH * HD
    tab = sb(f"rtab{hh}", [P, 4, TILES, HD])
    wraw = sb(f"wraw{hh}", [P, KC, W4])
    wh = sb(f"wh{hh}", [P, 2, KC, W4], F32R)
    wl = sb(f"wl{hh}", [P, 2, KC, W4], F32R)
    vs = sb(f"vs{hh}", [P, 2, W4])
    sq = sb(f"sq{hh}", [P, 2, HH, HD])
    ss = sb(f"ss{hh}", [P, 2, HH])
    rt = sb(f"rt{hh}", [P, 2, HH])
    ri = sb(f"ri{hh}", [P, 2, HH])
    qc = sb(f"qc{hh}", [P, 2, W4])
    qs = sb(f"qs{hh}", [P, 2, W4])
    pq = ctx.enter_context(nc.psum_tensor(f"pq{hh}", [P, 4, 512], F32))
    pt = ctx.enter_context(nc.psum_tensor(f"ptq{hh}", [P, 2, 512], F32))
    n = lambda name: k.sem(f"{name}{hh}")
    tab_in, wraw_in, whigh, wlow, proj_done, v_kept, ss_ready, qrt_ready = (
        n(x) for x in ("tab_in", "wraw_in", "whigh", "wlow", "proj_done", "v_kept", "ss_ready", "qrt_ready"))
    parts_ready, sum_ready, q_ready, qT_done, qT_kept, ss_done = (
        n(x) for x in ("parts_ready", "sum_ready", "q_ready", "qT_done", "qT_kept", "ss_done"))
    v_out = [n("v_out_a"), n("v_out_b")]
    GROUPS = 2 + HH
    wsrc = dram["wqkv"]
    vdst = dram["vnew"].rearrange("h (t p) d -> h t p d", p=P)[hh]

    def unit(j, t):
        return j * UT + t

    with nc.Block() as block:
        @block.sync
        def _(sp):
            sp.dma_start(wraw[:], wsrc[hh, 0]).then_inc(wraw_in, 16)
            sp.dma_start(tab[:].rearrange("p j t d -> p (j t d)"), dram["ropetab"]).then_inc(tab_in, 16)
            for j in range(1, GROUPS):
                sp.wait_ge(wlow, j)
                sp.dma_start(wraw[:], wsrc[hh, j]).then_inc(wraw_in, 16)
                if j == 1:
                    for t in range(TILES):
                        sp.wait_ge(v_kept, t + 1)
                        sp.dma_start(vdst[t], vs[:, t % 2, :]).then_inc(v_out[t % 2], 16)
            for o in v_out:
                sp.wait_ge(o, 16 * TILES // 2)

        @block.tensor
        def _(pe):
            def project(slot, t, u):
                i = 0
                for c in range(KC):
                    for x, w in ((k.x3h, wh), (k.x3h, wl), (k.x3l, wh)):
                        last = pe.matmul(pq[:, t % 4, :], x[:, c, t * P:(t + 1) * P], w[:, slot, c, :],
                                         start=(i == 0), stop=(i == 3 * KC - 1))
                        i += 1
                last.then_inc(proj_done, 1)

            def turn(t, r):
                pe.wait_ge(q_ready, r + 1)
                if not isinstance(r, int) or r >= 2:
                    pe.wait_ge(qT_kept, r - 1)
                for g in range(HH):
                    last = pe.transpose(pt[:, t % 2, g * P:(g + 1) * P], qc[:, t % 2, g * HD:(g + 1) * HD], k.c("ident"))
                last.then_inc(qT_done, 1)

            pe.wait_ge(wlow, 1)
            for t in range(TILES):
                if t >= 4:
                    pe.wait_ge(v_kept, t - 3)
                project(0, t, t)

            def rotated(j, slot, k_group):
                pe.wait_ge(wlow, j + 2)
                for t in range(TILES):
                    r = j * TILES + t
                    if k_group and t < 4:
                        pe.wait_ge(v_kept, 5 + t)
                    else:
                        pe.wait_ge(parts_ready, r - 3)
                    project(slot, t, r)
                    if not (k_group and t < 2):
                        turn((t - 2) % TILES, r - 2)
            rotated(0, 1, True)
            with pe.Fori(0, HH // 2) as i:
                for s in range(2):
                    rotated(i * 2 + s + 1, s, False)
            R = (1 + HH) * TILES
            for r in (R - 2, R - 1):
                turn(r % TILES, r)

        @block.scalar
        def _(act):
            for t in range(TILES):
                act.wait_ge(proj_done, t + 1)
                if t >= 2:
                    act.wait_ge(v_out[t % 2], 16 * (t // 2))
                act.copy(vs[:, t % 2, :], pq[:, t % 4, :]).then_inc(v_kept, 1)

            def keep(t, r, group):
                act.wait_ge(qT_done, r + 1)
                dst = k.qkT[:].rearrange("p (h n) -> p h n", n=TOK)
                dst = dst[:, 0:HH, :] if isinstance(group, int) and group == 0 else dst[:, bass.ds(group * HH, HH), :]
                act.copy(dst[:, :, t * P:(t + 1) * P], pt[:, t % 2, :].rearrange("p (h n) -> p h n", h=HH)).then_inc(qT_kept, 1)

            def rotated(j, k_group):
                for t in range(TILES):
                    r = j * TILES + t
                    act.wait_ge(proj_done, TILES + r + 1)
                    if not (k_group and t < 2):
                        act.wait_ge(qrt_ready, r - 1)
                    for g in range(HH):
                        last = act.activation(sq[:, t % 2, g], pq[:, t % 4, g * HD:(g + 1) * HD], ACT.Square,
                                              accum_out=ss[:, t % 2, g:g + 1])
                    last.then_inc(ss_done, 1)
                    act.wait_ge(ss_done, r + 1)
                    act.activation(rt[:, t % 2, :], ss[:, t % 2, :], ACT.Sqrt, scale=1.0 / HD, bias=k.c("eps")).then_inc(ss_ready, 1)
                    if not (k_group and t < 2):
                        keep((t - 2) % TILES, r - 2, j if t >= 2 else j - 1)
            rotated(0, True)
            with act.Fori(1, 1 + HH) as j:
                rotated(j, False)
            R = (1 + HH) * TILES
            for r in (R - 2, R - 1):
                keep(r % TILES, r, HH)

        @block.vector
        def _(dve):
            def split(g):
                dve.wait_ge(wraw_in, g * 16 + 16)
                if not isinstance(g, int) or g >= 2:
                    dve.wait_ge(proj_done, (g - 1) * TILES)
                high, low = (w[:, bass.ds(g % 2, 1)].rearrange("p o c n -> p (o c) n") for w in (wh, wl))
                dve.tensor_copy(high, wraw[:]).then_inc(whigh, 1)
                dve.wait_ge(whigh, g + 1)
                dve.tensor_tensor(low, wraw[:], high.bitcast(F32), ALU.subtract).then_inc(wlow, 1)

            split(0)
            split(1)
            dve.wait_ge(tab_in, 16)

            def scale(t, r):
                dve.wait_ge(sum_ready, r + 1)
                dve.wait_ge(qrt_ready, r + 1)
                v = qc[:, t % 2, :].rearrange("p (g d) -> p g d", d=HD)
                dve.tensor_tensor(v, v, bc(ri[:, t % 2, :], 2, HD), ALU.mult).then_inc(q_ready, 1)

            def rotated(j, k_group, more):
                cosw, sinw = (tab[:, 2], tab[:, 3]) if k_group else (tab[:, 0], tab[:, 1])
                for t in range(TILES):
                    r = j * TILES + t
                    dve.wait_ge(ss_ready, r + 1)
                    if not (k_group and t < 2):
                        dve.wait_ge(qT_done, r - 1)
                    dve.reciprocal(ri[:, t % 2, :], rt[:, t % 2, :]).then_inc(qrt_ready, 1)
                    src = pq[:, t % 4, :].rearrange("p (g d) -> p g d", d=HD)
                    dst = qc[:, t % 2, :].rearrange("p (g d) -> p g d", d=HD)
                    dve.tensor_tensor(dst, src, bc(cosw[:, t], 1, HH), ALU.mult)
                    src2 = pq[:, t % 4, :].rearrange("p (g two f) -> p g two f", two=2, f=HD // 2)
                    dst2 = qs[:, t % 2, :].rearrange("p (g two f) -> p g two f", two=2, f=HD // 2)
                    for o in range(2):
                        last = dve.tensor_tensor(dst2[:, :, o], src2[:, :, 1 - o],
                                                 bc(sinw[:, t, o * HD // 2:(o + 1) * HD // 2], 1, HH), ALU.mult)
                    last.then_inc(parts_ready, 1)
                    if not (k_group and t < 1):
                        scale((t - 1) % 2, r - 1)
                    if t == 0 and more:
                        split(j + 2)
            rotated(0, True, True)
            with dve.Fori(1, HH) as j:
                rotated(j, False, True)
            rotated(HH, False, False)
            scale((TILES - 1) % 2, (1 + HH) * TILES - 1)

        @block.gpsimd
        def _(pool):
            def rotated(j):
                for t in range(TILES):
                    pool.wait_ge(parts_ready, j * TILES + t + 1)
                    pool.tensor_tensor(qc[:, t % 2, :], qc[:, t % 2, :], qs[:, t % 2, :], ALU.add).then_inc(sum_ready, 1)
            with pool.Fori(0, 1 + HH) as j:
                rotated(j)
    k.end_phase(ctx)


def attend_phase(k, hh):
    nc, dram = k.nc, k.dram
    ctx = ExitStack()
    sb = lambda name, shape, dt=F32: k.sb(f"{name}{hh}", shape, dt, ctx)
    n = lambda name: k.sem(f"{name}{hh}")
    SLOTS = NPP + 1
    CUT = 9
    CA, CB = CUT * PS, (SLOTS - CUT) * PS
    VC = CL // P
    table = sb("table", [1, NB * NPP], I32)
    rows = sb("rows", [P, NB * VC], I32)
    rows_f = sb("rows_f", [P, NB * VC])
    vidx = sb("vidx", [P, 2, VC], I32)
    len_i = sb("klen_i", [P, NB], I32)
    len_f = sb("klen_f", [P, NB])
    kb = sb("kb", [P, 2, SLOTS, HH, PS])
    vb = sb("vb", [P, 2, VC + 1, HH * HD])
    qb = sb("qb", [P, 2, HH * G, NS])
    mask = sb("mask", [P, 2, KL])
    sm = sb("smax", [P, 2, KL])
    pm = sb("pm", [P, 2, KL])
    mxs = sb("mxs", [P, 2, 2])
    nmx = sb("nmx", [P, 2])
    rs = sb("rs", [P, 2])
    rv = sb("rv", [P, 2])
    pT = sb("pT", [P, 2, VC * P + P])
    sps = ctx.enter_context(nc.psum_tensor(f"sps{hh}", [P, 2, 2, 512], F32))
    tps = ctx.enter_context(nc.psum_tensor(f"tps{hh}", [P, 2, 512], F32))
    ops = ctx.enter_context(nc.psum_tensor(f"ops{hh}", [P, 2, 512], F32))
    att_in, rows_ready, att_steps, mask_ready, vidx_ready, kq_ready = (
        n(x) for x in ("att_in", "rows_ready", "att_steps", "mask_ready", "vidx_ready", "kq_ready"))
    k_in = [n("k_in_a"), n("k_in_b")]
    v_in = [n("v_in_a"), n("v_in_b")]
    vn_in = [n("vn_in_a"), n("vn_in_b")]
    qk_done, max_a, max_done, nmx_ready, exp_done, rv_ready, p_ready, t_done, pT_kept, pv_done, o_kept = (
        n(x) for x in ("qk_done", "max_a", "max_done", "nmx_ready", "exp_done", "rv_ready", "p_ready", "t_done",
                       "pT_kept", "pv_done", "o_kept"))
    kpages, vrows, vnew = dram["kpages"], dram[f"vrows{hh}"], dram["vnew"][hh]
    heads = lambda ap: ap.rearrange("p (h n) -> p h n", n=TOK)
    NU, BU = 2 * HH, 2

    passed = k.sem(f"passed_attend{hh}")
    with nc.Block() as block:
        @block.sync
        def _(sp):
            sp.dma_start(table[:], dram["table"]).then_inc(att_in, 16)
            sp.dma_start(rows[:], dram["table_b"]).then_inc(att_in, 16)
            sp.dma_start(len_i[:], dram["start_rep"]).then_inc(att_in, 16)
            sp.wait_ge(att_in, 48)

            def body(i, first):
                for s in range(2):
                    b = i * 2 + s
                    if not first:
                        sp.wait_ge(qk_done, (b - 1) * HH)
                    for j in range(NPP):
                        page = sp.value_load(table[0:1, bass.ds(b * NPP + j, 1)], min_val=0, max_val=PAGES - 1)
                        sp.dma_start(kb[:, s, j], kpages[bass.ds(page * 2 + hh, 1)].rearrange("o p (h t) -> (o p) h t", h=HH))\
                            .then_inc(k_in[s], 16)
                    if not first:
                        sp.wait_ge(pv_done, (b - 1) * HH)
                    sp.dma_start(vb[0:NS, s, VC, :], vnew[bass.ds(b * NS, NS), :]).then_inc(vn_in[s], 16)
            peeled(sp, NB // 2, body)

        @block.gpsimd
        def _(pool):
            pool.wait_ge(rows_ready, 1)

            def body(i, first):
                for s in range(2):
                    b = i * 2 + s
                    if not first:
                        pool.wait_ge(v_in[s], i * (16 * VC))
                    pool.tensor_copy(vidx[:, s, :], rows[:, bass.ds(b * VC, VC)]).then_inc(vidx_ready, 1)
                    if not first:
                        pool.wait_ge(qk_done, (b - 1) * HH)
                    pool.tensor_copy(qb[:, s], heads(k.qkT[:])[:, HH:, bass.ds(b * NS, NS)])
                    pool.tensor_copy(kb[:, s, NPP], heads(k.qkT[:])[:, 0:HH, bass.ds(b * NS, NS)]).then_inc(kq_ready, 1)
                    pool.wait_ge(vidx_ready, b + 1)
                    if not first:
                        lone_wait(pool, pv_done, (b - 1) * HH, passed)
                    for c in range(VC):
                        pool.indirect_dma_start(vb[:, s, c, :], None, vrows,
                                                bass.IndirectOffsetOnAxis(vidx[:, s, c:c + 1], 0)).then_inc(v_in[s], 16)
            peeled(pool, NB // 2, body)

        @block.tensor
        def _(pe):
            def scores(i, m, first):
                s, h, us = m // HH, m % HH, m % 2
                u = i * NU + m
                if h == 0:
                    pe.wait_ge(k_in[s], i * (16 * NPP) + 16 * NPP)
                    pe.wait_ge(kq_ready, i * 2 + s + 1)
                if not (first and m < 2):
                    pe.wait_ge(max_done, u - 1)
                q = qb[:, s, h * G:(h + 1) * G, :].rearrange("p g n -> p (g n)")
                pe.matmul(sps[:, us, 0, 0:CA].rearrange("p (j t) -> p j t", t=PS), q, kb[:, s, 0:CUT, h, :],
                          start=True, stop=True)
                pe.matmul(sps[:, us, 1, 0:CB].rearrange("p (j t) -> p j t", t=PS), q, kb[:, s, CUT:, h, :],
                          start=True, stop=True).then_inc(qk_done, 1)

            def turn(m, u):
                us = m % 2
                pe.wait_ge(p_ready, u + 1)
                if not isinstance(u, int) or u > 0:
                    pe.wait_ge(pT_kept, u)
                for c in range(VC):
                    pe.transpose(tps[:, 0, c * P:(c + 1) * P], pm[:, us, c * P:(c + 1) * P], k.c("ident"))
                pe.transpose(tps[0:NS, 1, 0:P], pm[:, us, CL:KL], k.c("ident")).then_inc(t_done, 1)

            def values(i, m, u):
                s, h, us = m // HH, m % HH, m % 2
                if h == 0:
                    pe.wait_ge(v_in[s], i * (16 * VC) + 16 * VC)
                    pe.wait_ge(vn_in[s], i * 16 + 16)
                pe.wait_ge(pT_kept, u + 1)
                if not isinstance(u, int) or u >= 2:
                    pe.wait_ge(o_kept, u - 1)
                for c in range(VC):
                    pe.matmul(ops[:, us, 0:P], vb[:, s, c, h * HD:(h + 1) * HD], pT[:, us, c * P:(c + 1) * P],
                              start=(c == 0), stop=False)
                pe.matmul(ops[:, us, 0:P], vb[0:NS, s, VC, h * HD:(h + 1) * HD], pT[0:NS, us, VC * P:],
                          start=False, stop=True).then_inc(pv_done, 1)

            def body(i, first):
                for m in range(NU):
                    u = i * NU + m
                    scores(i, m, first)
                    if not (first and m < 2):
                        values(i if m >= 2 else i - 1, (m - 2) % NU, u - 2)
                    if not (first and m < 1):
                        turn((m - 1) % NU, u - 1)
            pe.wait_ge(mask_ready, 1)
            peeled(pe, NB // 2, body)
            U = NB * HH
            values(NB // 2 - 1, NU - 2, U - 2)
            turn(NU - 1, U - 1)
            values(NB // 2 - 1, NU - 1, U - 1)

        @block.scalar
        def _(act):
            def keep(m, u):
                us = m % 2
                act.wait_ge(t_done, u + 1)
                if not isinstance(u, int) or u >= 2:
                    act.wait_ge(pv_done, u - 1)
                act.copy(pT[:, us, 0:CL], tps[:, 0, :])
                act.copy(pT[0:NS, us, CL:], tps[0:NS, 1, 0:P]).then_inc(pT_kept, 1)

            def body(i, first):
                for m in range(NU):
                    us, u = m % 2, i * NU + m
                    act.wait_ge(nmx_ready, u + 1)
                    if not (first and m < 2):
                        act.wait_ge(t_done, u - 1)
                    act.activation(pm[:, us, :], sm[:, us, :], ACT.Exp, bias=nmx[:, us:us + 1], scale=SCALE,
                                   accum_out=rs[:, us:us + 1]).then_inc(exp_done, 1)
                    if not (first and m < 1):
                        keep((m - 1) % NU, u - 1)
            peeled(act, NB // 2, body)
            keep(NU - 1, NB * HH - 1)

        @block.vector
        def _(dve):
            link = Link(dve, att_steps)
            dve.wait_ge(att_in, 48)
            link(dve.tensor_copy(rows_f[:], rows[:]))
            link(dve.tensor_scalar(rows_f[:], rows_f[:], float(PS), k.c("smod"), ALU.mult, ALU.add))
            dve.tensor_copy(rows[:], rows_f[:]).then_inc(rows_ready, 1)
            link(dve.tensor_copy(len_f[:], len_i[:]))
            dve.memset(mask[:], 0.0).then_inc(mask_ready, 1)
            dve.wait_ge(mask_ready, 1)

            def body(i, first):
                for m in range(NU):
                    s, h, us = m // HH, m % HH, m % 2
                    u, b = i * NU + m, i * 2 + s
                    if h == 0:
                        if not first:
                            dve.wait_ge(max_done, (b - 1) * HH)
                        dve.tensor_scalar(mask[:, s, 0:CL], k.c("iota512"), len_f[:, bass.ds(b, 1)], NEG,
                                          ALU.is_ge, ALU.mult).then_inc(mask_ready, 1)
                        dve.wait_ge(mask_ready, b + 2)
                    dve.wait_ge(qk_done, u + 1)
                    if not (first and m < 2):
                        lone_wait(dve, exp_done, u - 1, passed)
                    dve.tensor_tensor_reduce(out=sm[:, us, 0:CA], in0=sps[:, us, 0, 0:CA], in1=mask[:, s, 0:CA], scale=1.0,
                                             scalar=-3e38, op0=ALU.add, op1=ALU.max, accum_out=mxs[:, us, 0:1]).then_inc(max_a, 1)
                    lone_wait(dve, max_a, u + 1, passed)
                    dve.tensor_tensor_reduce(out=sm[:, us, CA:KL], in0=sps[:, us, 1, 0:CB], in1=mask[:, s, CA:KL], scale=1.0,
                                             scalar=mxs[:, us, 0:1], op0=ALU.add, op1=ALU.max,
                                             accum_out=mxs[:, us, 1:2]).then_inc(max_done, 1)
                    dve.wait_ge(max_done, u + 1)
                    dve.tensor_scalar(nmx[:, us:us + 1], mxs[:, us, 1:2], -SCALE, None, ALU.mult).then_inc(nmx_ready, 1)
                    if not (first and m < 2):
                        out(i if m >= 2 else i - 1, (m - 2) % NU, u - 2)
                    dve.wait_ge(exp_done, u + 1)
                    dve.reciprocal(rv[:, us:us + 1], rs[:, us:us + 1]).then_inc(rv_ready, 1)
                    dve.wait_ge(rv_ready, u + 1)
                    dve.tensor_scalar(pm[:, us, :], pm[:, us, :], rv[:, us:us + 1], None, ALU.mult).then_inc(p_ready, 1)

            def out(i, m, u):
                s, h, us = m // HH, m % HH, m % 2
                dve.wait_ge(pv_done, u + 1)
                dve.tensor_copy(heads(k.qkT[:])[:, HH + G * h:HH + G * (h + 1), bass.ds((i * 2 + s) * NS, NS)],
                                ops[:, us, 0:P].rearrange("p (g n) -> p g n", g=G)).then_inc(o_kept, 1)
            peeled(dve, NB // 2, body)
            for m in (NU - 2, NU - 1):
                out(NB // 2 - 1, m, NB * HH - NU + m)
    k.end_phase(ctx)


def output_phase(k, hh):
    nc, dram = k.nc, k.dram
    ctx = ExitStack()
    sb = lambda name, shape, dt=F32: k.sb(f"{name}{hh}", shape, dt, ctx)
    n = lambda name: k.sem(f"{name}{hh}")
    NH = HH * G
    worw = sb("worw", [P, 2, D])
    woh = sb("woh", [P, 2, D], F32R)
    wol = sb("wol", [P, 2, D], F32R)
    oh = sb("ohi", [P, 2, TOK], F32R)
    ol = sb("olo", [P, 2, TOK], F32R)
    acc = ctx.enter_context(nc.psum_tensor(f"acc{hh}", [P, TILES, 512], F32))
    wo_in = [n("wo_in_a"), n("wo_in_b")]
    wo_high, wo_low, o_high, o_low, head_done, y3_kept = (
        n(x) for x in ("wo_high", "wo_low", "o_high", "o_low", "head_done", "y3_kept"))
    wo = dram["wo"][hh]
    heads = k.qkT[:].rearrange("p (h n) -> p h n", n=TOK)

    with nc.Block() as block:
        @block.sync
        def _(sp):
            def body(i, first):
                for s in range(2):
                    h = i * 2 + s
                    if not first:
                        sp.wait_ge(wo_low, h - 1)
                    sp.dma_start(worw[:, s, :], wo[bass.ds(h, 1)].rearrange("o p n -> (o p) n")).then_inc(wo_in[s], 16)
            peeled(sp, NH // 2, body)

        @block.scalar
        def _(act):
            def body(i, first):
                for s in range(2):
                    h = i * 2 + s
                    if not first:
                        act.wait_ge(head_done, h - 1)
                    act.copy(oh[:, s, :], heads[:, bass.ds(h + HH, 1), :].rearrange("p o n -> p (o n)")).then_inc(o_high, 1)
            peeled(act, NH // 2, body)

        @block.vector
        def _(dve):
            def body(i, first):
                for s in range(2):
                    h = i * 2 + s
                    dve.wait_ge(o_high, h + 1)
                    dve.tensor_tensor(ol[:, s, :], heads[:, bass.ds(h + HH, 1), :].rearrange("p o n -> p (o n)"),
                                      oh[:, s, :].bitcast(F32), ALU.subtract).then_inc(o_low, 1)
                    dve.wait_ge(wo_in[s], i * 16 + 16)
                    if not first:
                        dve.wait_ge(head_done, h - 1)
                    dve.tensor_copy(woh[:, s, :], worw[:, s, :]).then_inc(wo_high, 1)
                    dve.wait_ge(wo_high, h + 1)
                    dve.tensor_tensor(wol[:, s, :], worw[:, s, :], woh[:, s, :].bitcast(F32), ALU.subtract).then_inc(wo_low, 1)
            peeled(dve, NH // 2, body)
            dve.wait_ge(head_done, NH)
            for t in range(TILES):
                if hh == 0:
                    dve.tensor_copy(k.y3[:, t, :], acc[:, t, :]).then_inc(y3_kept, 1)
                else:
                    dve.tensor_tensor(k.y3[:, t, :], k.y3[:, t, :], acc[:, t, :], ALU.add).then_inc(y3_kept, 1)

        @block.tensor
        def _(pe):
            def head(h, s, first, last_head):
                pe.wait_ge(o_low, h + 1)
                pe.wait_ge(wo_low, h + 1)
                for t in range(TILES):
                    cols = slice(t * P, (t + 1) * P)
                    for j, (o, w) in enumerate(((oh, woh), (oh, wol), (ol, woh))):
                        last = pe.matmul(acc[:, t, :], o[:, s, cols], w[:, s, :], start=(first and j == 0),
                                         stop=(last_head and j == 2))
                last.then_inc(head_done, 1)
            head(0, 0, True, False)
            head(1, 1, False, False)
            with pe.Fori(1, NH // 2 - 1) as i:
                for s in range(2):
                    head(i * 2 + s, s, False, False)
            head(NH - 2, 0, False, False)
            head(NH - 1, 1, False, True)
    k.end_phase(ctx)


def expert_phase(k):
    nc, dram = k.nc, k.dram
    ctx = ExitStack()
    sb = lambda name, shape, dt=F32: k.sb(name, shape, dt, ctx)
    S2 = (0, 1)
    NRK = E3 * R3
    EC = NRK // P
    wr = sb("wr", [P, KC, E3])
    a3 = sb("a3", [P, KC, NRK])
    b3 = sb("b3", [P, EC, D])
    yt = sb("yt", [P, 2, D])
    y3T = sb("y3T", [P, 2, KC, P])
    sc = sb("sc3", [P, 2, E3])
    m1 = sb("m1", [P, 2, 8])
    m2 = sb("m2", [P, 2, 8])
    r1 = sb("r1", [P, 2, E3])
    r2 = sb("r2", [P, 2, E3])
    pick = sb("pick", [P, 2, E3])
    nm = sb("nm3", [P, 2, 1])
    ex = sb("ex3", [P, 2, E3])
    gate = sb("gate", [P, 2, E3])
    sr = sb("sr3", [P, 2, 2])
    hg = sb("hg", [P, 2, NRK])
    hgT = sb("hgT", [P, 2, EC, P])
    xres = sb("xres", [P, 2, D])
    fin = sb("fin", [P, 2, D])
    pa = ctx.enter_context(nc.psum_tensor("pa3", [P, 2, 512], F32))
    psc = ctx.enter_context(nc.psum_tensor("psc3", [P, 2, 512], F32))
    pr = ctx.enter_context(nc.psum_tensor("pr3", [P, 2, 2, 512], F32))
    e_in = k.sem("e_in")
    yt_ready, y3T_done, y3T_kept, sc_done, rank_done, nm3_ready, ex3_done, hg_ready = (
        k.sem(n) for n in ("yt_ready", "y3T_done", "y3T_kept", "sc_done", "rank_done", "nm3_ready", "ex3_done", "hg_ready"))
    fin_done, fin_ready, e_steps = (k.sem(n) for n in ("fin_done", "fin_ready", "e_steps"))
    half_done = [k.sem("half_done0"), k.sem("half_done1")]
    half_kept = [k.sem("half_kept0"), k.sem("half_kept1")]
    res_in = [k.sem("res_in0"), k.sem("res_in1")]
    out_done = [k.sem("out_done0"), k.sem("out_done1")]
    x3res = dram["x3res"].rearrange("(t p) d -> t p d", p=P)
    out = dram["out"].rearrange("(t p) d -> t p d", p=P)

    passed = k.sem("passed_expert")
    with nc.Block() as block:
        @block.sync
        def _(sp):
            for dst, src in ((wr, "wr"), (a3, "a3"), (b3, "b3")):
                sp.dma_start(dst[:], dram[src]).then_inc(e_in, 16)

            def body(it, first):
                for s in S2:
                    t = it * 2 + s
                    if not first:
                        sp.wait_ge(fin_ready, t - 1)
                    sp.dma_start(xres[:, s, :], x3res[bass.ds(t, 1)].rearrange("o p d -> (o p) d")).then_inc(res_in[s], 16)
                for s in S2:
                    t = it * 2 + s
                    sp.wait_ge(fin_ready, t + 1)
                    sp.dma_start(out[bass.ds(t, 1)].rearrange("o p d -> (o p) d"), fin[:, s, :]).then_inc(out_done[s], 16)
            peeled(sp, TILES // 2, body)
            for s in S2:
                sp.wait_ge(out_done[s], 16 * TILES // 2)

        @block.gpsimd
        def _(pool):
            def body(it, first):
                for s in S2:
                    t = it * 2 + s
                    if not first:
                        pool.wait_ge(y3T_done, t - 1)
                    pool.tensor_copy(yt[:, s, :], k.y3[:].rearrange("p t d -> p (t d)")[:, bass.ds(t * D, D)]).then_inc(yt_ready, 1)
            peeled(pool, TILES // 2, body)

        @block.tensor
        def _(pe):
            def body(it, first):
                for s in S2:
                    at = it * 2 + s + 1
                    pe.wait_ge(yt_ready, at)
                    if not first:
                        pe.wait_ge(fin_ready, at - 2)
                    for c in range(KC):
                        last = pe.transpose(pa[:, s, c * P:(c + 1) * P], yt[:, s, c * P:(c + 1) * P], k.c("ident"))
                    last.then_inc(y3T_done, 1)
                if first:
                    pe.wait_ge(e_in, 48)
                for s in S2:
                    pe.wait_ge(y3T_kept, it * 2 + s + 1)
                    for c in range(KC):
                        last = pe.matmul(psc[:, s, 0:E3], y3T[:, s, c, :], wr[:, c, :], start=(c == 0), stop=(c == KC - 1))
                    last.then_inc(sc_done, 1)
                    for j in range(2):
                        for c in range(KC):
                            last = pe.matmul(pr[:, s, j, :], y3T[:, s, c, :], a3[:, c, j * 512:(j + 1) * 512],
                                             start=(c == 0), stop=(c == KC - 1))
                    last.then_inc(rank_done, 1)
                for half in range(2):
                    for s in S2:
                        at = it * 2 + s + 1
                        pe.wait_ge(hg_ready, at)
                        if half:
                            pe.wait_ge(hgT_kept, 2 * at - 2 + (1 if s == 0 else 0) - (1 if s == 1 else 0) + 0) if False else \
                                pe.wait_ge(half_kept[s], it * 2 + 1)
                        for c in range(KC):
                            last = pe.transpose(psc[:, s, c * P:(c + 1) * P], hg[:, s, (half * KC + c) * P:(half * KC + c + 1) * P],
                                                k.c("ident"))
                        last.then_inc(half_done[s], 1)
                for s in S2:
                    at = it * 2 + s + 1
                    pe.wait_ge(half_kept[s], it * 2 + 2)
                    for c in range(EC):
                        last = pe.matmul(pa[:, s, :], hgT[:, s, c, :], b3[:, c, :], start=(c == 0), stop=(c == EC - 1))
                    last.then_inc(fin_done, 1)
            peeled(pe, TILES // 2, body)

        @block.scalar
        def _(act):
            def body(it, first):
                for s in S2:
                    act.wait_ge(y3T_done, it * 2 + s + 1)
                    act.copy(y3T[:, s].rearrange("p c t -> p (c t)"), pa[:, s, :]).then_inc(y3T_kept, 1)
                for s in S2:
                    act.wait_ge(nm3_ready, it * 2 + s + 1)
                    act.activation(ex[:, s, :], sc[:, s, :], ACT.Exp, bias=nm[:, s, :]).then_inc(ex3_done, 1)
                for half in range(2):
                    for s in S2:
                        act.wait_ge(half_done[s], it * 2 + half + 1)
                        act.copy(hgT[:, s, half * KC:(half + 1) * KC].rearrange("p c t -> p (c t)"), psc[:, s, :])\
                            .then_inc(half_kept[s], 1)
            peeled(act, TILES // 2, body)

        @block.vector
        def _(dve):
            TS, TT = dve.tensor_scalar, dve.tensor_tensor
            PER = 20
            dve.wait_ge(e_in, 48)

            def body(it, first):
                link = Link(dve, e_steps, it * PER)
                for s in S2:
                    at = it * 2 + s + 1
                    dve.wait_ge(sc_done, at)
                    link(dve.tensor_copy(sc[:, s, :], psc[:, s, 0:E3]), passed)
                    link(dve.max(m1[:, s, :], sc[:, s, :]))
                    TS(nm[:, s, :], m1[:, s, 0:1], -1.0, None, ALU.mult).then_inc(nm3_ready, 1)
                    link(dve.match_replace(r1[:, s, :], m1[:, s, :], sc[:, s, :], NEG), passed)
                    link(dve.max(m2[:, s, :], r1[:, s, :]), passed)
                    link(dve.match_replace(r2[:, s, :], m2[:, s, :], r1[:, s, :], NEG))
                    link(TT(pick[:, s, :], r2[:, s, :], sc[:, s, :], ALU.not_equal))
                    dve.wait_ge(ex3_done, at)
                    link(TT(gate[:, s, :], ex[:, s, :], pick[:, s, :], ALU.mult))
                    link(dve.tensor_reduce(sr[:, s, 0:1], gate[:, s, :], AX.X, ALU.add))
                    link(dve.reciprocal(sr[:, s, 1:2], sr[:, s, 0:1]))
                    link(TS(gate[:, s, :], gate[:, s, :], sr[:, s, 1:2], 2.0, ALU.mult, ALU.mult))
                    dve.wait_ge(rank_done, at)
                    for j in range(2):
                        last = TT(hg[:, s, j * 512:(j + 1) * 512].rearrange("p (e r) -> p e r", r=R3),
                                  pr[:, s, j, :].rearrange("p (e r) -> p e r", r=R3),
                                  bc(gate[:, s, j * 32:(j + 1) * 32], 2, R3), ALU.mult)
                    last.then_inc(hg_ready, 1)
                for s in S2:
                    at = it * 2 + s + 1
                    dve.wait_ge(fin_done, at)
                    dve.wait_ge(res_in[s], it * 16 + 16)
                    if not first:
                        dve.wait_ge(out_done[s], it * 16)
                    TT(fin[:, s, :], pa[:, s, :], xres[:, s, :], ALU.add).then_inc(fin_ready, 1)
                assert link.n == PER, link.n
            peeled(dve, TILES // 2, body)
    k.end_phase(ctx)


def build(nc, dram):
    with ExitStack() as ctx:
        k = Core(nc, ctx, dram)
        kpad = dram["kpad"]
        dram["toeplitz"] = lambda h: overlapped(kpad, h)
        k.cst = k.sb("cst", [P, CONST_N])
        k.x3h = k.sb("x3h", [P, KC, TOK], F32R)
        k.x3l = k.sb("x3l", [P, KC, TOK], F32R)
        low = ExitStack()
        k.y0T = k.sb("y0T", [P, KC, TOK], F32, low)
        s4_phase(k)
        k.hx = k.sb("hx", [P, TILES * D], F32, low)
        k.z1 = k.sb("z1", [P, TILES * R1], F32, low)
        k.hs1 = k.sb("hs1", [P, TILES * E1], F32, low)
        k.ds1 = k.sb("dl1", [P, TILES * E1], F32, low)
        mix_phase(k)
        route_phase(k)
        low.close()
        k.qkT = k.sb("qkT", [P, (HH + HH * G) * TOK])
        rope_phase(k)
        for hh in range(2):
            project_phase(k, hh)
            attend_phase(k, hh)
            if hh == 0:
                k.y3 = k.sb("y3", [P, TILES, D])
            output_phase(k, hh)
        expert_phase(k)
    return nc


def overlapped(kpad, h):
    return bass.AP(kpad.tensor, h * KPAD + 1, [[1, P], [1, D]])


def layouts(i):
    a = np.ascontiguousarray
    rep = lambda v: np.broadcast_to(v, (P,) + v.shape)
    f = {n: np.asarray(v) for n, v in i.items()}
    d = {"cst": constants()}
    dup = lambda v: np.concatenate([v.T, v.T], 0)
    d["s4in"] = a(np.stack([rep(f["L0_cond_log_dt"]), dup(f["L0_cond_log_A_real"]), dup(f["L0_cond_A_imag"]),
                            dup(f["L0_cond_C"][:, :, 0]), dup(f["L0_cond_C"][:, :, 1])], 1))
    d["L0_cond_D"] = f["L0_cond_D"]
    d["len_b"] = a(rep(f["itok_B_78_3631"]))
    x = f["x"]
    d["x_rev"] = a(x.reshape(NB, NS, KC, P)[..., ::-1].transpose(3, 2, 1, 0))
    chunks = lambda m: a(m.reshape(-1, P, m.shape[1]).transpose(1, 0, 2))
    d["xtok"] = chunks(x.reshape(TOK, D))
    d["wup"] = chunks(f["L0_ffn_W_up"].T)
    d["gzw"] = chunks(np.concatenate([f["L0_ffn_gate_w"].T, f["L0_ffn_lora_A"].reshape(E0 * R0, D).T], 1))
    d["bias0"] = a(rep(f["L0_ffn_expert_bias"]))
    d["lb0"] = a(f["L0_ffn_lora_B"].transpose(0, 2, 1).reshape(E0 * R0, D))
    d["cond_b"] = a(np.repeat(f["itok_B_0_15"], NS).reshape(TILES, P).T)
    d["l1w"] = a(f["L1_cond_weights"].reshape(-1, NS))
    d["w1t"] = chunks(f["L1_ffn_W"].T)
    d["a1w"] = chunks(f["L1_ffn_A"])
    d["a1h"] = chunks(np.concatenate([f["L1_ffn_W"].T[:, :E1], f["L1_ffn_A"]], 1))
    d["b1"] = a(rep(f["L1_ffn_b"]))
    d["lime"] = a(rep(f["L1_ffn_LiMEs"]))
    d["lime_re"] = a(rep(f["L1_ffn_LiMEs"].T))
    d["bmat"] = f["L1_ffn_Bmat"]
    d["ids_b"] = a(rep(np.repeat(f["itok_B_3_7"], NS)))
    d["b2t"] = chunks(f["L2_cond_B"].reshape(AD2 * RC2, D).T)
    d["a2"] = a(f["L2_cond_A"].transpose(0, 2, 1).reshape(AD2 * RC2, D))
    d["rw2"] = chunks(np.concatenate([f["L2_ffn_W_router"].T, f["L2_ffn_lora_A"].reshape(E2 * R2, D).T], 1))
    d["w2t"] = chunks(f["L2_ffn_W_base"].T)
    d["lb2"] = a(f["L2_ffn_lora_B"].transpose(0, 2, 1).reshape(E2 * R2, D))
    d["bb2"] = a(rep(f["L2_ffn_b_base"]))
    d["start_b"] = a(np.repeat(f["itok_B_207_1644"], NS).reshape(TILES, P).T)
    swap = lambda v: np.concatenate([v[HD // 2:], v[:HD // 2]])
    qw, kw = f["L3_cond_q_norm_w"], f["L3_cond_k_norm_w"]
    d["norm_w"] = a(rep(np.stack([qw, swap(qw), kw, swap(kw)])))
    halves = lambda w: w.T.reshape(KC, P, 2, -1, HH * HD).transpose(2, 3, 1, 0, 4)
    d["wqkv"] = a(np.concatenate([halves(f["L3_cond_Wv"]), halves(f["L3_cond_Wk"]), halves(f["L3_cond_Wq"])], 1))
    d["table"] = a(f["itok_Bx16_0_63"].reshape(1, -1))
    d["table_b"] = a(np.repeat(f["itok_Bx16_0_63"].reshape(NB * CL // P, P // PS).T, PS, 0))
    d["start_rep"] = a(rep(f["itok_B_207_1644"]))
    kc, vc = f["L3_cond_k_cache"], f["L3_cond_v_cache"]
    d["kpages"] = a(kc.reshape(PAGES, PS, 2, HH, HD).transpose(0, 2, 4, 3, 1).reshape(PAGES * 2, HD, HH * PS))
    for hh in range(2):
        d[f"vrows{hh}"] = a(vc.reshape(PAGES * PS, 2, HH * HD)[:, hh])
    d["wo"] = a(f["L3_cond_Wo"].T.reshape(2, HH * G, HD, D))
    d["wr"] = chunks(f["L3_ffn_Wr"].T)
    d["a3"] = chunks(f["L3_ffn_A"].reshape(E3 * R3, D).T)
    d["b3"] = chunks(f["L3_ffn_B"].transpose(0, 2, 1).reshape(E3 * R3, D))
    return d


SCRATCH = {"kpad": (NS, KPAD), "x3res": (TOK, D), "ropetab": (P, 4 * TILES * HD), "vnew": (2, TOK, HH * HD)}


def kernel(**inputs):
    import concourse.bacc as bacc
    from concourse.bass_utils import run_bass_kernel_spmd

    arrays = layouts(inputs)
    nc = bacc.Bacc("TRN2", target_bir_lowering=False, num_devices=1)
    dram = {n: nc.dram_tensor(f"in_{n}", v.shape, mybir.dt.from_np(v.dtype), kind="ExternalInput").ap()
            for n, v in arrays.items()}
    for n, shape in SCRATCH.items():
        dram[n] = nc.dram_tensor(f"scratch_{n}", shape, F32, kind="Internal").ap()
    dram["out"] = nc.dram_tensor("out", (TOK, D), F32, kind="ExternalOutput").ap()
    build(nc, dram)
    r = run_bass_kernel_spmd(nc, [{f"in_{n}": v for n, v in arrays.items()}], core_ids=[0])
    return r.results[0]["out"].reshape(NB, NS, D)
```

```python
import math
from contextlib import ExitStack

import numpy as np
import concourse.bass as bass
from concourse import mybir

F32 = mybir.dt.float32
F32R = mybir.dt.float32r
I32 = mybir.dt.int32
U32 = mybir.dt.uint32
ALU = mybir.AluOpType
ACT = mybir.ActivationFunctionType
AX = mybir.AxisListType

P = 128
NB, NS, D = 32, 32, 512
TOK = NB * NS
TILES = TOK // P
KC = D // P
BPT = P // NS

MODES = 64
A_STEP, A_N, B_N = 32, 16, 32
KPAD = 640
E0, R0 = 4, 8
E1, R1 = 8, 32
AD2, RC2 = 8, 16
E2, R2 = 8, 16
HD, HQ, HK = 128, 32, 8
G = HQ // HK
PAGES, PS, NPP = 64, 32, 16
CL = NPP * PS
KL = CL + NS
E3, TOP3, R3 = 64, 16, 16
SCALE = 1.0 / math.sqrt(HD)
NEG = -1e30

MAGIC = 12582912.0
TWO_PI_1 = 6.28125
TWO_PI_2 = float(np.uint32(np.float32(2 * math.pi - 6.28125).view(np.uint32) & np.uint32(0xFFFFF000)).view(np.float32))
TWO_PI_3 = 2 * math.pi - TWO_PI_1 - TWO_PI_2
INV_2PI = 1.0 / (2 * math.pi)
PI_IN = float(np.nextafter(np.float32(math.pi), np.float32(0)))

CONST_PARTS = [("ident", P), ("iota8", 8), ("block4", BPT), ("cmod", 1), ("bvals", B_N), ("avals", A_N),
               ("phase", 1), ("phase2", 1), ("halfpi", 1), ("sign", 1), ("lpos", KC), ("adapter", 1), ("smod", 1),
               ("invf", HD // 2), ("sinsign", HD), ("iota512", CL), ("experts", E3), ("eps", 1), ("prow", 1)]
CONST_AT, _n = {}, 0
for _name, _len in CONST_PARTS:
    CONST_AT[_name] = (_n, _n + _len)
    _n += _len
CONST_N = _n


def constants():
    p = np.arange(P, dtype=np.float32)
    c = np.zeros((P, CONST_N), np.float32)

    def put(name, value):
        a, b = CONST_AT[name]
        c[:, a:b] = value

    put("ident", np.eye(P))
    put("iota8", np.arange(8)[None])
    put("block4", (p[:, None] // NS == np.arange(BPT)[None]))
    put("cmod", (p % NS)[:, None])
    put("bvals", np.arange(B_N)[None])
    put("avals", (A_STEP * np.arange(A_N))[None])
    put("phase", np.where(p < MODES, np.float32(math.pi / 2), 0)[:, None])
    put("phase2", np.where(p < MODES, np.float32(math.pi), np.float32(math.pi / 2))[:, None])
    put("halfpi", np.float32(math.pi / 2))
    put("sign", np.where(p < MODES, 1, -1)[:, None])
    put("lpos", p[:, None] + P * np.arange(KC)[None])
    put("adapter", (p // RC2)[:, None])
    put("smod", (p % NS)[:, None])
    put("invf", (np.float32(1) / np.float32(10000.0) ** (np.arange(0, HD, 2, dtype=np.float32) / np.float32(HD)))[None])
    put("sinsign", np.where(np.arange(HD) < HD // 2, -1, 1)[None])
    put("iota512", np.arange(CL)[None])
    put("eps", 1e-6)
    put("prow", p[:, None])
    put("experts", np.arange(E3)[None])
    return c


class Link:

    def __init__(self, eng, sem, base=0):
        self.eng, self.sem, self.base, self.n = eng, sem, base, 0

    def __call__(self, ins, passed=None):
        self.n += 1
        ins.then_inc(self.sem, 1)
        if passed:
            lone_wait(self.eng, self.sem, self.base + self.n, passed)
        else:
            self.eng.wait_ge(self.sem, self.base + self.n)


def lone_wait(eng, sem, value, passed):
    eng.wait_ge(sem, value)
    eng.sem_inc(passed, 1)


def bc(ap, axis, n):
    shape = list(ap.shape)
    shape.insert(axis, n)
    return ap.unsqueeze(axis).broadcast_to(shape)


def reduce_angles(link, dve, theta, turns, phases, spare=None):
    for (a, b), ph, in_turns in phases:
        if ph is None:
            link(dve.tensor_scalar(turns[:, a:b], theta[:, a:b], INV_2PI, None, ALU.mult))
        else:
            link(dve.tensor_scalar(turns[:, a:b], theta[:, a:b], ph, INV_2PI, ALU.add, ALU.mult))
    link(dve.tensor_scalar(turns, turns, MAGIC, None, ALU.add))
    link(dve.tensor_scalar(turns, turns, MAGIC, None, ALU.subtract))
    for part in (TWO_PI_1, TWO_PI_2, TWO_PI_3):
        if spare is None:
            link(dve.scalar_tensor_tensor(out=theta, in0=turns, scalar=-part, in1=theta, op0=ALU.mult, op1=ALU.add))
        else:
            link(dve.tensor_scalar(spare, turns, part, None, ALU.mult))
            link(dve.tensor_tensor(theta, theta, spare, ALU.subtract))
    for (a, b), ph, _ in phases:
        if ph is not None:
            link(dve.tensor_scalar(theta[:, a:b], theta[:, a:b], ph, None, ALU.add))
    link(dve.tensor_scalar(theta, theta, PI_IN, -PI_IN, ALU.min, ALU.max))


class Core:

    def __init__(self, nc, ctx, dram):
        self.nc, self.ctx, self.dram = nc, ctx, dram
        self.sems = []

    def sb(self, name, shape, dt=F32, ctx=None):
        return (ctx or self.ctx).enter_context(self.nc.sbuf_tensor(name, shape, dt))

    def sem(self, name):
        self.sems.append(self.nc.alloc_semaphore(name=name))
        return self.sems[-1]

    def end_phase(self, ctx):
        ctx.close()
        self.nc.clear_and_free_semaphores(self.sems)
        self.nc.all_engine_barrier()
        self.sems = []

    def c(self, name):
        a, b = CONST_AT[name]
        return self.cst[:, a:b]


class Rotary:
    HALF = HD // 2
    NA = TILES * HALF

    def __init__(self, k, sb):
        self.k = k
        self.start_i = sb("start_i", [P, TILES], I32)
        self.pos = sb("pos", [P, TILES])
        self.nw = sb("nw", [P, 4, HD])
        self.ang = sb("ang", [P, 2 * self.NA])
        self.turns = sb("turns3", [P, 2 * self.NA])
        self.tab = sb("tab", [P, 4, TILES, HD])
        self.rope_in, self.ang_ready, self.trig3_done, self.tab_out, self.rope_steps = (
            k.sem(n) for n in ("rope_in", "ang_ready", "trig3_done", "tab_out", "rope_steps"))

    def load(self, sp):
        sp.dma_start(self.start_i[:], self.k.dram["start_b"]).then_inc(self.rope_in, 16)
        sp.dma_start(self.nw[:], self.k.dram["norm_w"]).then_inc(self.rope_in, 16)

    def tables(self, pool, const_in):
        k, HALF, NA, ang, turns, tab = self.k, self.HALF, self.NA, self.ang, self.turns, self.tab
        link = Link(pool, self.rope_steps)
        pool.wait_ge(const_in, 16)
        pool.wait_ge(self.rope_in, 32)
        link(pool.tensor_copy(self.pos[:], self.start_i[:]))
        link(pool.tensor_scalar(self.pos[:], self.pos[:], k.c("smod"), None, ALU.add))
        for j in range(2):
            link(pool.tensor_tensor(ang[:, j * NA:(j + 1) * NA].rearrange("p (t f) -> p t f", f=HALF),
                                    bc(self.pos[:], 2, HALF), bc(k.c("invf"), 1, TILES), ALU.mult))
        reduce_angles(link, pool, ang[:], turns[:], [((0, NA), k.c("halfpi"), 0), ((NA, 2 * NA), None, 0)],
                      tab[:, 0].rearrange("p t d -> p (t d)"))
        pool.sem_inc(self.ang_ready, 1)
        pool.wait_ge(self.trig3_done, 1)
        link(pool.tensor_scalar(ang[:, NA:], turns[:, NA:], -1.0, None, ALU.mult))
        cos = turns[:, 0:NA].rearrange("p (t f) -> p t f", f=HALF)
        sin = turns[:, NA:].rearrange("p (t f) -> p t f", f=HALF)
        neg = ang[:, NA:].rearrange("p (t f) -> p t f", f=HALF)
        for j, (lo, hi) in enumerate(((cos, cos), (neg, sin), (cos, cos), (neg, sin))):
            for part, src in ((slice(0, HALF), lo), (slice(HALF, HD), hi)):
                link(pool.tensor_tensor(tab[:, j, :, part], src, bc(self.nw[:, j, part], 1, TILES), ALU.mult))
        pool.dma_start(k.dram["ropetab"], tab[:].rearrange("p j t d -> p (j t d)")).then_inc(self.tab_out, 16)
        pool.wait_ge(self.tab_out, 16)

    def sines(self, act):
        act.wait_ge(self.ang_ready, 1)
        act.activation(self.turns[:], self.ang[:], ACT.Sin).then_inc(self.trig3_done, 1)


def s4_phase(k):
    nc, dram = k.nc, k.dram
    ctx = ExitStack()
    sb = lambda name, shape, dt=F32: k.sb(name, shape, dt, ctx)
    NY, NX = NS * B_N, NS * A_N
    NT = NY + 2 * NX + 3 * NS
    s4in = sb("s4in", [P, 5, NS])
    drow = sb("drow", [1, NS])
    len_i = sb("len_i", [P, NB], I32)
    len_f = sb("len_f", [P, NB])
    lmask = sb("lmask", [P, KC, NB])
    xr = sb("xr", [P, KC, NS, NB])
    th = sb("th", [P, 2, NS])
    w1 = sb("w1", [P, 2, NS])
    w2 = sb("w2", [P, 2, NS])
    dm = sb("dm", [P, 2, NS])
    dta = sb("dta", [P, 2, NS])
    sm = sb("sm", [P, 12, NS])
    theta = sb("theta", [P, NT])
    turns = sb("turns", [P, NT])
    trig = sb("trig", [P, NT])
    mag = sb("mag", [P, NY + NX])
    ey = sb("ey", [P, NS, B_N])
    ex1 = sb("ex1", [P, NS, A_N])
    ex2 = sb("ex2", [P, NS, A_N])
    xx = sb("xx", [P, NS, A_N])
    ksb = sb("ksb", [A_N, NS * B_N])
    zeros = sb("zeros", [NS, P])
    RING = 8
    BANKS = RING // 2
    toep = sb("toep", [P, RING, D])
    kps = ctx.enter_context(nc.psum_tensor("kps", [A_N, 2, 512], F32))
    yps = ctx.enter_context(nc.psum_tensor("yps", [P, BANKS, 512], F32))
    const_in, s4_in, u_in, zero_made, kpad_out = (k.sem(n) for n in ("const_in", "s4_in", "u_in", "zero_made", "kpad_out"))
    s4_steps, tanh_done, half_ready, angle_ready, trig_done, expo_ready, mag_done = (
        k.sem(n) for n in ("s4_steps", "tanh_done", "half_ready", "angle_ready", "trig_done", "expo_ready", "mag_done"))
    xy_ready, kern_done, kern_kept = (k.sem(n) for n in ("xy_ready", "kern_done", "kern_kept"))
    toep_in = [k.sem(f"toep_in{s}") for s in range(RING // 2)]
    conv_done, conv_kept = k.sem("conv_done"), k.sem("conv_kept")

    rotary = Rotary(k, sb)

    kpad = dram["kpad"]
    kpad_dst = kpad[:, P:].rearrange("h (a b) -> a h b", b=B_N)

    with nc.Block() as block:
        @block.sync
        def _(sp):
            sp.dma_start(s4in[:], dram["s4in"]).then_inc(s4_in, 16)
            sp.dma_start(k.cst[:], dram["cst"]).then_inc(const_in, 16)
            sp.dma_start(drow[:], dram["L0_cond_D"].unsqueeze(0)).then_inc(s4_in, 16)
            sp.dma_start(len_i[:], dram["len_b"]).then_inc(s4_in, 16)
            rotary.load(sp)
            sp.dma_start(xr[:], dram["x_rev"]).then_inc(u_in, 16)
            sp.wait_ge(zero_made, 1)
            sp.dma_start(kpad[:, 0:P], zeros[:]).then_inc(kpad_out, 16)
            sp.wait_ge(kern_kept, 1)
            sp.dma_start(kpad_dst, ksb[:].rearrange("a (h b) -> a h b", b=B_N)).then_inc(kpad_out, 16)
            sp.wait_ge(kpad_out, 32)
            for s in range(0, RING, 2):
                sp.dma_start(toep[:, s:s + 2, :], dram["toeplitz"](s)).then_inc(toep_in[s // 2], 16)
            with sp.Fori(1, NS // RING) as i:
                for s in range(0, RING, 2):
                    sp.wait_ge(conv_done, i * RING + s - RING + 2)
                    sp.dma_start(toep[:, s:s + 2, :], dram["toeplitz"](i * RING + s)).then_inc(toep_in[s // 2], 16)

        @block.scalar
        def _(act):
            act.wait_ge(s4_in, 48)
            act.activation(th[:], s4in[:, 0:2, :], ACT.Tanh, scale=1.0 / 16).then_inc(tanh_done, 1)
            act.wait_ge(half_ready, 1)
            act.activation(sm[:, 0, :], dta[:, 0, :], ACT.Tanh, scale=0.5).then_inc(tanh_done, 1)
            act.wait_ge(expo_ready, 1)
            act.activation(mag[:], mag[:], ACT.Exp).then_inc(mag_done, 1)
            act.wait_ge(angle_ready, 1)
            act.activation(trig[:], theta[:], ACT.Sin).then_inc(trig_done, 1)
            rotary.sines(act)

        @block.gpsimd
        def _(pool):
            rotary.tables(pool, const_in)

        @block.vector
        def _(dve):
            link = Link(dve, s4_steps)
            TS, TT, STT = dve.tensor_scalar, dve.tensor_tensor, dve.scalar_tensor_tensor
            TT_ = lambda out, a, b, op: link(TT(out, a, b, op))
            dve.memset(zeros[:], 0.0).then_inc(zero_made, 1)
            dve.wait_ge(tanh_done, 1)
            link(TS(w1[:], th[:], -1.0, 1.0, ALU.mult, ALU.add))
            link(dve.reciprocal(w2[:], w1[:]))
            link(STT(out=w1[:], in0=th[:], scalar=1.0, in1=w2[:], op0=ALU.add, op1=ALU.mult))
            TT_(w2[:], w1[:], w1[:], ALU.mult)
            TT_(w1[:], w2[:], w2[:], ALU.mult)
            TT_(dm[:], w1[:], w1[:], ALU.mult)
            dt, mre, im = dm[:, 0, :], dm[:, 1, :], s4in[:, 2, :]
            cr, ci = s4in[:, 3, :], s4in[:, 4, :]
            link(STT(out=dta[:, 0, :], in0=mre, scalar=-1.0, in1=dt, op0=ALU.mult, op1=ALU.mult))
            TT(dta[:, 1, :], im, dt, ALU.mult).then_inc(half_ready, 1)
            dve.wait_ge(const_in, 16)
            dve.wait_ge(half_ready, 1)
            magy = mag[:, 0:NY].rearrange("p (h b) -> p h b", b=B_N)
            magx = mag[:, NY:].rearrange("p (h a) -> p h a", a=A_N)
            bv, av = bc(k.c("bvals"), 1, NS), bc(k.c("avals"), 1, NS)
            link(TT(magy, bc(dta[:, 0, :], 2, B_N), bv, ALU.mult))
            TT(magx, bc(dta[:, 0, :], 2, A_N), av, ALU.mult).then_inc(expo_ready, 1)
            thy = theta[:, 0:NY].rearrange("p (h b) -> p h b", b=B_N)
            thx = [theta[:, NY + j * NX:NY + (j + 1) * NX].rearrange("p (h a) -> p h a", a=A_N) for j in range(2)]
            last = NY + 2 * NX
            link(TT(thy, bc(dta[:, 1, :], 2, B_N), bv, ALU.mult))
            for j in range(2):
                link(TT(thx[j], bc(dta[:, 1, :], 2, A_N), av, ALU.mult))
            link(dve.tensor_copy(theta[:, last:last + 2 * NS].rearrange("p (j h) -> p j h", j=2), bc(dta[:, 1, :], 1, 2)))
            link(TS(theta[:, last + 2 * NS:], dta[:, 1, :], 0.5, None, ALU.mult))
            reduce_angles(link, dve, theta[:], turns[:], [
                ((0, NY + NX), k.c("phase"), 0), ((NY + NX, last), k.c("phase2"), 0),
                ((last, last + NS), k.c("halfpi"), 0), ((last + NS, NT), None, 0)])
            dve.sem_inc(angle_ready, 1)
            dve.wait_ge(tanh_done, 2)
            S = lambda j: sm[:, j, :]
            link(TS(S(1), S(0), -1.0, 1.0, ALU.mult, ALU.add))
            link(dve.reciprocal(S(2), S(1)))
            link(STT(out=S(3), in0=S(0), scalar=2.0, in1=S(2), op0=ALU.mult, op1=ALU.mult))
            dve.wait_ge(trig_done, 1)
            cosb, sinb, sinh = (trig[:, last + j * NS:last + (j + 1) * NS] for j in range(3))
            link(STT(out=S(4), in0=sinh, scalar=-2.0, in1=sinh, op0=ALU.mult, op1=ALU.mult))
            TT_(S(5), S(3), cosb, ALU.mult)
            TT_(S(4), S(4), S(5), ALU.add)
            link(STT(out=S(5), in0=S(3), scalar=1.0, in1=sinb, op0=ALU.add, op1=ALU.mult))
            TT_(S(6), cr, S(4), ALU.mult)
            TT_(S(7), ci, S(5), ALU.mult)
            TT_(S(6), S(6), S(7), ALU.subtract)
            TT_(S(7), cr, S(5), ALU.mult)
            TT_(S(8), ci, S(4), ALU.mult)
            TT_(S(7), S(7), S(8), ALU.add)
            TT_(S(8), mre, mre, ALU.mult)
            TT_(S(9), im, im, ALU.mult)
            TT_(S(8), S(8), S(9), ALU.add)
            link(dve.reciprocal(S(9), S(8)))
            TT_(S(8), S(6), mre, ALU.mult)
            TT_(S(10), S(7), im, ALU.mult)
            TT_(S(8), S(10), S(8), ALU.subtract)
            TT_(S(10), S(7), mre, ALU.mult)
            TT_(S(11), S(6), im, ALU.mult)
            TT_(S(10), S(10), S(11), ALU.add)
            TT_(S(0), S(8), S(9), ALU.mult)
            link(STT(out=S(1), in0=S(10), scalar=-1.0, in1=S(9), op0=ALU.mult, op1=ALU.mult))
            dve.wait_ge(mag_done, 1)
            trigx = [trig[:, NY + j * NX:NY + (j + 1) * NX].rearrange("p (h a) -> p h a", a=A_N) for j in range(2)]
            link(STT(out=ey[:].rearrange("p h b -> p (h b)"), in0=trig[:, 0:NY], scalar=k.c("sign"),
                     in1=mag[:, 0:NY], op0=ALU.mult, op1=ALU.mult))
            TT_(ex1[:], trigx[0], magx, ALU.mult)
            TT_(ex2[:], trigx[1], magx, ALU.mult)
            TT_(ex1[:], ex1[:], bc(S(0), 2, A_N), ALU.mult)
            TT_(ex2[:], ex2[:], bc(S(1), 2, A_N), ALU.mult)
            TT(xx[:], ex1[:], ex2[:], ALU.add).then_inc(xy_ready, 1)
            link(dve.tensor_copy(len_f[:], len_i[:]))
            for c in range(KC):
                link(TS(lmask[:, c, :], len_f[:], k.c("lpos")[:, c:c + 1], None, ALU.is_gt))
            dve.wait_ge(kern_done, 1)
            link(TS(ksb[:].rearrange("a (j n) -> a j n", j=2), kps[:], 2.0, None, ALU.mult))
            tap = ksb[0:1, :].rearrange("a (h b) -> a h b", b=B_N)[:, :, 0]
            TT(tap, tap, drow[:], ALU.add).then_inc(kern_kept, 1)
            with dve.Fori(0, NS // BANKS) as i:
                for s in range(BANKS):
                    dve.wait_ge(conv_done, i * BANKS + s + 1)
                    out = k.y0T[:].rearrange("p c (b h) -> p c b h", h=NS)[:, :, :, bass.ds(i * BANKS + s, 1)]
                    TT(out.rearrange("p c b o -> p c (b o)"), yps[:, s, 0:KC * NB].rearrange("p (c b) -> p c b", b=NB),
                       lmask[:], ALU.mult).then_inc(conv_kept, 1)

        @block.tensor
        def _(pe):
            pe.wait_ge(xy_ready, 1)
            for h in range(NS):
                last = pe.matmul(kps[:, h // 16, (h % 16) * B_N:(h % 16 + 1) * B_N], xx[:, h, :], ey[:, h, :],
                                 start=True, stop=True)
            last.then_inc(kern_done, 1)
            pe.wait_ge(u_in, 16)

            def head(i, s):
                if s % 2 == 0:
                    pe.wait_ge(toep_in[s // 2], i * 16 + 16)
                for d in range(KC):
                    last = pe.matmul(yps[:, s % BANKS, d * NB:KC * NB].rearrange("p (c b) -> p c b", b=NB),
                                     toep[:, s, d * P:(d + 1) * P],
                                     xr[:, 0:KC - d, bass.ds(i * RING + s, 1), :].rearrange("p c o b -> p c (o b)"),
                                     start=(d == 0), stop=(d == KC - 1))
                last.then_inc(conv_done, 1)

            for s in range(RING):
                if s >= BANKS:
                    pe.wait_ge(conv_kept, s - BANKS + 1)
                head(0, s)
            with pe.Fori(1, NS // RING) as i:
                for s in range(RING):
                    pe.wait_ge(conv_kept, i * RING + s - BANKS + 1)
                    head(i, s)
    k.end_phase(ctx)


def peeled(eng, n, body):
    body(0, True)
    with eng.Fori(1, n) as i:
        body(i, False)


def mix_phase(k):
    nc, dram = k.nc, k.dram
    ctx = ExitStack()
    sb = lambda name, shape, dt=F32: k.sb(name, shape, dt, ctx)
    S2 = (0, 1)
    NGZ, NH1 = E0 + E0 * R0, E1 + R1
    xtok = sb("xtok", [P, TILES, D])
    wup = sb("wup", [P, KC, D])
    gzw = sb("gzw", [P, KC, NGZ])
    lb0 = sb("lb0", [E0 * R0, D])
    bias0 = sb("bias0", [P, E0])
    w1t = sb("w1t", [P, KC, D])
    a1h = sb("a1h", [P, KC, NH1])
    a1w = sb("a1w", [P, KC, R1])
    b1 = sb("b1", [P, D])
    lime = sb("lime", [P, E1, R1])
    cidx_i = sb("cidx_i", [P, TILES], I32)
    cidx_f = sb("cidx_f", [P, TILES])
    cidx = sb("cidx", [P, TILES], I32)
    wg = sb("wg", [P, TILES, NS])
    bd = sb("bd", [P, TILES, BPT, NS])
    ys = sb("ys", [P, 2, KC, P])
    lg = sb("lg", [P, 2, 8])
    mx = sb("mx", [P, 2, 8])
    ix = sb("ix", [P, 2, 8], U32)
    ixf = sb("ixf", [P, 2, 1])
    oh = sb("oh", [P, 2, E0])
    zm = sb("zm", [P, 2, E0 * R0])
    zmT = sb("zmT", [E0 * R0, 2, P])
    x1 = sb("x1", [P, 2, D])
    x1b = sb("x1b", [P, 2, D])
    y1T = sb("y1T", [P, 2, KC, P])
    y1d = sb("y1d", [P, 2, KC, P])
    ds1 = sb("ds1", [P, 2, E1, R1])
    pb = ctx.enter_context(nc.psum_tensor("pb", [P, 2, 512], F32))
    ps = ctx.enter_context(nc.psum_tensor("ps", [P, 2, 512], F32))
    pt = ctx.enter_context(nc.psum_tensor("pt", [P, 2, 512], F32))
    ph = ctx.enter_context(nc.psum_tensor("ph", [P, 2, 512], F32))
    idx_in, w0_in, w1_in, x_in, rows_in = (k.sem(n) for n in ("idx_in", "w0_in", "w1_in", "x_in", "rows_in"))
    idx_ready, bd_ready, ys_ready, proj0_done, zm_ready, zmT_done, zmT_kept, base0_done = (
        k.sem(n) for n in ("idx_ready", "bd_ready", "ys_ready", "proj0_done", "zm_ready", "zmT_done", "zmT_kept",
                           "base0_done"))
    x1_ready, y1T_done, y1T_kept, y1d_kept, x1b_ready, h_done, hx_kept, mix_steps = (
        k.sem(n) for n in ("x1_ready", "y1T_done", "y1T_kept", "y1d_kept", "x1b_ready", "h_done", "hx_kept",
                           "mix_steps"))

    passed = k.sem("passed_mix")
    with nc.Block() as block:
        @block.sync
        def _(sp):
            for dst, src, done in ((cidx_i, "cond_b", idx_in), (gzw, "gzw", w0_in), (bias0, "bias0", w0_in),
                                   (wup, "wup", w0_in), (lb0, "lb0", w0_in)):
                sp.dma_start(dst[:], dram[src]).then_inc(done, 16)
            sp.dma_start(xtok[:], dram["xtok"]).then_inc(x_in, 16)
            for dst, src in ((w1t, "w1t"), (a1h, "a1h"), (a1w, "a1w"), (b1, "b1"), (lime, "lime")):
                sp.dma_start(dst[:], dram[src]).then_inc(w1_in, 16)

        @block.gpsimd
        def _(pool):
            pool.wait_ge(idx_ready, 1)
            for t in range(TILES):
                pool.indirect_dma_start(wg[:, t, :], None, dram["l1w"],
                                        bass.IndirectOffsetOnAxis(cidx[:, t:t + 1], 0)).then_inc(rows_in, 16)

            def body(it, first):
                for s in S2:
                    at = it * 2 + s + 1
                    if not first:
                        pool.wait_ge(proj0_done, at - 2)
                    pool.tensor_copy(ys[:, s], k.y0T[:, :, bass.ds((it * 2 + s) * P, P)]).then_inc(ys_ready, 1)
                for s in S2:
                    at = it * 2 + s + 1
                    pool.wait_ge(x1_ready, at)
                    if first:
                        pool.wait_ge(w1_in, 80)
                    else:
                        pool.wait_ge(hx_kept, at - 2)
                    pool.tensor_tensor(x1b[:, s], x1[:, s], b1[:], ALU.add).then_inc(x1b_ready, 1)
            peeled(pool, TILES // 2, body)

        @block.tensor
        def _(pe):
            pe.wait_ge(w0_in, 64)

            def body(it, first):
                for s in S2:
                    at = it * 2 + s + 1
                    pe.wait_ge(ys_ready, at)
                    if not first:
                        pe.wait_ge(hx_kept, at - 2)
                    for c in range(KC):
                        pe.matmul(ps[:, s, 0:NGZ], ys[:, s, c, :], gzw[:, c, :], start=(c == 0), stop=(c == KC - 1))
                    for c in range(KC):
                        last = pe.matmul(pb[:, s, :], ys[:, s, c, :], wup[:, c, :], start=(c == 0), stop=False)
                    last.then_inc(proj0_done, 1)
                for s in S2:
                    pe.wait_ge(zm_ready, it * 2 + s + 1)
                    pe.transpose(ps[0:E0 * R0, s, 64:64 + P], zm[:, s, :], k.c("ident")).then_inc(zmT_done, 1)
                for s in S2:
                    pe.wait_ge(zmT_kept, it * 2 + s + 1)
                    pe.matmul(pb[:, s, :], zmT[:, s, :], lb0[:], start=False, stop=True).then_inc(base0_done, 1)
                if first:
                    pe.wait_ge(bd_ready, 1)
                for s in S2:
                    pe.wait_ge(x1_ready, it * 2 + s + 1)
                    mixer = bd[:].rearrange("p t b d -> p (t b d)")[:, bass.ds((it * 2 + s) * P, P)]
                    for c in range(KC):
                        last = pe.matmul(pt[:, s, c * P:(c + 1) * P], x1[:, s, c * P:(c + 1) * P], mixer,
                                         start=True, stop=True)
                    last.then_inc(y1T_done, 1)
                if first:
                    pe.wait_ge(w1_in, 80)
                for s in S2:
                    at = it * 2 + s + 1
                    pe.wait_ge(y1d_kept, at)
                    for c in range(KC):
                        pe.matmul(ps[:, s, 192:192 + NH1], y1d[:, s, c, :], a1h[:, c, :], start=(c == 0), stop=(c == KC - 1))
                    pe.wait_ge(y1T_kept, at)
                    for c in range(KC):
                        pe.matmul(ps[:, s, 256:256 + R1], y1T[:, s, c, :], a1w[:, c, :], start=(c == 0), stop=(c == KC - 1))
                    for c in range(KC):
                        last = pe.matmul(ph[:, s, :], y1T[:, s, c, :], w1t[:, c, :], start=(c == 0), stop=(c == KC - 1))
                    last.then_inc(h_done, 1)
            peeled(pe, TILES // 2, body)

        @block.scalar
        def _(act):
            def body(it, first):
                for s in S2:
                    act.wait_ge(zmT_done, it * 2 + s + 1)
                    act.copy(zmT[:, s, :], ps[0:E0 * R0, s, 64:64 + P]).then_inc(zmT_kept, 1)
                for s in S2:
                    act.wait_ge(y1T_done, it * 2 + s + 1)
                    act.copy(y1T[:, s].rearrange("p c t -> p (c t)"), pt[:, s, :]).then_inc(y1T_kept, 1)
            peeled(act, TILES // 2, body)

        @block.vector
        def _(dve):
            link = Link(dve, mix_steps)
            dve.wait_ge(idx_in, 16)
            link(dve.tensor_copy(cidx_f[:], cidx_i[:]))
            link(dve.tensor_scalar(cidx_f[:], cidx_f[:], float(NS), k.c("cmod"), ALU.mult, ALU.add))
            dve.tensor_copy(cidx[:], cidx_f[:]).then_inc(idx_ready, 1)
            link(dve.memset(lg[:], NEG))
            dve.wait_ge(rows_in, 16 * TILES)
            wide = lambda ap: ap.rearrange("p t (o d) -> p t o d", o=1).broadcast_to([P, TILES, BPT, NS])
            blk = bc(bc(k.c("block4"), 1, TILES), 3, NS)
            dve.tensor_tensor(bd[:], wide(wg[:]), blk, ALU.mult).then_inc(bd_ready, 1)
            dve.wait_ge(w0_in, 64)
            PER, pre = 12, link.n

            def body(it, first):
                link = Link(dve, mix_steps, pre + it * PER)
                for s in S2:
                    dve.wait_ge(proj0_done, it * 2 + s + 1)
                    link(dve.tensor_tensor(lg[:, s, 0:E0], ps[:, s, 0:E0], bias0[:], ALU.add), passed)
                    link(dve.max(mx[:, s, :], lg[:, s, :]), passed)
                    link(dve.max_index(ix[:, s, :], mx[:, s, :], lg[:, s, :]))
                    link(dve.tensor_copy(ixf[:, s, :], ix[:, s, 0:1]))
                    link(dve.tensor_scalar(oh[:, s, :], k.c("iota8")[:, 0:E0], ixf[:, s, :], None, ALU.is_equal))
                    dve.tensor_tensor(zm[:, s, :].rearrange("p (e r) -> p e r", e=E0),
                                      ps[:, s, E0:NGZ].rearrange("p (e r) -> p e r", e=E0),
                                      bc(oh[:, s, :], 2, R0), ALU.mult).then_inc(zm_ready, 1)
                if first:
                    dve.wait_ge(x_in, 16)
                for s in S2:
                    at = it * 2 + s + 1
                    dve.wait_ge(base0_done, at)
                    if not first:
                        dve.wait_ge(x1b_ready, at - 2)
                    dve.tensor_tensor(x1[:, s, :], pb[:, s, :], xtok[:].rearrange("p t d -> p (t d)")[:, bass.ds((it * 2 + s) * D, D)],
                                      ALU.add).then_inc(x1_ready, 1)
                for s in S2:
                    dve.wait_ge(y1T_kept, it * 2 + s + 1)
                    anchors = y1T[:, s].rearrange("p c (n two) -> p (c n) two", two=2)[:, :, 1]
                    dve.tensor_copy(y1d[:, s].rearrange("p c (n two) -> p (c n) two", two=2), bc(anchors, 2, 2))\
                        .then_inc(y1d_kept, 1)
                if first:
                    dve.wait_ge(w1_in, 80)
                for s in S2:
                    at = it * 2 + s + 1
                    t = it * 2 + s
                    dve.wait_ge(h_done, at)
                    row = lambda ap, n: ap[:, bass.ds(t * n, n)]
                    dve.tensor_copy(row(k.z1, R1), ps[:, s, 256:256 + R1])
                    dve.tensor_tensor(row(k.hs1, E1), ps[:, s, 192:192 + E1], b1[:, 0:E1], ALU.add)
                    link(dve.tensor_tensor(ds1[:, s], bc(ps[:, s, 192 + E1:192 + NH1], 1, E1), lime[:], ALU.mult))
                    dve.tensor_reduce(row(k.ds1, E1), ds1[:, s], AX.X, ALU.add)
                    dve.wait_ge(x1b_ready, at)
                    dve.tensor_tensor(row(k.hx, D), ph[:, s, :], x1b[:, s, :], ALU.add).then_inc(hx_kept, 1)
                assert link.n == PER
            peeled(dve, TILES // 2, body)
    k.end_phase(ctx)


def route_phase(k):
    nc, dram = k.nc, k.dram
    ctx = ExitStack()
    sb = lambda name, shape, dt=F32: k.sb(name, shape, dt, ctx)
    S2 = (0, 1)
    NRH = E2 + E2 * R2
    lime = sb("lime_re", [P, R1, E1])
    bmat = sb("bmat", [R1, D])
    b2t = sb("b2t", [P, KC, AD2 * RC2])
    a2 = sb("a2", [AD2 * RC2, D])
    ids_i = sb("ids_i", [P, TOK], I32)
    amask = sb("amask", [P, TOK])
    rw2 = sb("rw2", [P, KC, NRH])
    w2t = sb("w2t", [P, KC, D])
    lb2 = sb("lb2", [E2 * R2, D])
    bb2 = sb("bb2", [P, D])
    amx = sb("amx", [P, 2])
    gmx = sb("gmx", [P, 2])
    half = sb("half", [P, 2])
    lg = sb("lg1", [P, TILES, E1])
    l2 = sb("lg1b", [P, TILES, E1])
    pr = sb("pr1", [P, TILES, E1])
    sg = sb("sg1", [P, TILES, E1])
    m8 = sb("m8", [P, TILES, 8])
    st = sb("st1", [P, 2, TILES])
    mixed = sb("mixed", [P, TILES, R1, E1])
    zp = sb("zp", [P, TILES, R1])
    zs = sb("zs", [P, 2, R1])
    zpT = sb("zpT", [R1, 2, P])
    x2 = sb("x2", [P, 2, D])
    x2b = sb("x2b", [P, 2, D])
    x2T = sb("x2T", [P, 2, KC, P])
    bxm = sb("bxm", [P, 2, P])
    y2T = sb("y2T", [P, 2, KC, P])
    l8 = sb("l8", [P, 2, E2])
    mx = sb("mx2", [P, 2, 8])
    ix = sb("ix2", [P, 2, 8], U32)
    ixf = sb("ixf2", [P, 2, 2])
    nm = sb("nm2", [P, 2, 1])
    ex = sb("ex_2", [P, 2, E2])
    oh = sb("oh2", [P, 2, E2])
    em = sb("em2", [P, 2, E2])
    sr = sb("sr2", [P, 2, 2])
    hw = sb("hw2", [P, 2, E2 * R2])
    hwT = sb("hwT2", [E2 * R2, 2, P])
    x3 = sb("x3", [P, 2, D])
    pb = ctx.enter_context(nc.psum_tensor("pb2", [P, 2, 512], F32))
    ps = ctx.enter_context(nc.psum_tensor("ps2", [P, 2, 512], F32))
    pt = ctx.enter_context(nc.psum_tensor("pt2", [P, 2, 512], F32))
    ph = ctx.enter_context(nc.psum_tensor("ph2", [P, 2, 512], F32))
    r_in, w2_in, amx_ready, gmx_ready, lg_ready, ex1_done, pr_ready, sg1_done, amask_ready, route_steps, tile_steps = (
        k.sem(n) for n in ("r_in", "w2_in", "amx_ready", "gmx_ready", "lg_ready", "ex1_done", "pr_ready", "sg1_done",
                           "amask_ready", "route_steps", "tile_steps"))
    zs_ready, zpT_done, zpT_kept, delta_done, x2_ready, x2T_done, x2T_kept, bx_done, bxm_ready, y2T_done, y2T_kept = (
        k.sem(n) for n in ("zs_ready", "zpT_done", "zpT_kept", "delta_done", "x2_ready", "x2T_done", "x2T_kept",
                           "bx_done", "bxm_ready", "y2T_done", "y2T_kept"))
    x2b_ready, rh_done, nm_ready, ex2_done, hw_ready, hwT_done, hwT_kept, base2_done, x3_ready, x3T_done, x3h_kept, x3l_kept = (
        k.sem(n) for n in ("x2b_ready", "rh_done", "nm_ready", "ex2_done", "hw_ready", "hwT_done", "hwT_kept",
                           "base2_done", "x3_ready", "x3T_done", "x3h_kept", "x3l_kept"))
    x3_out = [k.sem("x3_out0"), k.sem("x3_out1")]
    x3res = dram["x3res"].rearrange("(t p) d -> t p d", p=P)

    passed = k.sem("passed_route")
    with nc.Block() as block:
        @block.sync
        def _(sp):
            for dst, src in ((lime, "lime_re"), (bmat, "bmat"), (ids_i, "ids_b"), (b2t, "b2t"), (a2, "a2")):
                sp.dma_start(dst[:], dram[src]).then_inc(r_in, 16)
            for dst, src in ((rw2, "rw2"), (w2t, "w2t"), (lb2, "lb2"), (bb2, "bb2")):
                sp.dma_start(dst[:], dram[src]).then_inc(w2_in, 16)

            def body(it, first):
                for s in S2:
                    sp.wait_ge(x3_ready, it * 2 + s + 1)
                    sp.dma_start(x3res[bass.ds(it * 2 + s, 1)].rearrange("o p d -> (o p) d"), x3[:, s, :])\
                        .then_inc(x3_out[s], 16)
            peeled(sp, TILES // 2, body)
            for s in S2:
                sp.wait_ge(x3_out[s], 16 * TILES // 2)

        @block.gpsimd
        def _(pool):
            pool.wait_ge(amx_ready, 1)
            pool.partition_all_reduce(gmx[:], amx[:], P, bass.bass_isa.ReduceOp.max).then_inc(gmx_ready, 1)
            pool.wait_ge(w2_in, 64)

            def body(it, first):
                for s in S2:
                    at = it * 2 + s + 1
                    pool.wait_ge(x2_ready, at)
                    if not first:
                        pool.wait_ge(x3_ready, at - 2)
                    pool.tensor_tensor(x2b[:, s], x2[:, s], bb2[:], ALU.add).then_inc(x2b_ready, 1)
            peeled(pool, TILES // 2, body)

        @block.tensor
        def _(pe):
            pe.wait_ge(r_in, 80)

            def body(it, first):
                for s in S2:
                    at = it * 2 + s + 1
                    pe.wait_ge(zs_ready, at)
                    pe.transpose(ps[0:R1, s, 0:P], zs[:, s, :], k.c("ident")).then_inc(zpT_done, 1)
                for s in S2:
                    pe.wait_ge(zpT_kept, it * 2 + s + 1)
                    pe.matmul(pb[:, s, :], zpT[:, s, :], bmat[:], start=True, stop=True).then_inc(delta_done, 1)
                for s in S2:
                    at = it * 2 + s + 1
                    pe.wait_ge(x2_ready, at)
                    if not first:
                        pe.wait_ge(x3l_kept, at - 2)
                    for c in range(KC):
                        last = pe.transpose(pt[:, s, c * P:(c + 1) * P], x2[:, s, c * P:(c + 1) * P], k.c("ident"))
                    last.then_inc(x2T_done, 1)
                for s in S2:
                    pe.wait_ge(x2T_kept, it * 2 + s + 1)
                    for c in range(KC):
                        last = pe.matmul(ps[:, s, P:2 * P], b2t[:, c, :], x2T[:, s, c, :], start=(c == 0), stop=(c == KC - 1))
                    last.then_inc(bx_done, 1)
                for s in S2:
                    pe.wait_ge(bxm_ready, it * 2 + s + 1)
                    for c in range(KC):
                        last = pe.matmul(ph[:, s, c * P:(c + 1) * P], a2[:, c * P:(c + 1) * P], bxm[:, s, :],
                                         start=True, stop=True)
                    last.then_inc(y2T_done, 1)
                if first:
                    pe.wait_ge(w2_in, 64)
                for s in S2:
                    pe.wait_ge(y2T_kept, it * 2 + s + 1)
                    for c in range(KC):
                        last = pe.matmul(ps[:, s, 256:256 + NRH], y2T[:, s, c, :], rw2[:, c, :], start=(c == 0), stop=(c == KC - 1))
                    last.then_inc(rh_done, 1)
                    for c in range(KC):
                        pe.matmul(pb[:, s, :], y2T[:, s, c, :], w2t[:, c, :], start=(c == 0), stop=False)
                for s in S2:
                    pe.wait_ge(hw_ready, it * 2 + s + 1)
                    pe.transpose(ps[:, s, 0:P], hw[:, s, :], k.c("ident")).then_inc(hwT_done, 1)
                for s in S2:
                    pe.wait_ge(hwT_kept, it * 2 + s + 1)
                    pe.matmul(pb[:, s, :], hwT[:, s, :], lb2[:], start=False, stop=True).then_inc(base2_done, 1)
                for s in S2:
                    pe.wait_ge(x3_ready, it * 2 + s + 1)
                    for c in range(KC):
                        last = pe.transpose(pt[:, s, c * P:(c + 1) * P], x3[:, s, c * P:(c + 1) * P], k.c("ident"))
                    last.then_inc(x3T_done, 1)
            peeled(pe, TILES // 2, body)

        @block.scalar
        def _(act):
            act.wait_ge(lg_ready, 1)
            act.activation(pr[:], l2[:], ACT.Exp).then_inc(ex1_done, 1)
            act.wait_ge(pr_ready, 1)
            act.activation(sg[:], sg[:], ACT.Exp, scale=-2.0).then_inc(sg1_done, 1)

            def body(it, first):
                for s in S2:
                    act.wait_ge(zpT_done, it * 2 + s + 1)
                    act.copy(zpT[:, s, :], ps[0:R1, s, 0:P]).then_inc(zpT_kept, 1)
                for s in S2:
                    act.wait_ge(x2T_done, it * 2 + s + 1)
                    act.copy(x2T[:, s].rearrange("p c t -> p (c t)"), pt[:, s, :]).then_inc(x2T_kept, 1)
                for s in S2:
                    act.wait_ge(y2T_done, it * 2 + s + 1)
                    act.copy(y2T[:, s].rearrange("p c t -> p (c t)"), ph[:, s, :]).then_inc(y2T_kept, 1)
                for s in S2:
                    act.wait_ge(nm_ready, it * 2 + s + 1)
                    act.activation(ex[:, s, :], l8[:, s, :], ACT.Exp, bias=nm[:, s, :]).then_inc(ex2_done, 1)
                for s in S2:
                    act.wait_ge(hwT_done, it * 2 + s + 1)
                    act.copy(hwT[:, s, :], ps[:, s, 0:P]).then_inc(hwT_kept, 1)
                for s in S2:
                    at = it * 2 + s + 1
                    act.wait_ge(x3T_done, at)
                    tile = k.x3h[:, :, bass.ds((it * 2 + s) * P, P)]
                    act.copy(tile, pt[:, s, :].rearrange("p (c t) -> p c t", c=KC)).then_inc(x3h_kept, 1)
            peeled(act, TILES // 2, body)

        @block.vector
        def _(dve):
            link = Link(dve, route_steps)
            TS, TT, STT = dve.tensor_scalar, dve.tensor_tensor, dve.scalar_tensor_tensor
            hs = k.hs1[:].rearrange("p (t e) -> p t e", e=E1)
            dl = k.ds1[:].rearrange("p (t e) -> p t e", e=E1)
            link(dve.tensor_reduce(amx[:, 0:1], k.hs1[:], AX.X, ALU.max, apply_absolute_value=True))
            dve.tensor_reduce(amx[:, 1:2], k.ds1[:], AX.X, ALU.max, apply_absolute_value=True).then_inc(amx_ready, 1)
            dve.wait_ge(gmx_ready, 1)
            link(TS(gmx[:], gmx[:], 1e-6, None, ALU.max))
            link(dve.reciprocal(half[:], gmx[:]))
            link(TS(half[:], half[:], 0.5, None, ALU.mult))
            link(TS(lg[:], hs, half[:, 0:1], None, ALU.mult))
            link(STT(out=lg[:], in0=dl, scalar=half[:, 1:2], in1=lg[:], op0=ALU.mult, op1=ALU.add))
            link(dve.tensor_reduce(st[:, 0, :], lg[:], AX.X, ALU.max))
            TT(l2[:], lg[:], bc(st[:, 0, :], 2, E1), ALU.subtract).then_inc(lg_ready, 1)
            dve.wait_ge(ex1_done, 1)
            link(dve.tensor_reduce(st[:, 1, :], pr[:], AX.X, ALU.add))
            link(dve.reciprocal(st[:, 0, :], st[:, 1, :]))
            link(TT(pr[:], pr[:], bc(st[:, 0, :], 2, E1), ALU.mult))
            for t in range(TILES):
                link(dve.max(m8[:, t, :], pr[:, t, :]))
            TT(sg[:], pr[:], bc(m8[:, :, 1], 2, E1), ALU.subtract).then_inc(pr_ready, 1)
            dve.wait_ge(sg1_done, 1)
            link(TS(sg[:], sg[:], 1.0, None, ALU.add))
            link(dve.reciprocal(l2[:], sg[:]))
            link(TT(pr[:], pr[:], l2[:], ALU.mult))
            link(dve.tensor_reduce(st[:, 1, :], pr[:], AX.X, ALU.add))
            link(TS(st[:, 1, :], st[:, 1, :], 1e-9, None, ALU.add))
            link(dve.reciprocal(st[:, 0, :], st[:, 1, :]))
            link(TT(pr[:], pr[:], bc(st[:, 0, :], 2, E1), ALU.mult))
            dve.wait_ge(r_in, 80)
            link(TT(mixed[:], pr[:].rearrange("p t (o e) -> p t o e", o=1).broadcast_to([P, TILES, R1, E1]),
                    bc(lime[:], 1, TILES), ALU.mult))
            link(dve.tensor_reduce(zp[:], mixed[:], AX.X, ALU.add))
            link(STT(out=zp[:], in0=zp[:], scalar=0.5, in1=k.z1[:].rearrange("p (t r) -> p t r", r=R1),
                     op0=ALU.mult, op1=ALU.mult))
            link(dve.tensor_copy(amask[:], ids_i[:]))
            link(TS(amask[:], amask[:], k.c("adapter"), None, ALU.is_equal))
            PER = 20

            def body(it, first):
                link = Link(dve, tile_steps, it * PER)
                for s in S2:
                    at = it * 2 + s + 1
                    dve.tensor_copy(zs[:, s, :], zp[:].rearrange("p t r -> p (t r)")[:, bass.ds((it * 2 + s) * R1, R1)])\
                        .then_inc(zs_ready, 1)
                for s in S2:
                    at = it * 2 + s + 1
                    dve.wait_ge(delta_done, at)
                    TT(x2[:, s, :], pb[:, s, :], k.hx[:, bass.ds((it * 2 + s) * D, D)], ALU.add).then_inc(x2_ready, 1)
                for s in S2:
                    dve.wait_ge(bx_done, it * 2 + s + 1)
                    TT(bxm[:, s, :], ps[:, s, P:2 * P], amask[:, bass.ds((it * 2 + s) * P, P)], ALU.mult).then_inc(bxm_ready, 1)
                if first:
                    dve.wait_ge(w2_in, 64)
                for s in S2:
                    at = it * 2 + s + 1
                    dve.wait_ge(rh_done, at)
                    link(dve.tensor_copy(l8[:, s, :], ps[:, s, 256:256 + E2]), passed)
                    link(dve.max(mx[:, s, :], l8[:, s, :]))
                    TS(nm[:, s, :], mx[:, s, 0:1], -1.0, None, ALU.mult).then_inc(nm_ready, 1)
                    link(dve.max_index(ix[:, s, :], mx[:, s, :], l8[:, s, :]))
                    link(dve.tensor_copy(ixf[:, s, :], ix[:, s, 0:2]))
                    link(TS(oh[:, s, :], k.c("iota8"), ixf[:, s, 0:1], None, ALU.is_equal))
                    link(STT(out=oh[:, s, :], in0=k.c("iota8"), scalar=ixf[:, s, 1:2], in1=oh[:, s, :],
                             op0=ALU.is_equal, op1=ALU.add))
                    dve.wait_ge(ex2_done, at)
                    link(TT(em[:, s, :], ex[:, s, :], oh[:, s, :], ALU.mult))
                    link(dve.tensor_reduce(sr[:, s, 0:1], em[:, s, :], AX.X, ALU.add))
                    link(dve.reciprocal(sr[:, s, 1:2], sr[:, s, 0:1]))
                    link(TS(em[:, s, :], em[:, s, :], sr[:, s, 1:2], 2.0, ALU.mult, ALU.mult))
                    TT(hw[:, s, :].rearrange("p (e r) -> p e r", e=E2),
                       ps[:, s, 256 + E2:256 + NRH].rearrange("p (e r) -> p e r", e=E2),
                       bc(em[:, s, :], 2, R2), ALU.mult).then_inc(hw_ready, 1)
                for s in S2:
                    at = it * 2 + s + 1
                    dve.wait_ge(base2_done, at)
                    dve.wait_ge(x2b_ready, at)
                    if not first:
                        dve.wait_ge(x3_out[s], it * 16)
                    TT(x3[:, s, :], pb[:, s, :], x2b[:, s, :], ALU.add).then_inc(x3_ready, 1)
                for s in S2:
                    at = it * 2 + s + 1
                    dve.wait_ge(x3h_kept, at)
                    tok = bass.ds((it * 2 + s) * P, P)
                    TT(k.x3l[:, :, tok], pt[:, s, :].rearrange("p (c t) -> p c t", c=KC),
                       k.x3h[:, :, tok].bitcast(F32), ALU.subtract).then_inc(x3l_kept, 1)
                assert link.n == PER, link.n
            peeled(dve, TILES // 2, body)
    k.end_phase(ctx)


HH = HK // 2
UT = TILES
def project_phase(k, hh):
    nc, dram = k.nc, k.dram
    ctx = ExitStack()
    sb = lambda name, shape, dt=F32: k.sb(name, shape, dt, ctx)
    W4 = HH * HD
    tab = sb(f"rtab{hh}", [P, 4, TILES, HD])
    wraw = sb(f"wraw{hh}", [P, KC, W4])
    wh = sb(f"wh{hh}", [P, 2, KC, W4], F32R)
    wl = sb(f"wl{hh}", [P, 2, KC, W4], F32R)
    sq = sb(f"sq{hh}", [P, HH, HD])
    ss = sb(f"ss{hh}", [P, 2, HH])
    rt = sb(f"rt{hh}", [P, 2, HH])
    ri = sb(f"ri{hh}", [P, 4, HH])
    qc = sb(f"qc{hh}", [P, 4, W4])
    vs = qc[:, 2:4]
    qs = sb(f"qs{hh}", [P, 2, W4])
    pq = ctx.enter_context(nc.psum_tensor(f"pq{hh}", [P, 4, 512], F32))
    pt = ctx.enter_context(nc.psum_tensor(f"ptq{hh}", [P, 2, 512], F32))
    n = lambda name: k.sem(f"{name}{hh}")
    wraw_in = [n(f"wraw_in{c}_") for c in range(KC)]
    tab_in, whigh, wlow, proj_done, v_kept, ss_ready, qrt_ready = (
        n(x) for x in ("tab_in", "whigh", "wlow", "proj_done", "v_kept", "ss_ready", "qrt_ready"))
    parts_ready, sum_ready, q_ready, qT_done, qT_kept, ss_done = (
        n(x) for x in ("parts_ready", "sum_ready", "q_ready", "qT_done", "qT_kept", "ss_done"))
    v_out = [n("v_out_a"), n("v_out_b")]
    GROUPS = 2 + HH
    wsrc = dram["wqkv"]
    vdst = dram["vnew"].rearrange("h (t p) d -> h t p d", p=P)[hh]

    def unit(j, t):
        return j * UT + t

    with nc.Block() as block:
        @block.sync
        def _(sp):
            for c in range(KC):
                sp.dma_start(wraw[:, c, :], wsrc[hh, 0, :, c, :]).then_inc(wraw_in[c], 16)
            sp.dma_start(tab[:].rearrange("p j t d -> p (j t d)"), dram["ropetab"]).then_inc(tab_in, 16)
            for j in range(1, GROUPS):
                for c in range(KC):
                    sp.wait_ge(wlow, (j - 1) * KC + c + 1)
                    sp.dma_start(wraw[:, c, :], wsrc[hh, j, :, c, :]).then_inc(wraw_in[c], 16)
                if j == 1:
                    for t in range(TILES):
                        sp.wait_ge(v_kept, t + 1)
                        sp.dma_start(vdst[t], vs[:, t % 2, :]).then_inc(v_out[t % 2], 16)
            for o in v_out:
                sp.wait_ge(o, 16 * TILES // 2)

        @block.tensor
        def _(pe):
            def project(slot, t, g):
                i = 0
                for c in range(KC):
                    if t == 0:
                        pe.wait_ge(wlow, g * KC + c + 1)
                    for x, w in ((k.x3h, wh), (k.x3h, wl), (k.x3l, wh)):
                        last = pe.matmul(pq[:, t % 4, :], x[:, c, t * P:(t + 1) * P], w[:, slot, c, :],
                                         start=(i == 0), stop=(i == 3 * KC - 1))
                        i += 1
                last.then_inc(proj_done, 1)

            def turn(t, r):
                pe.wait_ge(q_ready, r + 1)
                if not isinstance(r, int) or r >= 2:
                    pe.wait_ge(qT_kept, r - 1)
                for g in range(HH):
                    last = pe.transpose(pt[:, t % 2, g * P:(g + 1) * P], qc[:, t % 4, g * HD:(g + 1) * HD], k.c("ident"))
                last.then_inc(qT_done, 1)

            for t in range(TILES):
                if t >= 4:
                    pe.wait_ge(v_kept, t - 3)
                project(0, t, 0)

            def rotated(j, slot, k_group):
                for t in range(TILES):
                    r = j * TILES + t
                    if k_group and t < 4:
                        pe.wait_ge(v_kept, 5 + t)
                    else:
                        pe.wait_ge(parts_ready, r - 3)
                    project(slot, t, j + 1)
                    if not (k_group and t < 3):
                        turn((t - 3) % TILES, r - 3)
            rotated(0, 1, True)
            with pe.Fori(0, HH // 2) as i:
                for s in range(2):
                    rotated(i * 2 + s + 1, s, False)
            R = (1 + HH) * TILES
            for r in (R - 3, R - 2, R - 1):
                turn(r % TILES, r)

        @block.scalar
        def _(act):
            for t in range(TILES):
                act.wait_ge(proj_done, t + 1)
                if t >= 2:
                    act.wait_ge(v_out[t % 2], 16 * (t // 2))
                act.copy(vs[:, t % 2, :], pq[:, t % 4, :]).then_inc(v_kept, 1)

            def keep(t, r, group):
                act.wait_ge(qT_done, r + 1)
                dst = k.qkT[:, t * BPT:(t + 1) * BPT, bass.ds(group * HH, HH), :]
                act.copy(dst, pt[:, t % 2, :].rearrange("p (h b n) -> p b h n", h=HH, b=BPT)).then_inc(qT_kept, 1)

            def rotated(j, k_group):
                for t in range(TILES):
                    r = j * TILES + t
                    act.wait_ge(proj_done, TILES + r + 1)
                    if not (k_group and t < 2):
                        act.wait_ge(qrt_ready, r - 1)
                    for g in range(HH):
                        last = act.activation(sq[:, g], pq[:, t % 4, g * HD:(g + 1) * HD], ACT.Square,
                                              accum_out=ss[:, t % 2, g:g + 1])
                    last.then_inc(ss_done, 1)
                    act.wait_ge(ss_done, r + 1)
                    act.activation(rt[:, t % 2, :], ss[:, t % 2, :], ACT.Sqrt, scale=1.0 / HD, bias=k.c("eps")).then_inc(ss_ready, 1)
                    if not (k_group and t < 3):
                        keep((t - 3) % TILES, r - 3, j if t >= 3 else j - 1)
            rotated(0, True)
            with act.Fori(1, 1 + HH) as j:
                rotated(j, False)
            R = (1 + HH) * TILES
            for r in (R - 3, R - 2, R - 1):
                keep(r % TILES, r, HH)

        @block.vector
        def _(dve):
            def split(g, c):
                dve.wait_ge(wraw_in[c], g * 16 + 16)
                if c == 0 and (not isinstance(g, int) or g >= 2):
                    dve.wait_ge(proj_done, (g - 1) * TILES)
                high, low = (w[:, bass.ds(g % 2, 1), c, :].rearrange("p o n -> p (o n)") for w in (wh, wl))
                dve.tensor_copy(high, wraw[:, c, :]).then_inc(whigh, 1)
                dve.wait_ge(whigh, g * KC + c + 1)
                dve.tensor_tensor(low, wraw[:, c, :], high.bitcast(F32), ALU.subtract).then_inc(wlow, 1)

            for g in range(2):
                for c in range(KC):
                    split(g, c)
            dve.wait_ge(tab_in, 16)

            def scale(t, r):
                dve.wait_ge(sum_ready, r + 1)
                dve.wait_ge(qrt_ready, r + 1)
                v = qc[:, t % 4, :].rearrange("p (g d) -> p g d", d=HD)
                dve.tensor_tensor(v, v, bc(ri[:, t % 4, :], 2, HD), ALU.mult).then_inc(q_ready, 1)

            def rotated(j, k_group, more):
                cosw, sinw = (tab[:, 2], tab[:, 3]) if k_group else (tab[:, 0], tab[:, 1])
                for t in range(TILES):
                    r = j * TILES + t
                    dve.wait_ge(ss_ready, r + 1)
                    if not (k_group and t < 4):
                        dve.wait_ge(qT_done, r - 3)
                    elif t >= 2:
                        dve.wait_ge(v_out[t % 2], 16 * TILES // 2)
                    dve.reciprocal(ri[:, t % 4, :], rt[:, t % 2, :]).then_inc(qrt_ready, 1)
                    src = pq[:, t % 4, :].rearrange("p (g d) -> p g d", d=HD)
                    dst = qc[:, t % 4, :].rearrange("p (g d) -> p g d", d=HD)
                    dve.tensor_tensor(dst, src, bc(cosw[:, t], 1, HH), ALU.mult)
                    src2 = pq[:, t % 4, :].rearrange("p (g two f) -> p g two f", two=2, f=HD // 2)
                    dst2 = qs[:, t % 2, :].rearrange("p (g two f) -> p g two f", two=2, f=HD // 2)
                    for o in range(2):
                        last = dve.tensor_tensor(dst2[:, :, o], src2[:, :, 1 - o],
                                                 bc(sinw[:, t, o * HD // 2:(o + 1) * HD // 2], 1, HH), ALU.mult)
                    last.then_inc(parts_ready, 1)
                    if not (k_group and t < 1):
                        scale((t - 1) % TILES, r - 1)
                    if t < KC and more:
                        split(j + 2, t)
            rotated(0, True, True)
            with dve.Fori(1, HH) as j:
                rotated(j, False, True)
            rotated(HH, False, False)
            scale(TILES - 1, (1 + HH) * TILES - 1)

        @block.gpsimd
        def _(pool):
            def rotated(j):
                for t in range(TILES):
                    pool.wait_ge(parts_ready, j * TILES + t + 1)
                    pool.tensor_tensor(qc[:, t % 4, :], qc[:, t % 4, :], qs[:, t % 2, :], ALU.add).then_inc(sum_ready, 1)
            with pool.Fori(0, 1 + HH) as j:
                rotated(j)
    k.end_phase(ctx)


def attend_phase(k, hh):
    nc, dram = k.nc, k.dram
    ctx = ExitStack()
    sb = lambda name, shape, dt=F32: k.sb(f"{name}{hh}", shape, dt, ctx)
    n = lambda name: k.sem(f"{name}{hh}")
    SLOTS = NPP + 1
    CUT = 9
    CA, CB = CUT * PS, (SLOTS - CUT) * PS
    VC = CL // P
    PG = 6
    PA = PG + 2
    table = sb("table", [1, NB * NPP], I32)
    pages = sb("pages", [P, NB * NPP], I32)
    pages_f = sb("pages_f", [P, NB * NPP])
    kidx = sb("kidx", [P, 2, PG], I32)
    rows = sb("rows", [P, NB * VC], I32)
    rows_f = sb("rows_f", [P, NB * VC])
    vidx = sb("vidx", [P, 2, VC], I32)
    len_i = sb("klen_i", [P, NB], I32)
    len_f = sb("klen_f", [P, NB])
    kqb = sb("kqb", [P, 2, SLOTS * HH + HH * G, PS])
    kb = kqb[:, :, 0:SLOTS * HH, :].rearrange("p s (j h) t -> p s j h t", h=HH)
    qb = kqb[:, :, SLOTS * HH:, :]
    vb = sb("vb", [P, 2, VC + 1, HH * HD])
    mask = sb("mask", [P, 2, KL])
    sm = sb("smax", [P, 2, KL])
    pm = sb("pm", [P, 4, KL])
    mxs = sb("mxs", [P, 2, 2])
    nmx = sb("nmx", [P, 2])
    rs = sb("rs", [P, 2])
    rv = sb("rv", [P, 2])
    pT = sb("pT", [P, 2, VC * P + P])
    sps = ctx.enter_context(nc.psum_tensor(f"sps{hh}", [P, 2, 2, 512], F32))
    tps = ctx.enter_context(nc.psum_tensor(f"tps{hh}", [P, 2, 512], F32))
    ops = ctx.enter_context(nc.psum_tensor(f"ops{hh}", [P, 2, 512], F32))
    att_in, rows_ready, att_steps, mask_ready, vidx_ready, kq_ready = (
        n(x) for x in ("att_in", "rows_ready", "att_steps", "mask_ready", "vidx_ready", "kq_ready"))
    table_ready = n("table_ready")
    k_in = [n("k_in_a"), n("k_in_b")]
    kg_in = [n("kg_in_a"), n("kg_in_b")]
    v_in = [n("v_in_a"), n("v_in_b")]
    vn_in = [n("vn_in_a"), n("vn_in_b")]
    qk_done, max_a, max_done, nmx_ready, exp_done, rv_ready, p_ready, t_done, pT_kept, pv_done, o_kept = (
        n(x) for x in ("qk_done", "max_a", "max_done", "nmx_ready", "exp_done", "rv_ready", "p_ready", "t_done",
                       "pT_kept", "pv_done", "o_kept"))
    krows = dram["kpages"].rearrange("r d c -> (r d) c")
    kpages, vrows, vnew = dram["kpages"], dram[f"vrows{hh}"], dram["vnew"][hh]
    NU, BU = 2 * HH, 2

    passed = k.sem(f"passed_attend{hh}")

    def load_page(eng, b, s, j):
        page = eng.value_load(table[0:1, bass.ds(b * NPP + j, 1)], min_val=0, max_val=2 * PAGES - 1)
        eng.dma_start(kb[:, s, j], kpages[bass.ds(page, 1)].rearrange("o p (h t) -> (o p) h t", h=HH)).then_inc(k_in[s], 16)

    with nc.Block() as block:
        @block.sync
        def _(sp):
            sp.dma_start(table[:], dram["table"]).then_inc(att_in, 16)
            sp.dma_start(rows[:], dram["table_b"]).then_inc(att_in, 16)
            sp.dma_start(pages[:], dram["table_rep"]).then_inc(att_in, 16)
            sp.dma_start(len_i[:], dram["start_rep"]).then_inc(att_in, 16)
            sp.wait_ge(table_ready, 1)

            def body(i, first):
                for s in range(2):
                    b = i * 2 + s
                    if not first:
                        sp.wait_ge(qk_done, (b - 1) * HH)
                    for j in range(PA, NPP):
                        load_page(sp, b, s, j)
                    if not first:
                        sp.wait_ge(pv_done, (b - 1) * HH)
                    sp.dma_start(vb[0:NS, s, VC, :], vnew[bass.ds(b * NS, NS), :]).then_inc(vn_in[s], 16)
            peeled(sp, NB // 2, body)

        @block.gpsimd
        def _(pool):
            pool.wait_ge(rows_ready, 1)

            def body(i, first):
                for s in range(2):
                    b = i * 2 + s
                    if not first:
                        pool.wait_ge(v_in[s], i * (16 * VC))
                        pool.wait_ge(kg_in[s], i * (16 * PG))
                    pool.tensor_copy(vidx[:, s, :], rows[:, bass.ds(b * VC, VC)])
                    pool.tensor_copy(kidx[:, s, :], pages[:, bass.ds(b * NPP, PG)]).then_inc(vidx_ready, 1)
                    if not first:
                        pool.wait_ge(qk_done, (b - 1) * HH)
                        pool.sem_inc(passed, 1)
                    pool.wait_ge(vidx_ready, b + 1)
                    pool.sem_inc(passed, 1)
                    for j in range(PG):
                        pool.indirect_dma_start(kb[:, s, j].rearrange("p h t -> p (h t)"), None, krows,
                                                bass.IndirectOffsetOnAxis(kidx[:, s, j:j + 1], 0)).then_inc(kg_in[s], 16)
                    if not first:
                        lone_wait(pool, pv_done, (b - 1) * HH, passed)
                    for c in range(VC):
                        pool.indirect_dma_start(vb[:, s, c, :], None, vrows,
                                                bass.IndirectOffsetOnAxis(vidx[:, s, c:c + 1], 0)).then_inc(v_in[s], 16)
            peeled(pool, NB // 2, body)

        @block.tensor
        def _(pe):
            def scores(i, m, first):
                s, h, us = m // HH, m % HH, m % 2
                u = i * NU + m
                if h == 0:
                    pe.wait_ge(k_in[s], i * (16 * (NPP - PG)) + 16 * (NPP - PG))
                    pe.wait_ge(kg_in[s], i * (16 * PG) + 16 * PG)
                    pe.wait_ge(kq_ready, i * 2 + s + 1)
                if not (first and m < 2):
                    pe.wait_ge(max_done, u - 1)
                q = qb[:, s, h * G:(h + 1) * G, :].rearrange("p g n -> p (g n)")
                pe.matmul(sps[:, us, 0, 0:CA].rearrange("p (j t) -> p j t", t=PS), q, kb[:, s, 0:CUT, h, :],
                          start=True, stop=True)
                pe.matmul(sps[:, us, 1, 0:CB].rearrange("p (j t) -> p j t", t=PS), q, kb[:, s, CUT:, h, :],
                          start=True, stop=True).then_inc(qk_done, 1)

            def turn(m, u):
                us = m % 4
                pe.wait_ge(p_ready, u + 1)
                if not isinstance(u, int) or u > 0:
                    pe.wait_ge(pT_kept, u)
                for c in range(VC):
                    pe.transpose(tps[:, 0, c * P:(c + 1) * P], pm[:, us, c * P:(c + 1) * P], k.c("ident"))
                pe.transpose(tps[0:NS, 1, 0:P], pm[:, us, CL:KL], k.c("ident")).then_inc(t_done, 1)

            def values(i, m, u):
                s, h, us = m // HH, m % HH, m % 2
                if h == 0:
                    pe.wait_ge(v_in[s], i * (16 * VC) + 16 * VC)
                    pe.wait_ge(vn_in[s], i * 16 + 16)
                pe.wait_ge(pT_kept, u + 1)
                if not isinstance(u, int) or u >= 2:
                    pe.wait_ge(o_kept, u - 1)
                for c in range(VC):
                    pe.matmul(ops[:, us, 0:P], vb[:, s, c, h * HD:(h + 1) * HD], pT[:, us, c * P:(c + 1) * P],
                              start=(c == 0), stop=False)
                pe.matmul(ops[:, us, 0:P], vb[0:NS, s, VC, h * HD:(h + 1) * HD], pT[0:NS, us, VC * P:],
                          start=False, stop=True).then_inc(pv_done, 1)

            def body(i, first):
                for m in range(NU):
                    u = i * NU + m
                    scores(i, m, first)
                    if not (first and m < 2):
                        turn((m - 2) % NU, u - 2)
                    if not (first and m < 3):
                        values(i if m >= 3 else i - 1, (m - 3) % NU, u - 3)
            pe.wait_ge(mask_ready, 1)
            peeled(pe, NB // 2, body)
            U = NB * HH
            turn(NU - 2, U - 2)
            values(NB // 2 - 1, NU - 3, U - 3)
            turn(NU - 1, U - 1)
            values(NB // 2 - 1, NU - 2, U - 2)
            values(NB // 2 - 1, NU - 1, U - 1)

        @block.scalar
        def _(act):
            def keep(m, u):
                us = m % 2
                act.wait_ge(t_done, u + 1)
                if not isinstance(u, int) or u >= 2:
                    act.wait_ge(pv_done, u - 1)
                act.copy(pT[:, us, 0:CL], tps[:, 0, :])
                act.copy(pT[0:NS, us, CL:], tps[0:NS, 1, 0:P]).then_inc(pT_kept, 1)

            def fetch(b, s):
                if not isinstance(b, int) or b >= 2:
                    act.wait_ge(qk_done, (b - 1) * HH)
                for j in range(PG, PA):
                    load_page(act, b, s, j)

            act.wait_ge(table_ready, 1)
            fetch(0, 0)

            def body(i, first, last):
                for m in range(NU):
                    us, u = m % 2, i * NU + m
                    if m % HH == 1 and not (last and m > HH):
                        fetch(i * 2 + m // HH + 1, 1 - m // HH)
                    if not (first and m < 2):
                        keep((m - 2) % NU, u - 2)
                        act.wait_ge(rv_ready, u - 1)
                    act.wait_ge(nmx_ready, u + 1)
                    if not (first and m < 4):
                        act.wait_ge(t_done, u - 3)
                    act.activation(pm[:, m % 4, :], sm[:, us, :], ACT.Exp, bias=nmx[:, us:us + 1], scale=SCALE,
                                   accum_out=rs[:, us:us + 1]).then_inc(exp_done, 1)
            body(0, True, False)
            with act.Fori(1, NB // 2 - 1) as i:
                body(i, False, False)
            body(NB // 2 - 1, False, True)
            keep(NU - 2, NB * HH - 2)
            keep(NU - 1, NB * HH - 1)

        @block.vector
        def _(dve):
            link = Link(dve, att_steps)
            dve.wait_ge(att_in, 64)
            link(dve.tensor_copy(pages_f[0:1, :], table[:]))
            link(dve.tensor_scalar(pages_f[0:1, :], pages_f[0:1, :], 2.0, float(hh), ALU.mult, ALU.add))
            dve.tensor_copy(table[:], pages_f[0:1, :]).then_inc(table_ready, 1)
            dve.wait_ge(table_ready, 1)
            link(dve.tensor_copy(pages_f[:], pages[:]))
            link(dve.tensor_scalar(pages_f[:], pages_f[:], 2.0 * HD, float(hh * HD), ALU.mult, ALU.add))
            link(dve.tensor_scalar(pages_f[:], pages_f[:], k.c("prow"), None, ALU.add))
            link(dve.tensor_copy(pages[:], pages_f[:]))
            link(dve.tensor_copy(rows_f[:], rows[:]))
            link(dve.tensor_scalar(rows_f[:], rows_f[:], float(PS), k.c("smod"), ALU.mult, ALU.add))
            dve.tensor_copy(rows[:], rows_f[:]).then_inc(rows_ready, 1)
            link(dve.tensor_copy(len_f[:], len_i[:]))
            dve.memset(mask[:], 0.0).then_inc(mask_ready, 1)
            dve.wait_ge(mask_ready, 1)

            def fetch(b, s):
                if not isinstance(b, int) or b >= 2:
                    dve.wait_ge(qk_done, (b - 1) * HH)
                dve.tensor_copy(kqb[:, s, NPP * HH:, :], k.qkT[:, bass.ds(b, 1)].rearrange("p o h n -> p (o h) n"))\
                    .then_inc(kq_ready, 1)
            fetch(0, 0)

            def body(i, first, last):
                for m in range(NU):
                    s, h, us = m // HH, m % HH, m % 2
                    u, b = i * NU + m, i * 2 + s
                    if h == 1 and not (last and s == 1):
                        fetch(b + 1, 1 - s)
                    if h == 0:
                        if not first:
                            dve.wait_ge(max_done, (b - 1) * HH)
                        dve.tensor_scalar(mask[:, s, 0:CL], k.c("iota512"), len_f[:, bass.ds(b, 1)], NEG,
                                          ALU.is_ge, ALU.mult).then_inc(mask_ready, 1)
                        dve.wait_ge(mask_ready, b + 2)
                    dve.wait_ge(qk_done, u + 1)
                    if not (first and m < 2):
                        lone_wait(dve, exp_done, u - 1, passed)
                    dve.tensor_tensor_reduce(out=sm[:, us, 0:CA], in0=sps[:, us, 0, 0:CA], in1=mask[:, s, 0:CA], scale=1.0,
                                             scalar=-3e38, op0=ALU.add, op1=ALU.max, accum_out=mxs[:, us, 0:1]).then_inc(max_a, 1)
                    lone_wait(dve, max_a, u + 1, passed)
                    dve.tensor_tensor_reduce(out=sm[:, us, CA:KL], in0=sps[:, us, 1, 0:CB], in1=mask[:, s, CA:KL], scale=1.0,
                                             scalar=mxs[:, us, 0:1], op0=ALU.add, op1=ALU.max,
                                             accum_out=mxs[:, us, 1:2]).then_inc(max_done, 1)
                    dve.wait_ge(max_done, u + 1)
                    dve.tensor_scalar(nmx[:, us:us + 1], mxs[:, us, 1:2], -SCALE, None, ALU.mult).then_inc(nmx_ready, 1)
                    if not (first and m < 1):
                        scale((m - 1) % NU, u - 1)
                    if not (first and m < 3):
                        out(i if m >= 3 else i - 1, (m - 3) % NU, u - 3)

            def scale(m, u):
                us = m % 2
                dve.wait_ge(exp_done, u + 1)
                dve.reciprocal(rv[:, us:us + 1], rs[:, us:us + 1]).then_inc(rv_ready, 1)
                dve.wait_ge(rv_ready, u + 1)
                dve.tensor_scalar(pm[:, m % 4, :], pm[:, m % 4, :], rv[:, us:us + 1], None, ALU.mult).then_inc(p_ready, 1)

            def out(i, m, u):
                s, h, us = m // HH, m % HH, m % 2
                dve.wait_ge(pv_done, u + 1)
                dve.tensor_copy(k.qkT[:, bass.ds(i * 2 + s, 1), HH + G * h:HH + G * (h + 1), :].rearrange("p o g n -> p (o g n)"),
                                ops[:, us, 0:P]).then_inc(o_kept, 1)
            body(0, True, False)
            with dve.Fori(1, NB // 2 - 1) as i:
                body(i, False, False)
            body(NB // 2 - 1, False, True)
            scale(NU - 1, NB * HH - 1)
            for m in (NU - 3, NU - 2, NU - 1):
                out(NB // 2 - 1, m, NB * HH - NU + m)
    k.end_phase(ctx)


def output_phase(k, hh):
    nc, dram = k.nc, k.dram
    ctx = ExitStack()
    sb = lambda name, shape, dt=F32: k.sb(f"{name}{hh}", shape, dt, ctx)
    n = lambda name: k.sem(f"{name}{hh}")
    NH = HH * G
    worw = sb("worw", [P, 2, D])
    woh = sb("woh", [P, 2, D], F32R)
    wol = sb("wol", [P, 2, D], F32R)
    oh = sb("ohi", [P, 2, TOK], F32R)
    ol = sb("olo", [P, 2, TOK], F32R)
    acc = ctx.enter_context(nc.psum_tensor(f"acc{hh}", [P, TILES, 512], F32))
    wo_in = [n("wo_in_a"), n("wo_in_b")]
    wo_high, wo_low, o_high, o_low, head_done, y3_kept = (
        n(x) for x in ("wo_high", "wo_low", "o_high", "o_low", "head_done", "y3_kept"))
    wo = dram["wo"][hh]
    head_of = lambda h: k.qkT[:, :, bass.ds(h + HH, 1), :].rearrange("p b o n -> p b (o n)")

    with nc.Block() as block:
        @block.sync
        def _(sp):
            def body(i, first):
                for s in range(2):
                    h = i * 2 + s
                    if not first:
                        sp.wait_ge(wo_low, h - 1)
                    sp.dma_start(worw[:, s, :], wo[bass.ds(h, 1)].rearrange("o p n -> (o p) n")).then_inc(wo_in[s], 16)
            peeled(sp, NH // 2, body)

        @block.scalar
        def _(act):
            def body(i, first):
                for s in range(2):
                    h = i * 2 + s
                    if not first:
                        act.wait_ge(head_done, h - 1)
                    act.copy(oh[:, s, :].rearrange("p (b n) -> p b n", n=NS), head_of(h)).then_inc(o_high, 1)
            peeled(act, NH // 2, body)

        @block.vector
        def _(dve):
            def body(i, first):
                for s in range(2):
                    h = i * 2 + s
                    dve.wait_ge(o_high, h + 1)
                    dve.tensor_tensor(ol[:, s, :].rearrange("p (b n) -> p b n", n=NS), head_of(h),
                                      oh[:, s, :].bitcast(F32).rearrange("p (b n) -> p b n", n=NS), ALU.subtract).then_inc(o_low, 1)
                    dve.wait_ge(wo_in[s], i * 16 + 16)
                    if not first:
                        dve.wait_ge(head_done, h - 1)
                    dve.tensor_copy(woh[:, s, :], worw[:, s, :]).then_inc(wo_high, 1)
                    dve.wait_ge(wo_high, h + 1)
                    dve.tensor_tensor(wol[:, s, :], worw[:, s, :], woh[:, s, :].bitcast(F32), ALU.subtract).then_inc(wo_low, 1)
            peeled(dve, NH // 2, body)
            dve.wait_ge(head_done, NH)
            for t in range(TILES):
                if hh == 0:
                    dve.tensor_copy(k.y3[:, t, :], acc[:, t, :]).then_inc(y3_kept, 1)
                else:
                    dve.tensor_tensor(k.y3[:, t, :], k.y3[:, t, :], acc[:, t, :], ALU.add).then_inc(y3_kept, 1)

        @block.tensor
        def _(pe):
            def head(h, s, first, last_head):
                pe.wait_ge(o_low, h + 1)
                pe.wait_ge(wo_low, h + 1)
                for t in range(TILES):
                    cols = slice(t * P, (t + 1) * P)
                    for j, (o, w) in enumerate(((oh, woh), (oh, wol), (ol, woh))):
                        last = pe.matmul(acc[:, t, :], o[:, s, cols], w[:, s, :], start=(first and j == 0),
                                         stop=(last_head and j == 2))
                last.then_inc(head_done, 1)
            head(0, 0, True, False)
            head(1, 1, False, False)
            with pe.Fori(1, NH // 2 - 1) as i:
                for s in range(2):
                    head(i * 2 + s, s, False, False)
            head(NH - 2, 0, False, False)
            head(NH - 1, 1, False, True)
    k.end_phase(ctx)


def expert_phase(k):
    nc, dram = k.nc, k.dram
    ctx = ExitStack()
    sb = lambda name, shape, dt=F32: k.sb(name, shape, dt, ctx)
    S2 = (0, 1)
    NRK = E3 * R3
    EC = NRK // P
    wr = sb("wr", [P, KC, E3])
    a3 = sb("a3", [P, KC, NRK])
    b3 = sb("b3", [P, EC, D])
    yt = sb("yt", [P, 2, D])
    y3T = sb("y3T", [P, 2, KC, P])
    sc = sb("sc3", [P, 2, E3])
    m1 = sb("m1", [P, 2, 8])
    m2 = sb("m2", [P, 2, 8])
    r1 = sb("r1", [P, 2, E3])
    r2 = sb("r2", [P, 2, E3])
    pick = sb("pick", [P, 2, E3])
    nm = sb("nm3", [P, 2, 1])
    ex = sb("ex3", [P, 2, E3])
    gate = sb("gate", [P, 2, E3])
    sr = sb("sr3", [P, 2, 2])
    hg = sb("hg", [P, 2, NRK])
    hgT = sb("hgT", [P, 2, EC, P])
    xres = sb("xres", [P, 2, D])
    fin = sb("fin", [P, 2, D])
    pa = ctx.enter_context(nc.psum_tensor("pa3", [P, 2, 512], F32))
    psc = ctx.enter_context(nc.psum_tensor("psc3", [P, 2, 512], F32))
    pr = ctx.enter_context(nc.psum_tensor("pr3", [P, 2, 2, 512], F32))
    e_in = k.sem("e_in")
    yt_ready, y3T_done, y3T_kept, sc_done, rank_done, nm3_ready, ex3_done, hg_ready = (
        k.sem(n) for n in ("yt_ready", "y3T_done", "y3T_kept", "sc_done", "rank_done", "nm3_ready", "ex3_done", "hg_ready"))
    fin_done, fin_ready, e_steps = (k.sem(n) for n in ("fin_done", "fin_ready", "e_steps"))
    half_done = [k.sem("half_done0"), k.sem("half_done1")]
    half_kept = [k.sem("half_kept0"), k.sem("half_kept1")]
    res_in = [k.sem("res_in0"), k.sem("res_in1")]
    out_done = [k.sem("out_done0"), k.sem("out_done1")]
    x3res = dram["x3res"].rearrange("(t p) d -> t p d", p=P)
    out = dram["out"].rearrange("(t p) d -> t p d", p=P)

    passed = k.sem("passed_expert")
    with nc.Block() as block:
        @block.sync
        def _(sp):
            for dst, src in ((wr, "wr"), (a3, "a3"), (b3, "b3")):
                sp.dma_start(dst[:], dram[src]).then_inc(e_in, 16)

            def body(it, first):
                for s in S2:
                    t = it * 2 + s
                    if not first:
                        sp.wait_ge(fin_ready, t - 1)
                    sp.dma_start(xres[:, s, :], x3res[bass.ds(t, 1)].rearrange("o p d -> (o p) d")).then_inc(res_in[s], 16)
                for s in S2:
                    t = it * 2 + s
                    sp.wait_ge(fin_ready, t + 1)
                    sp.dma_start(out[bass.ds(t, 1)].rearrange("o p d -> (o p) d"), fin[:, s, :]).then_inc(out_done[s], 16)
            peeled(sp, TILES // 2, body)
            for s in S2:
                sp.wait_ge(out_done[s], 16 * TILES // 2)

        @block.gpsimd
        def _(pool):
            def body(it, first):
                for s in S2:
                    t = it * 2 + s
                    if not first:
                        pool.wait_ge(y3T_done, t - 1)
                    pool.tensor_copy(yt[:, s, :], k.y3[:].rearrange("p t d -> p (t d)")[:, bass.ds(t * D, D)]).then_inc(yt_ready, 1)
            peeled(pool, TILES // 2, body)

        @block.tensor
        def _(pe):
            def body(it, first):
                for s in S2:
                    at = it * 2 + s + 1
                    pe.wait_ge(yt_ready, at)
                    if not first:
                        pe.wait_ge(fin_ready, at - 2)
                    for c in range(KC):
                        last = pe.transpose(pa[:, s, c * P:(c + 1) * P], yt[:, s, c * P:(c + 1) * P], k.c("ident"))
                    last.then_inc(y3T_done, 1)
                if first:
                    pe.wait_ge(e_in, 48)
                for s in S2:
                    pe.wait_ge(y3T_kept, it * 2 + s + 1)
                    for c in range(KC):
                        last = pe.matmul(psc[:, s, 0:E3], y3T[:, s, c, :], wr[:, c, :], start=(c == 0), stop=(c == KC - 1))
                    last.then_inc(sc_done, 1)
                    for j in range(2):
                        for c in range(KC):
                            last = pe.matmul(pr[:, s, j, :], y3T[:, s, c, :], a3[:, c, j * 512:(j + 1) * 512],
                                             start=(c == 0), stop=(c == KC - 1))
                    last.then_inc(rank_done, 1)
                for half in range(2):
                    for s in S2:
                        at = it * 2 + s + 1
                        pe.wait_ge(hg_ready, at)
                        if half:
                            pe.wait_ge(hgT_kept, 2 * at - 2 + (1 if s == 0 else 0) - (1 if s == 1 else 0) + 0) if False else \
                                pe.wait_ge(half_kept[s], it * 2 + 1)
                        for c in range(KC):
                            last = pe.transpose(psc[:, s, c * P:(c + 1) * P], hg[:, s, (half * KC + c) * P:(half * KC + c + 1) * P],
                                                k.c("ident"))
                        last.then_inc(half_done[s], 1)
                for s in S2:
                    at = it * 2 + s + 1
                    pe.wait_ge(half_kept[s], it * 2 + 2)
                    for c in range(EC):
                        last = pe.matmul(pa[:, s, :], hgT[:, s, c, :], b3[:, c, :], start=(c == 0), stop=(c == EC - 1))
                    last.then_inc(fin_done, 1)
            peeled(pe, TILES // 2, body)

        @block.scalar
        def _(act):
            def body(it, first):
                for s in S2:
                    act.wait_ge(y3T_done, it * 2 + s + 1)
                    act.copy(y3T[:, s].rearrange("p c t -> p (c t)"), pa[:, s, :]).then_inc(y3T_kept, 1)
                for s in S2:
                    act.wait_ge(nm3_ready, it * 2 + s + 1)
                    act.activation(ex[:, s, :], sc[:, s, :], ACT.Exp, bias=nm[:, s, :]).then_inc(ex3_done, 1)
                for half in range(2):
                    for s in S2:
                        act.wait_ge(half_done[s], it * 2 + half + 1)
                        act.copy(hgT[:, s, half * KC:(half + 1) * KC].rearrange("p c t -> p (c t)"), psc[:, s, :])\
                            .then_inc(half_kept[s], 1)
            peeled(act, TILES // 2, body)

        @block.vector
        def _(dve):
            TS, TT = dve.tensor_scalar, dve.tensor_tensor
            PER = 20
            dve.wait_ge(e_in, 48)

            def body(it, first):
                link = Link(dve, e_steps, it * PER)
                for s in S2:
                    at = it * 2 + s + 1
                    dve.wait_ge(sc_done, at)
                    link(dve.tensor_copy(sc[:, s, :], psc[:, s, 0:E3]), passed)
                    link(dve.max(m1[:, s, :], sc[:, s, :]))
                    TS(nm[:, s, :], m1[:, s, 0:1], -1.0, None, ALU.mult).then_inc(nm3_ready, 1)
                    link(dve.match_replace(r1[:, s, :], m1[:, s, :], sc[:, s, :], NEG), passed)
                    link(dve.max(m2[:, s, :], r1[:, s, :]), passed)
                    link(dve.match_replace(r2[:, s, :], m2[:, s, :], r1[:, s, :], NEG))
                    link(TT(pick[:, s, :], r2[:, s, :], sc[:, s, :], ALU.not_equal))
                    dve.wait_ge(ex3_done, at)
                    link(TT(gate[:, s, :], ex[:, s, :], pick[:, s, :], ALU.mult))
                    link(dve.tensor_reduce(sr[:, s, 0:1], gate[:, s, :], AX.X, ALU.add))
                    link(dve.reciprocal(sr[:, s, 1:2], sr[:, s, 0:1]))
                    link(TS(gate[:, s, :], gate[:, s, :], sr[:, s, 1:2], 2.0, ALU.mult, ALU.mult))
                    dve.wait_ge(rank_done, at)
                    for j in range(2):
                        last = TT(hg[:, s, j * 512:(j + 1) * 512].rearrange("p (e r) -> p e r", r=R3),
                                  pr[:, s, j, :].rearrange("p (e r) -> p e r", r=R3),
                                  bc(gate[:, s, j * 32:(j + 1) * 32], 2, R3), ALU.mult)
                    last.then_inc(hg_ready, 1)
                for s in S2:
                    at = it * 2 + s + 1
                    dve.wait_ge(fin_done, at)
                    dve.wait_ge(res_in[s], it * 16 + 16)
                    if not first:
                        dve.wait_ge(out_done[s], it * 16)
                    TT(fin[:, s, :], pa[:, s, :], xres[:, s, :], ALU.add).then_inc(fin_ready, 1)
                assert link.n == PER, link.n
            peeled(dve, TILES // 2, body)
    k.end_phase(ctx)


def build(nc, dram):
    with ExitStack() as ctx:
        k = Core(nc, ctx, dram)
        kpad = dram["kpad"]
        dram["toeplitz"] = lambda h: overlapped(kpad, h)
        k.cst = k.sb("cst", [P, CONST_N])
        k.x3h = k.sb("x3h", [P, KC, TOK], F32R)
        k.x3l = k.sb("x3l", [P, KC, TOK], F32R)
        low = ExitStack()
        k.y0T = k.sb("y0T", [P, KC, TOK], F32, low)
        s4_phase(k)
        k.hx = k.sb("hx", [P, TILES * D], F32, low)
        k.z1 = k.sb("z1", [P, TILES * R1], F32, low)
        k.hs1 = k.sb("hs1", [P, TILES * E1], F32, low)
        k.ds1 = k.sb("dl1", [P, TILES * E1], F32, low)
        mix_phase(k)
        route_phase(k)
        low.close()
        k.qkT = k.sb("qkT", [P, NB, HH + HH * G, NS])
        for hh in range(2):
            project_phase(k, hh)
            attend_phase(k, hh)
            if hh == 0:
                k.y3 = k.sb("y3", [P, TILES, D])
            output_phase(k, hh)
        expert_phase(k)
    return nc


def overlapped(kpad, h):
    return bass.AP(kpad.tensor, h * KPAD + 1, [[1, P], [KPAD, 2], [1, D]])


def layouts(i):
    a = np.ascontiguousarray
    rep = lambda v: np.broadcast_to(v, (P,) + v.shape)
    f = {n: np.asarray(v) for n, v in i.items()}
    d = {"cst": constants()}
    dup = lambda v: np.concatenate([v.T, v.T], 0)
    d["s4in"] = a(np.stack([rep(f["L0_cond_log_dt"]), dup(f["L0_cond_log_A_real"]), dup(f["L0_cond_A_imag"]),
                            dup(f["L0_cond_C"][:, :, 0]), dup(f["L0_cond_C"][:, :, 1])], 1))
    d["L0_cond_D"] = f["L0_cond_D"]
    d["len_b"] = a(rep(f["itok_B_78_3631"]))
    x = f["x"]
    d["x_rev"] = a(x.reshape(NB, NS, KC, P)[..., ::-1].transpose(3, 2, 1, 0))
    chunks = lambda m: a(m.reshape(-1, P, m.shape[1]).transpose(1, 0, 2))
    d["xtok"] = chunks(x.reshape(TOK, D))
    d["wup"] = chunks(f["L0_ffn_W_up"].T)
    d["gzw"] = chunks(np.concatenate([f["L0_ffn_gate_w"].T, f["L0_ffn_lora_A"].reshape(E0 * R0, D).T], 1))
    d["bias0"] = a(rep(f["L0_ffn_expert_bias"]))
    d["lb0"] = a(f["L0_ffn_lora_B"].transpose(0, 2, 1).reshape(E0 * R0, D))
    d["cond_b"] = a(np.repeat(f["itok_B_0_15"], NS).reshape(TILES, P).T)
    d["l1w"] = a(f["L1_cond_weights"].reshape(-1, NS))
    d["w1t"] = chunks(f["L1_ffn_W"].T)
    d["a1w"] = chunks(f["L1_ffn_A"])
    d["a1h"] = chunks(np.concatenate([f["L1_ffn_W"].T[:, :E1], f["L1_ffn_A"]], 1))
    d["b1"] = a(rep(f["L1_ffn_b"]))
    d["lime"] = a(rep(f["L1_ffn_LiMEs"]))
    d["lime_re"] = a(rep(f["L1_ffn_LiMEs"].T))
    d["bmat"] = f["L1_ffn_Bmat"]
    d["ids_b"] = a(rep(np.repeat(f["itok_B_3_7"], NS)))
    d["b2t"] = chunks(f["L2_cond_B"].reshape(AD2 * RC2, D).T)
    d["a2"] = a(f["L2_cond_A"].transpose(0, 2, 1).reshape(AD2 * RC2, D))
    d["rw2"] = chunks(np.concatenate([f["L2_ffn_W_router"].T, f["L2_ffn_lora_A"].reshape(E2 * R2, D).T], 1))
    d["w2t"] = chunks(f["L2_ffn_W_base"].T)
    d["lb2"] = a(f["L2_ffn_lora_B"].transpose(0, 2, 1).reshape(E2 * R2, D))
    d["bb2"] = a(rep(f["L2_ffn_b_base"]))
    d["start_b"] = a(np.repeat(f["itok_B_207_1644"], NS).reshape(TILES, P).T)
    swap = lambda v: np.concatenate([v[HD // 2:], v[:HD // 2]])
    qw, kw = f["L3_cond_q_norm_w"], f["L3_cond_k_norm_w"]
    d["norm_w"] = a(rep(np.stack([qw, swap(qw), kw, swap(kw)])))
    halves = lambda w: w.T.reshape(KC, P, 2, -1, HH * HD).transpose(2, 3, 1, 0, 4)
    d["wqkv"] = a(np.concatenate([halves(f["L3_cond_Wv"]), halves(f["L3_cond_Wk"]), halves(f["L3_cond_Wq"])], 1))
    d["table"] = a(f["itok_Bx16_0_63"].reshape(1, -1))
    d["table_b"] = a(np.repeat(f["itok_Bx16_0_63"].reshape(NB * CL // P, P // PS).T, PS, 0))
    d["table_rep"] = a(rep(f["itok_Bx16_0_63"].reshape(-1)))
    d["start_rep"] = a(rep(f["itok_B_207_1644"]))
    kc, vc = f["L3_cond_k_cache"], f["L3_cond_v_cache"]
    d["kpages"] = a(kc.reshape(PAGES, PS, 2, HH, HD).transpose(0, 2, 4, 3, 1).reshape(PAGES * 2, HD, HH * PS))
    for hh in range(2):
        d[f"vrows{hh}"] = a(vc.reshape(PAGES * PS, 2, HH * HD)[:, hh])
    d["wo"] = a(f["L3_cond_Wo"].T.reshape(2, HH * G, HD, D))
    d["wr"] = chunks(f["L3_ffn_Wr"].T)
    d["a3"] = chunks(f["L3_ffn_A"].reshape(E3 * R3, D).T)
    d["b3"] = chunks(f["L3_ffn_B"].transpose(0, 2, 1).reshape(E3 * R3, D))
    return d


SCRATCH = {"kpad": (NS, KPAD), "x3res": (TOK, D), "ropetab": (P, 4 * TILES * HD), "vnew": (2, TOK, HH * HD)}


def kernel(**inputs):
    import concourse.bacc as bacc
    from concourse.bass_utils import run_bass_kernel_spmd

    arrays = layouts(inputs)
    nc = bacc.Bacc("TRN2", target_bir_lowering=False, num_devices=1)
    dram = {n: nc.dram_tensor(f"in_{n}", v.shape, mybir.dt.from_np(v.dtype), kind="ExternalInput").ap()
            for n, v in arrays.items()}
    for n, shape in SCRATCH.items():
        dram[n] = nc.dram_tensor(f"scratch_{n}", shape, F32, kind="Internal").ap()
    dram["out"] = nc.dram_tensor("out", (TOK, D), F32, kind="ExternalOutput").ap()
    build(nc, dram)
    r = run_bass_kernel_spmd(nc, [{f"in_{n}": v for n, v in arrays.items()}], core_ids=[0])
    return r.results[0]["out"].reshape(NB, NS, D)
```

```python
import math
from contextlib import ExitStack

import numpy as np
import concourse.bass as bass
from concourse import mybir

F32 = mybir.dt.float32
F32R = mybir.dt.float32r
I32 = mybir.dt.int32
U32 = mybir.dt.uint32
ALU = mybir.AluOpType
ACT = mybir.ActivationFunctionType
AX = mybir.AxisListType

P = 128
NB, NS, D = 32, 32, 512
TOK = NB * NS
TILES = TOK // P
KC = D // P
BPT = P // NS

MODES = 64
A_STEP, A_N, B_N = 32, 16, 32
KPAD = 640
E0, R0 = 4, 8
E1, R1 = 8, 32
AD2, RC2 = 8, 16
E2, R2 = 8, 16
HD, HQ, HK = 128, 32, 8
G = HQ // HK
PAGES, PS, NPP = 64, 32, 16
CL = NPP * PS
KL = CL + NS
E3, TOP3, R3 = 64, 16, 16
SCALE = 1.0 / math.sqrt(HD)
NEG = -1e30

MAGIC = 12582912.0
TWO_PI_1 = 6.28125
TWO_PI_2 = float(np.uint32(np.float32(2 * math.pi - 6.28125).view(np.uint32) & np.uint32(0xFFFFF000)).view(np.float32))
TWO_PI_3 = 2 * math.pi - TWO_PI_1 - TWO_PI_2
INV_2PI = 1.0 / (2 * math.pi)
PI_IN = float(np.nextafter(np.float32(math.pi), np.float32(0)))

CONST_PARTS = [("ident", P), ("iota8", 8), ("block4", BPT), ("cmod", 1), ("bvals", B_N), ("avals", A_N),
               ("phase", 1), ("phase2", 1), ("halfpi", 1), ("sign", 1), ("lpos", KC), ("adapter", 1), ("smod", 1),
               ("invf", HD // 2), ("sinsign", HD), ("iota512", CL), ("experts", E3), ("eps", 1), ("prow", 1)]
CONST_AT, _n = {}, 0
for _name, _len in CONST_PARTS:
    CONST_AT[_name] = (_n, _n + _len)
    _n += _len
CONST_N = _n


def constants():
    p = np.arange(P, dtype=np.float32)
    c = np.zeros((P, CONST_N), np.float32)

    def put(name, value):
        a, b = CONST_AT[name]
        c[:, a:b] = value

    put("ident", np.eye(P))
    put("iota8", np.arange(8)[None])
    put("block4", (p[:, None] // NS == np.arange(BPT)[None]))
    put("cmod", (p % NS)[:, None])
    put("bvals", np.arange(B_N)[None])
    put("avals", (A_STEP * np.arange(A_N))[None])
    put("phase", np.where(p < MODES, np.float32(math.pi / 2), 0)[:, None])
    put("phase2", np.where(p < MODES, np.float32(math.pi), np.float32(math.pi / 2))[:, None])
    put("halfpi", np.float32(math.pi / 2))
    put("sign", np.where(p < MODES, 1, -1)[:, None])
    put("lpos", p[:, None] + P * np.arange(KC)[None])
    put("adapter", (p // RC2)[:, None])
    put("smod", (p % NS)[:, None])
    put("invf", (np.float32(1) / np.float32(10000.0) ** (np.arange(0, HD, 2, dtype=np.float32) / np.float32(HD)))[None])
    put("sinsign", np.where(np.arange(HD) < HD // 2, -1, 1)[None])
    put("iota512", np.arange(CL)[None])
    put("eps", 1e-6)
    put("prow", p[:, None])
    put("experts", np.arange(E3)[None])
    return c


class Link:

    def __init__(self, eng, sem, base=0):
        self.eng, self.sem, self.base, self.n = eng, sem, base, 0

    def __call__(self, ins, passed=None):
        self.n += 1
        ins.then_inc(self.sem, 1)
        if passed:
            lone_wait(self.eng, self.sem, self.base + self.n, passed)
        else:
            self.eng.wait_ge(self.sem, self.base + self.n)


def lone_wait(eng, sem, value, passed):
    eng.wait_ge(sem, value)
    eng.sem_inc(passed, 1)


def bc(ap, axis, n):
    shape = list(ap.shape)
    shape.insert(axis, n)
    return ap.unsqueeze(axis).broadcast_to(shape)


def reduce_angles(link, dve, theta, turns, phases, spare=None):
    for (a, b), ph, in_turns in phases:
        if ph is None:
            link(dve.tensor_scalar(turns[:, a:b], theta[:, a:b], INV_2PI, None, ALU.mult))
        else:
            link(dve.tensor_scalar(turns[:, a:b], theta[:, a:b], ph, INV_2PI, ALU.add, ALU.mult))
    link(dve.tensor_scalar(turns, turns, MAGIC, None, ALU.add))
    link(dve.tensor_scalar(turns, turns, MAGIC, None, ALU.subtract))
    for part in (TWO_PI_1, TWO_PI_2, TWO_PI_3):
        if spare is None:
            link(dve.scalar_tensor_tensor(out=theta, in0=turns, scalar=-part, in1=theta, op0=ALU.mult, op1=ALU.add))
        else:
            link(dve.tensor_scalar(spare, turns, part, None, ALU.mult))
            link(dve.tensor_tensor(theta, theta, spare, ALU.subtract))
    for (a, b), ph, _ in phases:
        if ph is not None:
            link(dve.tensor_scalar(theta[:, a:b], theta[:, a:b], ph, None, ALU.add))
    link(dve.tensor_scalar(theta, theta, PI_IN, -PI_IN, ALU.min, ALU.max))


class Core:

    def __init__(self, nc, ctx, dram):
        self.nc, self.ctx, self.dram = nc, ctx, dram
        self.sems = []

    def sb(self, name, shape, dt=F32, ctx=None):
        return (ctx or self.ctx).enter_context(self.nc.sbuf_tensor(name, shape, dt))

    def sem(self, name):
        self.sems.append(self.nc.alloc_semaphore(name=name))
        return self.sems[-1]

    def end_phase(self, ctx):
        ctx.close()
        self.nc.clear_and_free_semaphores(self.sems)
        self.nc.all_engine_barrier()
        self.sems = []

    def c(self, name):
        a, b = CONST_AT[name]
        return self.cst[:, a:b]


PG = 6
VC = CL // P


class Rotary:
    HALF = HD // 2
    NA = TILES * HALF

    def __init__(self, k, sb):
        self.k = k
        self.start_i = sb("start_i", [P, TILES], I32)
        self.pos = sb("pos", [P, TILES])
        self.len_i = sb("klen_i", [P, NB], I32)
        self.nw = sb("nw", [P, 4, HD])
        self.ang = sb("ang", [P, 2 * self.NA])
        self.turns = sb("turns3", [P, 2 * self.NA])
        self.tab = sb("tab", [P, 4, TILES, HD])
        self.rows_in = k.sem("rows_in")
        self.rope_in, self.ang_ready, self.trig3_done, self.tab_out, self.rope_steps = (
            k.sem(n) for n in ("rope_in", "ang_ready", "trig3_done", "tab_out", "rope_steps"))

    def load(self, sp):
        sp.dma_start(self.start_i[:], self.k.dram["start_b"]).then_inc(self.rope_in, 16)
        for dst, src in ((self.nw, "norm_w"), (self.k.table, "table"), (self.k.kpage, "pages_b"), (self.k.vrow, "table_b"),
                         (self.len_i, "start_rep"), (self.k.cond, "cond_b")):
            sp.dma_start(dst[:], self.k.dram[src]).then_inc(self.rope_in, 16)

    def tables(self, pool, const_in):
        k, HALF, NA, ang, turns, tab = self.k, self.HALF, self.NA, self.ang, self.turns, self.tab
        link = Link(pool, self.rope_steps)
        pool.wait_ge(const_in, 16)
        pool.wait_ge(self.rope_in, 112)
        cond = ang[:, 0:TILES]
        link(pool.tensor_copy(cond, k.cond[:]))
        link(pool.tensor_scalar(cond, cond, float(NS), k.c("cmod"), ALU.mult, ALU.add))
        link(pool.tensor_copy(k.cond[:], cond))
        for t in range(TILES):
            pool.indirect_dma_start(k.wg[:, t, :], None, k.dram["l1w"],
                                    bass.IndirectOffsetOnAxis(k.cond[:, t:t + 1], 0)).then_inc(self.rows_in, 16)
        link(pool.tensor_copy(self.pos[:], self.start_i[:]))
        link(pool.tensor_scalar(self.pos[:], self.pos[:], k.c("smod"), None, ALU.add))
        for j in range(2):
            link(pool.tensor_tensor(ang[:, j * NA:(j + 1) * NA].rearrange("p (t f) -> p t f", f=HALF),
                                    bc(self.pos[:], 2, HALF), bc(k.c("invf"), 1, TILES), ALU.mult))
        reduce_angles(link, pool, ang[:], turns[:], [((0, NA), k.c("halfpi"), 0), ((NA, 2 * NA), None, 0)],
                      tab[:, 0].rearrange("p t d -> p (t d)"))
        pool.sem_inc(self.ang_ready, 1)
        pool.wait_ge(self.trig3_done, 1)
        link(pool.tensor_scalar(ang[:, NA:], turns[:, NA:], -1.0, None, ALU.mult))
        cos = turns[:, 0:NA].rearrange("p (t f) -> p t f", f=HALF)
        sin = turns[:, NA:].rearrange("p (t f) -> p t f", f=HALF)
        neg = ang[:, NA:].rearrange("p (t f) -> p t f", f=HALF)
        for j, (lo, hi) in enumerate(((cos, cos), (neg, sin), (cos, cos), (neg, sin))):
            for part, src in ((slice(0, HALF), lo), (slice(HALF, HD), hi)):
                link(pool.tensor_tensor(tab[:, j, :, part], src, bc(self.nw[:, j, part], 1, TILES), ALU.mult))
        pool.dma_start(k.dram["ropetab"], tab[:].rearrange("p j t d -> p (j t d)")).then_inc(self.tab_out, 16)

        kf, vf = ang[:, 0:NB * PG], ang[:, self.NA:self.NA + NB * VC]
        for idx, f, rows, offset in ((k.kpage, kf, HD, "prow"), (k.vrow, vf, PS, "smod")):
            link(pool.tensor_copy(f, idx[:]))
            link(pool.tensor_scalar(f, f, float(rows), k.c(offset), ALU.mult, ALU.add))
            link(pool.tensor_copy(idx[:], f))
        link(pool.tensor_copy(k.klen[:], self.len_i[:]))
        pool.wait_ge(self.tab_out, 16)
        pool.wait_ge(self.rows_in, 16 * TILES)

    def sines(self, act):
        act.wait_ge(self.ang_ready, 1)
        act.activation(self.turns[:], self.ang[:], ACT.Sin).then_inc(self.trig3_done, 1)


def s4_phase(k):
    nc, dram = k.nc, k.dram
    ctx = ExitStack()
    sb = lambda name, shape, dt=F32: k.sb(name, shape, dt, ctx)
    NY, NX = NS * B_N, NS * A_N
    NT = NY + 2 * NX + 3 * NS
    s4in = sb("s4in", [P, 5, NS])
    drow = sb("drow", [1, NS])
    len_i = sb("len_i", [P, NB], I32)
    len_f = sb("len_f", [P, NB])
    lmask = sb("lmask", [P, KC, NB])
    xr = sb("xr", [P, KC, NS, NB])
    th = sb("th", [P, 2, NS])
    w1 = sb("w1", [P, 2, NS])
    w2 = sb("w2", [P, 2, NS])
    dm = sb("dm", [P, 2, NS])
    dta = sb("dta", [P, 2, NS])
    sm = sb("sm", [P, 12, NS])
    theta = sb("theta", [P, NT])
    turns = sb("turns", [P, NT])
    trig = sb("trig", [P, NT])
    mag = sb("mag", [P, NY + NX])
    ey = sb("ey", [P, NS, B_N])
    ex1 = sb("ex1", [P, NS, A_N])
    ex2 = sb("ex2", [P, NS, A_N])
    xx = sb("xx", [P, NS, A_N])
    ksb = sb("ksb", [A_N, NS * B_N])
    zeros = sb("zeros", [NS, P])
    RING = 8
    BANKS = RING // 2
    toep = sb("toep", [P, RING, D])
    kps = ctx.enter_context(nc.psum_tensor("kps", [A_N, 2, 512], F32))
    yps = ctx.enter_context(nc.psum_tensor("yps", [P, BANKS, 512], F32))
    const_in, s4_in, u_in, zero_made, kpad_out = (k.sem(n) for n in ("const_in", "s4_in", "u_in", "zero_made", "kpad_out"))
    s4_steps, tanh_done, half_ready, angle_ready, trig_done, expo_ready, mag_done = (
        k.sem(n) for n in ("s4_steps", "tanh_done", "half_ready", "angle_ready", "trig_done", "expo_ready", "mag_done"))
    xy_ready, kern_done, kern_kept = (k.sem(n) for n in ("xy_ready", "kern_done", "kern_kept"))
    toep_in = [k.sem(f"toep_in{s}") for s in range(RING // 2)]
    conv_done, conv_kept, early_in = k.sem("conv_done"), k.sem("conv_kept"), k.sem("early_in")

    rotary = Rotary(k, sb)

    kpad = dram["kpad"]
    kpad_dst = kpad[:, P:].rearrange("h (a b) -> a h b", b=B_N)

    with nc.Block() as block:
        @block.sync
        def _(sp):
            sp.dma_start(s4in[:], dram["s4in"]).then_inc(s4_in, 16)
            sp.dma_start(k.cst[:], dram["cst"]).then_inc(const_in, 16)
            sp.dma_start(drow[:], dram["L0_cond_D"].unsqueeze(0)).then_inc(s4_in, 16)
            sp.dma_start(len_i[:], dram["len_b"]).then_inc(s4_in, 16)
            rotary.load(sp)
            sp.dma_start(xr[:], dram["x_rev"]).then_inc(u_in, 16)
            for src, dst in k.early.items():
                sp.dma_start(dst[:], dram[src]).then_inc(early_in, 16)
            sp.wait_ge(zero_made, 1)
            sp.dma_start(kpad[:, 0:P], zeros[:]).then_inc(kpad_out, 16)
            sp.wait_ge(kern_kept, 1)
            sp.dma_start(kpad_dst, ksb[:].rearrange("a (h b) -> a h b", b=B_N)).then_inc(kpad_out, 16)
            sp.wait_ge(kpad_out, 32)
            for s in range(0, RING, 2):
                sp.dma_start(toep[:, s:s + 2, :], dram["toeplitz"](s)).then_inc(toep_in[s // 2], 16)
            with sp.Fori(1, NS // RING) as i:
                for s in range(0, RING, 2):
                    sp.wait_ge(conv_done, i * RING + s - RING + 2)
                    sp.dma_start(toep[:, s:s + 2, :], dram["toeplitz"](i * RING + s)).then_inc(toep_in[s // 2], 16)
            sp.wait_ge(early_in, 16 * len(k.early))

        @block.scalar
        def _(act):
            act.wait_ge(s4_in, 48)
            act.activation(th[:], s4in[:, 0:2, :], ACT.Tanh, scale=1.0 / 16).then_inc(tanh_done, 1)
            act.wait_ge(half_ready, 1)
            act.activation(sm[:, 0, :], dta[:, 0, :], ACT.Tanh, scale=0.5).then_inc(tanh_done, 1)
            act.wait_ge(expo_ready, 1)
            act.activation(mag[:], mag[:], ACT.Exp).then_inc(mag_done, 1)
            act.wait_ge(angle_ready, 1)
            act.activation(trig[:], theta[:], ACT.Sin).then_inc(trig_done, 1)
            rotary.sines(act)

        @block.gpsimd
        def _(pool):
            rotary.tables(pool, const_in)

        @block.vector
        def _(dve):
            link = Link(dve, s4_steps)
            TS, TT, STT = dve.tensor_scalar, dve.tensor_tensor, dve.scalar_tensor_tensor
            TT_ = lambda out, a, b, op: link(TT(out, a, b, op))
            dve.memset(zeros[:], 0.0).then_inc(zero_made, 1)
            dve.wait_ge(tanh_done, 1)
            link(TS(w1[:], th[:], -1.0, 1.0, ALU.mult, ALU.add))
            link(dve.reciprocal(w2[:], w1[:]))
            link(STT(out=w1[:], in0=th[:], scalar=1.0, in1=w2[:], op0=ALU.add, op1=ALU.mult))
            TT_(w2[:], w1[:], w1[:], ALU.mult)
            TT_(w1[:], w2[:], w2[:], ALU.mult)
            TT_(dm[:], w1[:], w1[:], ALU.mult)
            dt, mre, im = dm[:, 0, :], dm[:, 1, :], s4in[:, 2, :]
            cr, ci = s4in[:, 3, :], s4in[:, 4, :]
            link(STT(out=dta[:, 0, :], in0=mre, scalar=-1.0, in1=dt, op0=ALU.mult, op1=ALU.mult))
            TT(dta[:, 1, :], im, dt, ALU.mult).then_inc(half_ready, 1)
            dve.wait_ge(const_in, 16)
            dve.wait_ge(half_ready, 1)
            magy = mag[:, 0:NY].rearrange("p (h b) -> p h b", b=B_N)
            magx = mag[:, NY:].rearrange("p (h a) -> p h a", a=A_N)
            bv, av = bc(k.c("bvals"), 1, NS), bc(k.c("avals"), 1, NS)
            link(TT(magy, bc(dta[:, 0, :], 2, B_N), bv, ALU.mult))
            TT(magx, bc(dta[:, 0, :], 2, A_N), av, ALU.mult).then_inc(expo_ready, 1)
            thy = theta[:, 0:NY].rearrange("p (h b) -> p h b", b=B_N)
            thx = [theta[:, NY + j * NX:NY + (j + 1) * NX].rearrange("p (h a) -> p h a", a=A_N) for j in range(2)]
            last = NY + 2 * NX
            link(TT(thy, bc(dta[:, 1, :], 2, B_N), bv, ALU.mult))
            for j in range(2):
                link(TT(thx[j], bc(dta[:, 1, :], 2, A_N), av, ALU.mult))
            link(dve.tensor_copy(theta[:, last:last + 2 * NS].rearrange("p (j h) -> p j h", j=2), bc(dta[:, 1, :], 1, 2)))
            link(TS(theta[:, last + 2 * NS:], dta[:, 1, :], 0.5, None, ALU.mult))
            reduce_angles(link, dve, theta[:], turns[:], [
                ((0, NY + NX), k.c("phase"), 0), ((NY + NX, last), k.c("phase2"), 0),
                ((last, last + NS), k.c("halfpi"), 0), ((last + NS, NT), None, 0)])
            dve.sem_inc(angle_ready, 1)
            dve.wait_ge(tanh_done, 2)
            S = lambda j: sm[:, j, :]
            link(TS(S(1), S(0), -1.0, 1.0, ALU.mult, ALU.add))
            link(dve.reciprocal(S(2), S(1)))
            link(STT(out=S(3), in0=S(0), scalar=2.0, in1=S(2), op0=ALU.mult, op1=ALU.mult))
            dve.wait_ge(trig_done, 1)
            cosb, sinb, sinh = (trig[:, last + j * NS:last + (j + 1) * NS] for j in range(3))
            link(STT(out=S(4), in0=sinh, scalar=-2.0, in1=sinh, op0=ALU.mult, op1=ALU.mult))
            TT_(S(5), S(3), cosb, ALU.mult)
            TT_(S(4), S(4), S(5), ALU.add)
            link(STT(out=S(5), in0=S(3), scalar=1.0, in1=sinb, op0=ALU.add, op1=ALU.mult))
            TT_(S(6), cr, S(4), ALU.mult)
            TT_(S(7), ci, S(5), ALU.mult)
            TT_(S(6), S(6), S(7), ALU.subtract)
            TT_(S(7), cr, S(5), ALU.mult)
            TT_(S(8), ci, S(4), ALU.mult)
            TT_(S(7), S(7), S(8), ALU.add)
            TT_(S(8), mre, mre, ALU.mult)
            TT_(S(9), im, im, ALU.mult)
            TT_(S(8), S(8), S(9), ALU.add)
            link(dve.reciprocal(S(9), S(8)))
            TT_(S(8), S(6), mre, ALU.mult)
            TT_(S(10), S(7), im, ALU.mult)
            TT_(S(8), S(10), S(8), ALU.subtract)
            TT_(S(10), S(7), mre, ALU.mult)
            TT_(S(11), S(6), im, ALU.mult)
            TT_(S(10), S(10), S(11), ALU.add)
            TT_(S(0), S(8), S(9), ALU.mult)
            link(STT(out=S(1), in0=S(10), scalar=-1.0, in1=S(9), op0=ALU.mult, op1=ALU.mult))
            dve.wait_ge(mag_done, 1)
            trigx = [trig[:, NY + j * NX:NY + (j + 1) * NX].rearrange("p (h a) -> p h a", a=A_N) for j in range(2)]
            link(STT(out=ey[:].rearrange("p h b -> p (h b)"), in0=trig[:, 0:NY], scalar=k.c("sign"),
                     in1=mag[:, 0:NY], op0=ALU.mult, op1=ALU.mult))
            TT_(ex1[:], trigx[0], magx, ALU.mult)
            TT_(ex2[:], trigx[1], magx, ALU.mult)
            TT_(ex1[:], ex1[:], bc(S(0), 2, A_N), ALU.mult)
            TT_(ex2[:], ex2[:], bc(S(1), 2, A_N), ALU.mult)
            TT(xx[:], ex1[:], ex2[:], ALU.add).then_inc(xy_ready, 1)
            link(dve.tensor_copy(len_f[:], len_i[:]))
            for c in range(KC):
                link(TS(lmask[:, c, :], len_f[:], k.c("lpos")[:, c:c + 1], None, ALU.is_gt))
            dve.wait_ge(kern_done, 1)
            link(TS(ksb[:].rearrange("a (j n) -> a j n", j=2), kps[:], 2.0, None, ALU.mult))
            tap = ksb[0:1, :].rearrange("a (h b) -> a h b", b=B_N)[:, :, 0]
            TT(tap, tap, drow[:], ALU.add).then_inc(kern_kept, 1)
            dve.wait_ge(early_in, 16 * len(k.early))
            for name in ("wup", "gzw"):
                link(dve.tensor_copy(k.high[name][:], k.early[name][:]))
                link(TT(k.low[name][:], k.early[name][:], k.high[name][:].bitcast(F32), ALU.subtract))
            with dve.Fori(0, NS // BANKS) as i:
                for s in range(BANKS):
                    dve.wait_ge(conv_done, i * BANKS + s + 1)
                    out = k.y0T[:].rearrange("p c (b h) -> p c b h", h=NS)[:, :, :, bass.ds(i * BANKS + s, 1)]
                    TT(out.rearrange("p c b o -> p c (b o)"), yps[:, s, 0:KC * NB].rearrange("p (c b) -> p c b", b=NB),
                       lmask[:], ALU.mult).then_inc(conv_kept, 1)

        @block.tensor
        def _(pe):
            pe.wait_ge(xy_ready, 1)
            for h in range(NS):
                last = pe.matmul(kps[:, h // 16, (h % 16) * B_N:(h % 16 + 1) * B_N], xx[:, h, :], ey[:, h, :],
                                 start=True, stop=True)
            last.then_inc(kern_done, 1)
            pe.wait_ge(u_in, 16)

            def head(i, s):
                if s % 2 == 0:
                    pe.wait_ge(toep_in[s // 2], i * 16 + 16)
                for d in range(KC):
                    last = pe.matmul(yps[:, s % BANKS, d * NB:KC * NB].rearrange("p (c b) -> p c b", b=NB),
                                     toep[:, s, d * P:(d + 1) * P],
                                     xr[:, 0:KC - d, bass.ds(i * RING + s, 1), :].rearrange("p c o b -> p c (o b)"),
                                     start=(d == 0), stop=(d == KC - 1))
                last.then_inc(conv_done, 1)

            for s in range(RING):
                if s >= BANKS:
                    pe.wait_ge(conv_kept, s - BANKS + 1)
                head(0, s)
            with pe.Fori(1, NS // RING) as i:
                for s in range(RING):
                    pe.wait_ge(conv_kept, i * RING + s - BANKS + 1)
                    head(i, s)
    k.end_phase(ctx)


def peeled(eng, n, body):
    body(0, True)
    with eng.Fori(1, n) as i:
        body(i, False)


def mix_phase(k):
    nc, dram = k.nc, k.dram
    ctx = ExitStack()
    sb = lambda name, shape, dt=F32: k.sb(name, shape, dt, ctx)
    S2 = (0, 1)
    NGZ, NH1 = E0 + E0 * R0, E1 + R1
    xtok = sb("xtok", [P, TILES, D])
    lb0, bias0 = k.early["lb0"], k.early["bias0"]
    (wuph, gzh), (wupl, gzl) = ((x["wup"], x["gzw"]) for x in (k.high, k.low))
    w1t = sb("w1t", [P, KC, D])
    w1h = sb("w1h", [P, KC, D], F32R)
    w1l = sb("w1l", [P, KC, D], F32R)
    a1h = sb("a1h", [P, KC, NH1])
    a1w = sb("a1w", [P, KC, R1])
    b1 = sb("b1", [P, D])
    lime = sb("lime", [P, E1, R1])
    bd = sb("bd", [P, TILES, BPT, NS])
    ysh = sb("ysh", [P, 2, KC, P], F32R)
    ysl = sb("ysl", [P, 2, KC, P], F32R)
    lg = sb("lg", [P, 2, 8])
    mx = sb("mx", [P, 2, 8])
    ix = sb("ix", [P, 2, 8], U32)
    ixf = sb("ixf", [P, 2, 1])
    oh = sb("oh", [P, 2, E0])
    zm = sb("zm", [P, 2, E0 * R0])
    zmT = sb("zmT", [E0 * R0, 2, P])
    x1 = sb("x1", [P, 2, D])
    x1b = sb("x1b", [P, 2, D])
    y1T = sb("y1T", [P, 2, KC, P])
    y1h = sb("y1h", [P, 2, KC, P], F32R)
    y1l = sb("y1l", [P, 2, KC, P], F32R)
    y1d = sb("y1d", [P, 2, KC, P])
    ds1 = sb("ds1", [P, 2, E1, R1])
    pb = ctx.enter_context(nc.psum_tensor("pb", [P, 2, 512], F32))
    ps = ctx.enter_context(nc.psum_tensor("ps", [P, 2, 512], F32))
    pt = ctx.enter_context(nc.psum_tensor("pt", [P, 2, 512], F32))
    ph = ctx.enter_context(nc.psum_tensor("ph", [P, 2, 512], F32))
    w1_in, x_in = k.sem("w1_in"), k.sem("x_in")
    bd_ready, ys_ready, proj0_done, zm_ready, zmT_done, zmT_kept, base0_done = (
        k.sem(n) for n in ("bd_ready", "ys_ready", "proj0_done", "zm_ready", "zmT_done", "zmT_kept",
                           "base0_done"))
    x1_ready, y1T_done, y1T_kept, y1d_kept, x1b_ready, h_done, hx_kept, mix_steps = (
        k.sem(n) for n in ("x1_ready", "y1T_done", "y1T_kept", "y1d_kept", "x1b_ready", "h_done", "hx_kept",
                           "mix_steps"))

    ysh_ready, w1h_ready, w1l_ready, y1h_kept, y1l_kept = (
        k.sem(n) for n in ("ysh_ready", "w1h_ready", "w1l_ready", "y1h_kept", "y1l_kept"))
    passed = k.sem("passed_mix")
    with nc.Block() as block:
        @block.sync
        def _(sp):
            sp.dma_start(xtok[:], dram["xtok"]).then_inc(x_in, 16)
            for dst, src in ((w1t, "w1t"), (a1h, "a1h"), (a1w, "a1w"), (b1, "b1"), (lime, "lime")):
                sp.dma_start(dst[:], dram[src]).then_inc(w1_in, 16)

        @block.gpsimd
        def _(pool):
            pool.wait_ge(ys_ready, 2)
            for c in range(KC):
                pool.wait_ge(w1h_ready, c + 1)
                pool.tensor_tensor(w1l[:, c, :], w1t[:, c, :], w1h[:, c, :].bitcast(F32), ALU.subtract).then_inc(w1l_ready, 1)

            def body(it, first):
                if not first:
                    for s in S2:
                        at = it * 2 + s + 1
                        tile = k.y0T[:, :, bass.ds((it * 2 + s) * P, P)]
                        pool.wait_ge(proj0_done, at - 2)
                        pool.tensor_copy(ysh[:, s], tile).then_inc(ysh_ready, 1)
                        lone_wait(pool, ysh_ready, at, passed)
                        pool.tensor_tensor(ysl[:, s], tile, ysh[:, s].bitcast(F32), ALU.subtract).then_inc(ys_ready, 1)
                for s in S2:
                    at = it * 2 + s + 1
                    pool.wait_ge(x1_ready, at)
                    if first:
                        pool.wait_ge(w1_in, 80)
                    else:
                        pool.wait_ge(hx_kept, at - 2)
                    pool.tensor_tensor(x1b[:, s], x1[:, s], b1[:], ALU.add).then_inc(x1b_ready, 1)
            peeled(pool, TILES // 2, body)

        @block.tensor
        def _(pe):
            def body(it, first):
                for s in S2:
                    at = it * 2 + s + 1
                    pe.wait_ge(ys_ready, at)
                    if not first:
                        pe.wait_ge(hx_kept, at - 2)
                    for c in range(KC):
                        for n, (y, w) in enumerate(((ysh, gzh), (ysh, gzl), (ysl, gzh))):
                            pe.matmul(ps[:, s, 0:NGZ], y[:, s, c, :], w[:, c, :], start=(c == 0 and n == 0),
                                      stop=(c == KC - 1 and n == 2))
                    for c in range(KC):
                        for n, (y, w) in enumerate(((ysh, wuph), (ysh, wupl), (ysl, wuph))):
                            last = pe.matmul(pb[:, s, :], y[:, s, c, :], w[:, c, :], start=(c == 0 and n == 0), stop=False)
                    last.then_inc(proj0_done, 1)
                for s in S2:
                    pe.wait_ge(zm_ready, it * 2 + s + 1)
                    pe.transpose(ps[0:E0 * R0, s, 64:64 + P], zm[:, s, :], k.c("ident")).then_inc(zmT_done, 1)
                for s in S2:
                    pe.wait_ge(zmT_kept, it * 2 + s + 1)
                    pe.matmul(pb[:, s, :], zmT[:, s, :], lb0[:], start=False, stop=True).then_inc(base0_done, 1)
                if first:
                    pe.wait_ge(bd_ready, 1)
                for s in S2:
                    pe.wait_ge(x1_ready, it * 2 + s + 1)
                    mixer = bd[:].rearrange("p t b d -> p (t b d)")[:, bass.ds((it * 2 + s) * P, P)]
                    for c in range(KC):
                        last = pe.matmul(pt[:, s, c * P:(c + 1) * P], x1[:, s, c * P:(c + 1) * P], mixer,
                                         start=True, stop=True)
                    last.then_inc(y1T_done, 1)
                if first:
                    pe.wait_ge(w1_in, 80)
                for s in S2:
                    at = it * 2 + s + 1
                    pe.wait_ge(y1d_kept, at)
                    for c in range(KC):
                        pe.matmul(ps[:, s, 192:192 + NH1], y1d[:, s, c, :], a1h[:, c, :], start=(c == 0), stop=(c == KC - 1))
                    pe.wait_ge(y1T_kept, at)
                    for c in range(KC):
                        pe.matmul(ps[:, s, 256:256 + R1], y1T[:, s, c, :], a1w[:, c, :], start=(c == 0), stop=(c == KC - 1))
                    if first and s == 0:
                        pe.wait_ge(w1l_ready, KC)
                    pe.wait_ge(y1l_kept, at)
                    for c in range(KC):
                        for n, (y, w) in enumerate(((y1h, w1h), (y1h, w1l), (y1l, w1h))):
                            last = pe.matmul(ph[:, s, :], y[:, s, c, :], w[:, c, :], start=(c == 0 and n == 0),
                                             stop=(c == KC - 1 and n == 2))
                    last.then_inc(h_done, 1)
            peeled(pe, TILES // 2, body)

        @block.scalar
        def _(act):
            for s in S2:
                act.copy(ysh[:, s], k.y0T[:, :, s * P:(s + 1) * P]).then_inc(ysh_ready, 1)
            act.wait_ge(w1_in, 80)
            for c in range(KC):
                act.copy(w1h[:, c, :], w1t[:, c, :]).then_inc(w1h_ready, 1)

            def body(it, first):
                for s in S2:
                    act.wait_ge(zmT_done, it * 2 + s + 1)
                    act.copy(zmT[:, s, :], ps[0:E0 * R0, s, 64:64 + P]).then_inc(zmT_kept, 1)
                for s in S2:
                    act.wait_ge(y1T_done, it * 2 + s + 1)
                    act.copy(y1T[:, s].rearrange("p c t -> p (c t)"), pt[:, s, :]).then_inc(y1T_kept, 1)
                    act.copy(y1h[:, s].rearrange("p c t -> p (c t)"), pt[:, s, :]).then_inc(y1h_kept, 1)
            peeled(act, TILES // 2, body)

        @block.vector
        def _(dve):
            link = Link(dve, mix_steps)
            for s in S2:
                dve.wait_ge(ysh_ready, s + 1)
                dve.tensor_tensor(ysl[:, s], k.y0T[:, :, s * P:(s + 1) * P], ysh[:, s].bitcast(F32), ALU.subtract)\
                    .then_inc(ys_ready, 1)
            link(dve.memset(lg[:], NEG))
            wide = lambda ap: ap.rearrange("p t (o d) -> p t o d", o=1).broadcast_to([P, TILES, BPT, NS])
            blk = bc(bc(k.c("block4"), 1, TILES), 3, NS)
            dve.tensor_tensor(bd[:], wide(k.wg[:]), blk, ALU.mult).then_inc(bd_ready, 1)
            PER, pre = 12, link.n

            def body(it, first):
                link = Link(dve, mix_steps, pre + it * PER)
                for s in S2:
                    dve.wait_ge(proj0_done, it * 2 + s + 1)
                    link(dve.tensor_tensor(lg[:, s, 0:E0], ps[:, s, 0:E0], bias0[:], ALU.add), passed)
                    link(dve.max(mx[:, s, :], lg[:, s, :]), passed)
                    link(dve.max_index(ix[:, s, :], mx[:, s, :], lg[:, s, :]))
                    link(dve.tensor_copy(ixf[:, s, :], ix[:, s, 0:1]))
                    link(dve.tensor_scalar(oh[:, s, :], k.c("iota8")[:, 0:E0], ixf[:, s, :], None, ALU.is_equal))
                    dve.tensor_tensor(zm[:, s, :].rearrange("p (e r) -> p e r", e=E0),
                                      ps[:, s, E0:NGZ].rearrange("p (e r) -> p e r", e=E0),
                                      bc(oh[:, s, :], 2, R0), ALU.mult).then_inc(zm_ready, 1)
                if first:
                    dve.wait_ge(x_in, 16)
                for s in S2:
                    at = it * 2 + s + 1
                    dve.wait_ge(base0_done, at)
                    if not first:
                        dve.wait_ge(x1b_ready, at - 2)
                    dve.tensor_tensor(x1[:, s, :], pb[:, s, :], xtok[:].rearrange("p t d -> p (t d)")[:, bass.ds((it * 2 + s) * D, D)],
                                      ALU.add).then_inc(x1_ready, 1)
                for s in S2:
                    dve.wait_ge(y1T_kept, it * 2 + s + 1)
                    anchors = y1T[:, s].rearrange("p c (n two) -> p (c n) two", two=2)[:, :, 1]
                    dve.tensor_copy(y1d[:, s].rearrange("p c (n two) -> p (c n) two", two=2), bc(anchors, 2, 2))\
                        .then_inc(y1d_kept, 1)
                for s in S2:
                    dve.wait_ge(y1h_kept, it * 2 + s + 1)
                    dve.tensor_tensor(y1l[:, s], y1T[:, s], y1h[:, s].bitcast(F32), ALU.subtract).then_inc(y1l_kept, 1)
                if first:
                    dve.wait_ge(w1_in, 80)
                for s in S2:
                    at = it * 2 + s + 1
                    t = it * 2 + s
                    dve.wait_ge(h_done, at)
                    row = lambda ap, n: ap[:, bass.ds(t * n, n)]
                    dve.tensor_copy(row(k.z1, R1), ps[:, s, 256:256 + R1])
                    dve.tensor_tensor(row(k.hs1, E1), ps[:, s, 192:192 + E1], b1[:, 0:E1], ALU.add)
                    link(dve.tensor_tensor(ds1[:, s], bc(ps[:, s, 192 + E1:192 + NH1], 1, E1), lime[:], ALU.mult))
                    dve.tensor_reduce(row(k.ds1, E1), ds1[:, s], AX.X, ALU.add)
                    dve.wait_ge(x1b_ready, at)
                    dve.tensor_tensor(row(k.hx, D), ph[:, s, :], x1b[:, s, :], ALU.add).then_inc(hx_kept, 1)
                assert link.n == PER
            peeled(dve, TILES // 2, body)
    k.end_phase(ctx)


def route_phase(k):
    nc, dram = k.nc, k.dram
    ctx = ExitStack()
    sb = lambda name, shape, dt=F32: k.sb(name, shape, dt, ctx)
    S2 = (0, 1)
    NRH = E2 + E2 * R2
    lime = sb("lime_re", [P, R1, E1])
    bmat = sb("bmat", [R1, D])
    b2t = sb("b2t", [P, KC, AD2 * RC2])
    a2 = sb("a2", [AD2 * RC2, D])
    ids_i = sb("ids_i", [P, TOK], I32)
    amask = sb("amask", [P, TOK])
    rw2 = sb("rw2", [P, KC, NRH])
    w2t = sb("w2t", [P, KC, D])
    w2h = sb("w2h", [P, KC, D], F32R)
    w2l = sb("w2l", [P, KC, D], F32R)
    lb2 = sb("lb2", [E2 * R2, D])
    bb2 = sb("bb2", [P, D])
    amx = sb("amx", [P, 2])
    gmx = sb("gmx", [P, 2])
    half = sb("half", [P, 2])
    lg = sb("lg1", [P, TILES, E1])
    l2 = sb("lg1b", [P, TILES, E1])
    pr = sb("pr1", [P, TILES, E1])
    sg = sb("sg1", [P, TILES, E1])
    m8 = sb("m8", [P, TILES, 8])
    st = sb("st1", [P, 2, TILES])
    mixed = sb("mixed", [P, TILES, R1, E1])
    zp = sb("zp", [P, TILES + 2, R1])
    zs = sb("zs", [P, 2, R1])
    zpT = sb("zpT", [R1, 2, P])
    x2 = sb("x2", [P, 2, D])
    x2b = sb("x2b", [P, 2, D])
    x2T = sb("x2T", [P, 2, KC, P])
    bxm = sb("bxm", [P, 2, P])
    y2T = sb("y2T", [P, 2, KC, P])
    y2h = sb("y2h", [P, 2, KC, P], F32R)
    y2l = sb("y2l", [P, 2, KC, P], F32R)
    l8 = sb("l8", [P, 2, E2])
    mx = sb("mx2", [P, 2, 8])
    ix = sb("ix2", [P, 2, 8], U32)
    ixf = sb("ixf2", [P, 2, 2])
    nm = sb("nm2", [P, 2, 1])
    ex = sb("ex_2", [P, 2, E2])
    oh = sb("oh2", [P, 2, E2])
    em = sb("em2", [P, 2, E2])
    sr = sb("sr2", [P, 2, 2])
    hw = sb("hw2", [P, 2, E2 * R2])
    hwT = sb("hwT2", [E2 * R2, 2, P])
    x3 = sb("x3", [P, 2, D])
    pb = ctx.enter_context(nc.psum_tensor("pb2", [P, 2, 512], F32))
    ps = ctx.enter_context(nc.psum_tensor("ps2", [P, 2, 512], F32))
    pt = ctx.enter_context(nc.psum_tensor("pt2", [P, 2, 512], F32))
    ph = ctx.enter_context(nc.psum_tensor("ph2", [P, 2, 512], F32))
    r_in, w2_in, amx_ready, gmx_ready, lg_ready, ex1_done, pr_ready, sg1_done, amask_ready, route_steps, tile_steps = (
        k.sem(n) for n in ("r_in", "w2_in", "amx_ready", "gmx_ready", "lg_ready", "ex1_done", "pr_ready", "sg1_done",
                           "amask_ready", "route_steps", "tile_steps"))
    zs_ready, zpT_done, zpT_kept, delta_done, x2_ready, x2T_done, x2T_kept, bx_done, bxm_ready, y2T_done, y2T_kept = (
        k.sem(n) for n in ("zs_ready", "zpT_done", "zpT_kept", "delta_done", "x2_ready", "x2T_done", "x2T_kept",
                           "bx_done", "bxm_ready", "y2T_done", "y2T_kept"))
    x2b_ready, rh_done, nm_ready, ex2_done, hw_ready, hwT_done, hwT_kept, base2_done, x3_ready, x3T_done, x3h_kept, x3l_kept = (
        k.sem(n) for n in ("x2b_ready", "rh_done", "nm_ready", "ex2_done", "hw_ready", "hwT_done", "hwT_kept",
                           "base2_done", "x3_ready", "x3T_done", "x3h_kept", "x3l_kept"))
    x3_out = [k.sem("x3_out0"), k.sem("x3_out1")]
    x3res = dram["x3res"].rearrange("(t p) d -> t p d", p=P)

    w2h_ready, w2l_ready, y2h_kept, y2l_kept = (k.sem(n) for n in ("w2h_ready", "w2l_ready", "y2h_kept", "y2l_kept"))
    passed = k.sem("passed_route")
    with nc.Block() as block:
        @block.sync
        def _(sp):
            for dst, src in ((lime, "lime_re"), (bmat, "bmat"), (ids_i, "ids_b"), (b2t, "b2t"), (a2, "a2")):
                sp.dma_start(dst[:], dram[src]).then_inc(r_in, 16)
            for dst, src in ((rw2, "rw2"), (w2t, "w2t"), (lb2, "lb2"), (bb2, "bb2")):
                sp.dma_start(dst[:], dram[src]).then_inc(w2_in, 16)

            def body(it, first):
                for s in S2:
                    sp.wait_ge(x3_ready, it * 2 + s + 1)
                    sp.dma_start(x3res[bass.ds(it * 2 + s, 1)].rearrange("o p d -> (o p) d"), x3[:, s, :])\
                        .then_inc(x3_out[s], 16)
            peeled(sp, TILES // 2, body)
            for s in S2:
                sp.wait_ge(x3_out[s], 16 * TILES // 2)

        @block.gpsimd
        def _(pool):
            pool.wait_ge(amx_ready, 1)
            pool.partition_all_reduce(gmx[:], amx[:], P, bass.bass_isa.ReduceOp.max).then_inc(gmx_ready, 1)
            pool.wait_ge(w2_in, 64)
            for c in range(KC):
                pool.wait_ge(w2h_ready, c + 1)
                pool.tensor_tensor(w2l[:, c, :], w2t[:, c, :], w2h[:, c, :].bitcast(F32), ALU.subtract).then_inc(w2l_ready, 1)

            def body(it, first):
                for s in S2:
                    at = it * 2 + s + 1
                    pool.wait_ge(x2_ready, at)
                    if not first:
                        pool.wait_ge(x3_ready, at - 2)
                    pool.tensor_tensor(x2b[:, s], x2[:, s], bb2[:], ALU.add).then_inc(x2b_ready, 1)
            peeled(pool, TILES // 2, body)

        @block.tensor
        def _(pe):
            pe.wait_ge(r_in, 80)

            def body(it, first):
                for s in S2:
                    at = it * 2 + s + 1
                    pe.wait_ge(zs_ready, at)
                    pe.transpose(ps[0:R1, s, 0:P], zs[:, s, :], k.c("ident")).then_inc(zpT_done, 1)
                for s in S2:
                    pe.wait_ge(zpT_kept, it * 2 + s + 1)
                    pe.matmul(pb[:, s, :], zpT[:, s, :], bmat[:], start=True, stop=True).then_inc(delta_done, 1)
                for s in S2:
                    at = it * 2 + s + 1
                    pe.wait_ge(x2_ready, at)
                    if not first:
                        pe.wait_ge(x3l_kept, at - 2)
                    for c in range(KC):
                        last = pe.transpose(pt[:, s, c * P:(c + 1) * P], x2[:, s, c * P:(c + 1) * P], k.c("ident"))
                    last.then_inc(x2T_done, 1)
                for s in S2:
                    pe.wait_ge(x2T_kept, it * 2 + s + 1)
                    for c in range(KC):
                        last = pe.matmul(ps[:, s, P:2 * P], b2t[:, c, :], x2T[:, s, c, :], start=(c == 0), stop=(c == KC - 1))
                    last.then_inc(bx_done, 1)
                for s in S2:
                    pe.wait_ge(bxm_ready, it * 2 + s + 1)
                    for c in range(KC):
                        last = pe.matmul(ph[:, s, c * P:(c + 1) * P], a2[:, c * P:(c + 1) * P], bxm[:, s, :],
                                         start=True, stop=True)
                    last.then_inc(y2T_done, 1)
                if first:
                    pe.wait_ge(w2_in, 64)
                for s in S2:
                    pe.wait_ge(y2T_kept, it * 2 + s + 1)
                    for c in range(KC):
                        last = pe.matmul(ps[:, s, 256:256 + NRH], y2T[:, s, c, :], rw2[:, c, :], start=(c == 0), stop=(c == KC - 1))
                    last.then_inc(rh_done, 1)
                    if first and s == 0:
                        pe.wait_ge(w2l_ready, KC)
                    pe.wait_ge(y2l_kept, it * 2 + s + 1)
                    for c in range(KC):
                        for n, (y, w) in enumerate(((y2h, w2h), (y2h, w2l), (y2l, w2h))):
                            pe.matmul(pb[:, s, :], y[:, s, c, :], w[:, c, :], start=(c == 0 and n == 0), stop=False)
                for s in S2:
                    pe.wait_ge(hw_ready, it * 2 + s + 1)
                    pe.transpose(ps[:, s, 0:P], hw[:, s, :], k.c("ident")).then_inc(hwT_done, 1)
                for s in S2:
                    pe.wait_ge(hwT_kept, it * 2 + s + 1)
                    pe.matmul(pb[:, s, :], hwT[:, s, :], lb2[:], start=False, stop=True).then_inc(base2_done, 1)
                for s in S2:
                    pe.wait_ge(x3_ready, it * 2 + s + 1)
                    for c in range(KC):
                        last = pe.transpose(pt[:, s, c * P:(c + 1) * P], x3[:, s, c * P:(c + 1) * P], k.c("ident"))
                    last.then_inc(x3T_done, 1)
            peeled(pe, TILES // 2, body)

        @block.scalar
        def _(act):
            act.wait_ge(lg_ready, 1)
            act.activation(pr[:], l2[:], ACT.Exp).then_inc(ex1_done, 1)
            act.wait_ge(pr_ready, 1)
            act.activation(sg[:], sg[:], ACT.Exp, scale=-2.0).then_inc(sg1_done, 1)

            def body(it, first):
                for s in S2:
                    act.wait_ge(zpT_done, it * 2 + s + 1)
                    act.copy(zpT[:, s, :], ps[0:R1, s, 0:P]).then_inc(zpT_kept, 1)
                if first:
                    act.wait_ge(w2_in, 64)
                    for c in range(KC):
                        act.copy(w2h[:, c, :], w2t[:, c, :]).then_inc(w2h_ready, 1)
                for s in S2:
                    act.wait_ge(x2T_done, it * 2 + s + 1)
                    act.copy(x2T[:, s].rearrange("p c t -> p (c t)"), pt[:, s, :]).then_inc(x2T_kept, 1)
                for s in S2:
                    act.wait_ge(y2T_done, it * 2 + s + 1)
                    act.copy(y2T[:, s].rearrange("p c t -> p (c t)"), ph[:, s, :]).then_inc(y2T_kept, 1)
                    act.copy(y2h[:, s].rearrange("p c t -> p (c t)"), ph[:, s, :]).then_inc(y2h_kept, 1)
                for s in S2:
                    act.wait_ge(nm_ready, it * 2 + s + 1)
                    act.activation(ex[:, s, :], l8[:, s, :], ACT.Exp, bias=nm[:, s, :]).then_inc(ex2_done, 1)
                for s in S2:
                    act.wait_ge(hwT_done, it * 2 + s + 1)
                    act.copy(hwT[:, s, :], ps[:, s, 0:P]).then_inc(hwT_kept, 1)
                for s in S2:
                    at = it * 2 + s + 1
                    act.wait_ge(x3T_done, at)
                    tile = k.x3h[:, :, bass.ds((it * 2 + s) * P, P)]
                    act.copy(tile, pt[:, s, :].rearrange("p (c t) -> p c t", c=KC)).then_inc(x3h_kept, 1)
            peeled(act, TILES // 2, body)

        @block.vector
        def _(dve):
            link = Link(dve, route_steps)
            TS, TT, STT = dve.tensor_scalar, dve.tensor_tensor, dve.scalar_tensor_tensor
            hs = k.hs1[:].rearrange("p (t e) -> p t e", e=E1)
            dl = k.ds1[:].rearrange("p (t e) -> p t e", e=E1)
            link(dve.tensor_reduce(amx[:, 0:1], k.hs1[:], AX.X, ALU.max, apply_absolute_value=True))
            dve.tensor_reduce(amx[:, 1:2], k.ds1[:], AX.X, ALU.max, apply_absolute_value=True).then_inc(amx_ready, 1)
            dve.wait_ge(gmx_ready, 1)
            link(TS(gmx[:], gmx[:], 1e-6, None, ALU.max))
            link(dve.reciprocal(half[:], gmx[:]))
            link(TS(half[:], half[:], 0.5, None, ALU.mult))
            link(TS(lg[:], hs, half[:, 0:1], None, ALU.mult))
            link(STT(out=lg[:], in0=dl, scalar=half[:, 1:2], in1=lg[:], op0=ALU.mult, op1=ALU.add))
            link(dve.tensor_reduce(st[:, 0, :], lg[:], AX.X, ALU.max))
            TT(l2[:], lg[:], bc(st[:, 0, :], 2, E1), ALU.subtract).then_inc(lg_ready, 1)
            dve.wait_ge(ex1_done, 1)
            link(dve.tensor_reduce(st[:, 1, :], pr[:], AX.X, ALU.add))
            link(dve.reciprocal(st[:, 0, :], st[:, 1, :]))
            link(TT(pr[:], pr[:], bc(st[:, 0, :], 2, E1), ALU.mult))
            for t in range(TILES - 1):
                dve.max(m8[:, t, :], pr[:, t, :])
            link(dve.max(m8[:, TILES - 1, :], pr[:, TILES - 1, :]))
            TT(sg[:], pr[:], bc(m8[:, :, 1], 2, E1), ALU.subtract).then_inc(pr_ready, 1)
            dve.wait_ge(sg1_done, 1)
            link(TS(sg[:], sg[:], 1.0, None, ALU.add))
            link(dve.reciprocal(l2[:], sg[:]))
            link(TT(pr[:], pr[:], l2[:], ALU.mult))
            link(dve.tensor_reduce(st[:, 1, :], pr[:], AX.X, ALU.add))
            link(TS(st[:, 1, :], st[:, 1, :], 1e-9, None, ALU.add))
            link(dve.reciprocal(st[:, 0, :], st[:, 1, :]))
            link(TT(pr[:], pr[:], bc(st[:, 0, :], 2, E1), ALU.mult))
            dve.wait_ge(r_in, 80)

            def ranks(a, b):
                link(TT(mixed[:, a:b], pr[:, a:b].rearrange("p t (o e) -> p t o e", o=1).broadcast_to([P, b - a, R1, E1]),
                        bc(lime[:], 1, b - a), ALU.mult))
                link(dve.tensor_reduce(zp[:, a:b], mixed[:, a:b], AX.X, ALU.add))
                link(STT(out=zp[:, a:b], in0=zp[:, a:b], scalar=0.5,
                         in1=k.z1[:].rearrange("p (t r) -> p t r", r=R1)[:, a:b], op0=ALU.mult, op1=ALU.mult))
            link(dve.memset(zp[:, TILES:], 0.0))
            ranks(0, 2)
            first_link = link

            def fetch(t, s):
                if not isinstance(t, int) or t >= 2:
                    dve.wait_ge(zpT_done, t - 1)
                dve.tensor_copy(zs[:, s, :], zp[:].rearrange("p t r -> p (t r)")[:, bass.ds(t * R1, R1)]).then_inc(zs_ready, 1)
            for s in S2:
                fetch(s, s)
            PER = 20

            def body(it, first):
                link = Link(dve, tile_steps, it * PER)
                if first:
                    first_link(dve.tensor_copy(amask[:], ids_i[:]))
                    first_link(TS(amask[:], amask[:], k.c("adapter"), None, ALU.is_equal))
                for s in S2:
                    at = it * 2 + s + 1
                    dve.wait_ge(delta_done, at)
                    TT(x2[:, s, :], pb[:, s, :], k.hx[:, bass.ds((it * 2 + s) * D, D)], ALU.add).then_inc(x2_ready, 1)
                for s in S2:
                    dve.wait_ge(bx_done, it * 2 + s + 1)
                    TT(bxm[:, s, :], ps[:, s, P:2 * P], amask[:, bass.ds((it * 2 + s) * P, P)], ALU.mult).then_inc(bxm_ready, 1)
                for s in S2:
                    dve.wait_ge(y2h_kept, it * 2 + s + 1)
                    TT(y2l[:, s], y2T[:, s], y2h[:, s].bitcast(F32), ALU.subtract).then_inc(y2l_kept, 1)
                    dve.wait_ge(w2_in, 64)
                for s in S2:
                    at = it * 2 + s + 1
                    dve.wait_ge(rh_done, at)
                    link(dve.tensor_copy(l8[:, s, :], ps[:, s, 256:256 + E2]), passed)
                    link(dve.max(mx[:, s, :], l8[:, s, :]))
                    TS(nm[:, s, :], mx[:, s, 0:1], -1.0, None, ALU.mult).then_inc(nm_ready, 1)
                    link(dve.max_index(ix[:, s, :], mx[:, s, :], l8[:, s, :]))
                    link(dve.tensor_copy(ixf[:, s, :], ix[:, s, 0:2]))
                    link(TS(oh[:, s, :], k.c("iota8"), ixf[:, s, 0:1], None, ALU.is_equal))
                    link(STT(out=oh[:, s, :], in0=k.c("iota8"), scalar=ixf[:, s, 1:2], in1=oh[:, s, :],
                             op0=ALU.is_equal, op1=ALU.add))
                    dve.wait_ge(ex2_done, at)
                    link(TT(em[:, s, :], ex[:, s, :], oh[:, s, :], ALU.mult))
                    link(dve.tensor_reduce(sr[:, s, 0:1], em[:, s, :], AX.X, ALU.add))
                    link(dve.reciprocal(sr[:, s, 1:2], sr[:, s, 0:1]))
                    link(TS(em[:, s, :], em[:, s, :], sr[:, s, 1:2], 2.0, ALU.mult, ALU.mult))
                    TT(hw[:, s, :].rearrange("p (e r) -> p e r", e=E2),
                       ps[:, s, 256 + E2:256 + NRH].rearrange("p (e r) -> p e r", e=E2),
                       bc(em[:, s, :], 2, R2), ALU.mult).then_inc(hw_ready, 1)
                    if first and s == 1:
                        ranks(2, TILES)
                for s in S2:
                    at = it * 2 + s + 1
                    dve.wait_ge(base2_done, at)
                    dve.wait_ge(x2b_ready, at)
                    if not first:
                        dve.wait_ge(x3_out[s], it * 16)
                    TT(x3[:, s, :], pb[:, s, :], x2b[:, s, :], ALU.add).then_inc(x3_ready, 1)
                for s in S2:
                    fetch(it * 2 + s + 2, s)
                for s in S2:
                    at = it * 2 + s + 1
                    dve.wait_ge(x3h_kept, at)
                    tok = bass.ds((it * 2 + s) * P, P)
                    TT(k.x3l[:, :, tok], pt[:, s, :].rearrange("p (c t) -> p c t", c=KC),
                       k.x3h[:, :, tok].bitcast(F32), ALU.subtract).then_inc(x3l_kept, 1)
                assert link.n == PER, link.n
            peeled(dve, TILES // 2, body)
    k.end_phase(ctx)


HH = HK // 2
def project_phase(k, hh):
    nc, dram = k.nc, k.dram
    ctx = ExitStack()
    sb = lambda name, shape, dt=F32: k.sb(name, shape, dt, ctx)
    W4 = HH * HD
    tab = sb(f"rtab{hh}", [P, 4, TILES, HD])
    wraw = sb(f"wraw{hh}", [P, KC, W4])
    wh = sb(f"wh{hh}", [P, 2, KC, W4], F32R)
    wl = sb(f"wl{hh}", [P, 2, KC, W4], F32R)
    sq = sb(f"sq{hh}", [P, HH, HD])
    ss = sb(f"ss{hh}", [P, 2, HH])
    rt = sb(f"rt{hh}", [P, 2, HH])
    ri = sb(f"ri{hh}", [P, 4, HH])
    qc = sb(f"qc{hh}", [P, 4, W4])
    vs = qc[:, 2:4]
    qs = sb(f"qs{hh}", [P, 2, W4])
    pq = ctx.enter_context(nc.psum_tensor(f"pq{hh}", [P, 4, 512], F32))
    pt = ctx.enter_context(nc.psum_tensor(f"ptq{hh}", [P, 2, 512], F32))
    n = lambda name: k.sem(f"{name}{hh}")
    wraw_in = [n(f"wraw_in{c}_") for c in range(KC)]
    tab_in, whigh, wlow, proj_done, v_kept, ss_ready, qrt_ready = (
        n(x) for x in ("tab_in", "whigh", "wlow", "proj_done", "v_kept", "ss_ready", "qrt_ready"))
    parts_ready, sum_ready, q_ready, qT_done, qT_kept, ss_done = (
        n(x) for x in ("parts_ready", "sum_ready", "q_ready", "qT_done", "qT_kept", "ss_done"))
    v_out = [n("v_out_a"), n("v_out_b")]
    GROUPS = 2 + HH
    wsrc = dram["wqkv"]
    vdst = dram["vnew"].rearrange("h (t p) d -> h t p d", p=P)[hh]

    with nc.Block() as block:
        @block.sync
        def _(sp):
            for c in range(KC):
                sp.dma_start(wraw[:, c, :], wsrc[hh, 0, :, c, :]).then_inc(wraw_in[c], 16)
            sp.dma_start(tab[:].rearrange("p j t d -> p (j t d)"), dram["ropetab"]).then_inc(tab_in, 16)
            for j in range(1, GROUPS):
                for c in range(KC):
                    sp.wait_ge(wlow, (j - 1) * KC + c + 1)
                    sp.dma_start(wraw[:, c, :], wsrc[hh, j, :, c, :]).then_inc(wraw_in[c], 16)
                if j == 1:
                    for t in range(TILES):
                        sp.wait_ge(v_kept, t + 1)
                        sp.dma_start(vdst[t], vs[:, t % 2, :]).then_inc(v_out[t % 2], 16)
            for o in v_out:
                sp.wait_ge(o, 16 * TILES // 2)

        @block.tensor
        def _(pe):
            def project(slot, t, g):
                i = 0
                for c in range(KC):
                    if t == 0:
                        pe.wait_ge(wlow, g * KC + c + 1)
                    for x, w in ((k.x3h, wh), (k.x3h, wl), (k.x3l, wh)):
                        last = pe.matmul(pq[:, t % 4, :], x[:, c, t * P:(t + 1) * P], w[:, slot, c, :],
                                         start=(i == 0), stop=(i == 3 * KC - 1))
                        i += 1
                last.then_inc(proj_done, 1)

            def turn(t, r):
                pe.wait_ge(q_ready, r + 1)
                if not isinstance(r, int) or r >= 2:
                    pe.wait_ge(qT_kept, r - 1)
                for g in range(HH):
                    last = pe.transpose(pt[:, t % 2, g * P:(g + 1) * P], qc[:, t % 4, g * HD:(g + 1) * HD], k.c("ident"))
                last.then_inc(qT_done, 1)

            for t in range(TILES):
                if t >= 4:
                    pe.wait_ge(v_kept, t - 3)
                project(0, t, 0)

            def rotated(j, slot, k_group):
                for t in range(TILES):
                    r = j * TILES + t
                    if k_group and t < 4:
                        pe.wait_ge(v_kept, 5 + t)
                    else:
                        pe.wait_ge(parts_ready, r - 3)
                    project(slot, t, j + 1)
                    if not (k_group and t < 3):
                        turn((t - 3) % TILES, r - 3)
            rotated(0, 1, True)
            with pe.Fori(0, HH // 2) as i:
                for s in range(2):
                    rotated(i * 2 + s + 1, s, False)
            R = (1 + HH) * TILES
            for r in (R - 3, R - 2, R - 1):
                turn(r % TILES, r)

        @block.scalar
        def _(act):
            for t in range(TILES):
                act.wait_ge(proj_done, t + 1)
                if t >= 2:
                    act.wait_ge(v_out[t % 2], 16 * (t // 2))
                act.copy(vs[:, t % 2, :], pq[:, t % 4, :]).then_inc(v_kept, 1)

            def keep(t, r, group):
                act.wait_ge(qT_done, r + 1)
                dst = k.qkT[:, t * BPT:(t + 1) * BPT, bass.ds(group * HH, HH), :]
                act.copy(dst, pt[:, t % 2, :].rearrange("p (h b n) -> p b h n", h=HH, b=BPT)).then_inc(qT_kept, 1)

            def rotated(j, k_group):
                for t in range(TILES):
                    r = j * TILES + t
                    act.wait_ge(proj_done, TILES + r + 1)
                    if not (k_group and t < 2):
                        act.wait_ge(qrt_ready, r - 1)
                    for g in range(HH):
                        last = act.activation(sq[:, g], pq[:, t % 4, g * HD:(g + 1) * HD], ACT.Square,
                                              accum_out=ss[:, t % 2, g:g + 1])
                    last.then_inc(ss_done, 1)
                    act.wait_ge(ss_done, r + 1)
                    act.activation(rt[:, t % 2, :], ss[:, t % 2, :], ACT.Sqrt, scale=1.0 / HD, bias=k.c("eps")).then_inc(ss_ready, 1)
                    if not (k_group and t < 3):
                        keep((t - 3) % TILES, r - 3, j if t >= 3 else j - 1)
            rotated(0, True)
            with act.Fori(1, 1 + HH) as j:
                rotated(j, False)
            R = (1 + HH) * TILES
            for r in (R - 3, R - 2, R - 1):
                keep(r % TILES, r, HH)

        @block.vector
        def _(dve):
            def split(g, c):
                dve.wait_ge(wraw_in[c], g * 16 + 16)
                if c == 0 and (not isinstance(g, int) or g >= 2):
                    dve.wait_ge(proj_done, (g - 1) * TILES)
                high, low = (w[:, bass.ds(g % 2, 1), c, :].rearrange("p o n -> p (o n)") for w in (wh, wl))
                dve.tensor_copy(high, wraw[:, c, :]).then_inc(whigh, 1)
                dve.wait_ge(whigh, g * KC + c + 1)
                dve.tensor_tensor(low, wraw[:, c, :], high.bitcast(F32), ALU.subtract).then_inc(wlow, 1)

            for g in range(2):
                for c in range(KC):
                    split(g, c)
            dve.wait_ge(tab_in, 16)

            def scale(t, r):
                dve.wait_ge(sum_ready, r + 1)
                dve.wait_ge(qrt_ready, r + 1)
                v = qc[:, t % 4, :].rearrange("p (g d) -> p g d", d=HD)
                dve.tensor_tensor(v, v, bc(ri[:, t % 4, :], 2, HD), ALU.mult).then_inc(q_ready, 1)

            def rotated(j, k_group, more):
                cosw, sinw = (tab[:, 2], tab[:, 3]) if k_group else (tab[:, 0], tab[:, 1])
                for t in range(TILES):
                    r = j * TILES + t
                    dve.wait_ge(ss_ready, r + 1)
                    if not (k_group and t < 4):
                        dve.wait_ge(qT_done, r - 3)
                    elif t >= 2:
                        dve.wait_ge(v_out[t % 2], 16 * TILES // 2)
                    dve.reciprocal(ri[:, t % 4, :], rt[:, t % 2, :]).then_inc(qrt_ready, 1)
                    src = pq[:, t % 4, :].rearrange("p (g d) -> p g d", d=HD)
                    dst = qc[:, t % 4, :].rearrange("p (g d) -> p g d", d=HD)
                    dve.tensor_tensor(dst, src, bc(cosw[:, t], 1, HH), ALU.mult)
                    src2 = pq[:, t % 4, :].rearrange("p (g two f) -> p g two f", two=2, f=HD // 2)
                    dst2 = qs[:, t % 2, :].rearrange("p (g two f) -> p g two f", two=2, f=HD // 2)
                    for o in range(2):
                        last = dve.tensor_tensor(dst2[:, :, o], src2[:, :, 1 - o],
                                                 bc(sinw[:, t, o * HD // 2:(o + 1) * HD // 2], 1, HH), ALU.mult)
                    last.then_inc(parts_ready, 1)
                    if not (k_group and t < 1):
                        scale((t - 1) % TILES, r - 1)
                    if t < KC and more:
                        split(j + 2, t)
            rotated(0, True, True)
            with dve.Fori(1, HH) as j:
                rotated(j, False, True)
            rotated(HH, False, False)
            scale(TILES - 1, (1 + HH) * TILES - 1)

        @block.gpsimd
        def _(pool):
            def rotated(j):
                for t in range(TILES):
                    pool.wait_ge(parts_ready, j * TILES + t + 1)
                    pool.tensor_tensor(qc[:, t % 4, :], qc[:, t % 4, :], qs[:, t % 2, :], ALU.add).then_inc(sum_ready, 1)
            with pool.Fori(0, 1 + HH) as j:
                rotated(j)
    k.end_phase(ctx)


def attend_phase(k, hh):
    nc, dram = k.nc, k.dram
    ctx = ExitStack()
    sb = lambda name, shape, dt=F32: k.sb(f"{name}{hh}", shape, dt, ctx)
    n = lambda name: k.sem(f"{name}{hh}")
    SLOTS = NPP + 1
    CUT = 9
    CA, CB = CUT * PS, (SLOTS - CUT) * PS
    PA = PG + 2
    PA0 = (PG + NPP) // 2
    kidx = sb("kidx", [P, 2, PG], I32)
    vidx = sb("vidx", [P, 2, VC], I32)
    kqb = sb("kqb", [P, 2, SLOTS * HH + HH * G, PS])
    kb = kqb[:, :, 0:SLOTS * HH, :].rearrange("p s (j h) t -> p s j h t", h=HH)
    qb = kqb[:, :, SLOTS * HH:, :]
    vb = sb("vb", [P, 2, VC + 1, HH * HD])
    mask = sb("mask", [P, 2, KL])
    sm = sb("smax", [P, 2, KL])
    pm = sb("pm", [P, 4, KL])
    mxs = sb("mxs", [P, 2, 2])
    nmx = sb("nmx", [P, 2])
    rs = sb("rs", [P, 2])
    rv = sb("rv", [P, 2])
    pT = sb("pT", [P, 2, VC * P + P])
    sps = ctx.enter_context(nc.psum_tensor(f"sps{hh}", [P, 2, 2, 512], F32))
    tps = ctx.enter_context(nc.psum_tensor(f"tps{hh}", [P, 2, 512], F32))
    ops = ctx.enter_context(nc.psum_tensor(f"ops{hh}", [P, 2, 512], F32))
    mask_ready, vidx_ready, kq_ready = (
        n(x) for x in ("mask_ready", "vidx_ready", "kq_ready"))
    k_in = [n("k_in_a"), n("k_in_b")]
    kg_in = [n("kg_in_a"), n("kg_in_b")]
    v_in = [n("v_in_a"), n("v_in_b")]
    vn_in = [n("vn_in_a"), n("vn_in_b")]
    qk_done, max_a, max_done, nmx_ready, exp_done, rv_ready, p_ready, t_done, pT_kept, pv_done, o_kept = (
        n(x) for x in ("qk_done", "max_a", "max_done", "nmx_ready", "exp_done", "rv_ready", "p_ready", "t_done",
                       "pT_kept", "pv_done", "o_kept"))
    krows = dram[f"kpages{hh}"].rearrange("r d c -> (r d) c")
    kpages, vrows, vnew = dram[f"kpages{hh}"], dram[f"vrows{hh}"], dram["vnew"][hh]
    NU, BU = 2 * HH, 2

    passed = k.sem(f"passed_attend{hh}")

    def load_page(eng, b, s, j):
        page = eng.value_load(k.table[0:1, bass.ds(b * NPP + j, 1)], min_val=0, max_val=PAGES - 1)
        eng.dma_start(kb[:, s, j], kpages[bass.ds(page, 1)].rearrange("o p (h t) -> (o p) h t", h=HH)).then_inc(k_in[s], 16)

    with nc.Block() as block:
        @block.sync
        def _(sp):
            def body(i, first):
                for s in range(2):
                    b = i * 2 + s
                    if not first:
                        sp.wait_ge(qk_done, (b - 1) * HH)
                    for j in range(PA0 if first and s == 0 else PA, NPP):
                        load_page(sp, b, s, j)
                    if not first:
                        sp.wait_ge(pv_done, (b - 1) * HH)
                    sp.dma_start(vb[0:NS, s, VC, :], vnew[bass.ds(b * NS, NS), :]).then_inc(vn_in[s], 16)
            peeled(sp, NB // 2, body)

        @block.gpsimd
        def _(pool):
            def body(i, first):
                for s in range(2):
                    b = i * 2 + s
                    if not first:
                        pool.wait_ge(v_in[s], i * (16 * VC))
                        pool.wait_ge(kg_in[s], i * (16 * PG))
                    pool.tensor_copy(vidx[:, s, :], k.vrow[:, bass.ds(b * VC, VC)])
                    pool.tensor_copy(kidx[:, s, :], k.kpage[:, bass.ds(b * PG, PG)]).then_inc(vidx_ready, 1)
                    if not first:
                        pool.wait_ge(qk_done, (b - 1) * HH)
                        pool.sem_inc(passed, 1)
                    pool.wait_ge(vidx_ready, b + 1)
                    pool.sem_inc(passed, 1)
                    for j in range(PG):
                        pool.indirect_dma_start(kb[:, s, j].rearrange("p h t -> p (h t)"), None, krows,
                                                bass.IndirectOffsetOnAxis(kidx[:, s, j:j + 1], 0)).then_inc(kg_in[s], 16)
                    if not first:
                        lone_wait(pool, pv_done, (b - 1) * HH, passed)
                    for c in range(VC):
                        pool.indirect_dma_start(vb[:, s, c, :], None, vrows,
                                                bass.IndirectOffsetOnAxis(vidx[:, s, c:c + 1], 0)).then_inc(v_in[s], 16)
            peeled(pool, NB // 2, body)

        @block.tensor
        def _(pe):
            def scores(i, m, first):
                s, h, us = m // HH, m % HH, m % 2
                u = i * NU + m
                if h == 0:
                    pe.wait_ge(k_in[s], i * (16 * (NPP - PG)) + 16 * (NPP - PG))
                    pe.wait_ge(kg_in[s], i * (16 * PG) + 16 * PG)
                    pe.wait_ge(kq_ready, i * 2 + s + 1)
                if not (first and m < 2):
                    pe.wait_ge(max_done, u - 1)
                q = qb[:, s, h * G:(h + 1) * G, :].rearrange("p g n -> p (g n)")
                pe.matmul(sps[:, us, 0, 0:CA].rearrange("p (j t) -> p j t", t=PS), q, kb[:, s, 0:CUT, h, :],
                          start=True, stop=True)
                pe.matmul(sps[:, us, 1, 0:CB].rearrange("p (j t) -> p j t", t=PS), q, kb[:, s, CUT:, h, :],
                          start=True, stop=True).then_inc(qk_done, 1)

            def turn(m, u):
                us = m % 4
                pe.wait_ge(p_ready, u + 1)
                if not isinstance(u, int) or u > 0:
                    pe.wait_ge(pT_kept, u)
                for c in range(VC):
                    pe.transpose(tps[:, 0, c * P:(c + 1) * P], pm[:, us, c * P:(c + 1) * P], k.c("ident"))
                pe.transpose(tps[0:NS, 1, 0:P], pm[:, us, CL:KL], k.c("ident")).then_inc(t_done, 1)

            def values(i, m, u):
                s, h, us = m // HH, m % HH, m % 2
                if h == 0:
                    pe.wait_ge(v_in[s], i * (16 * VC) + 16 * VC)
                    pe.wait_ge(vn_in[s], i * 16 + 16)
                pe.wait_ge(pT_kept, u + 1)
                if not isinstance(u, int) or u >= 2:
                    pe.wait_ge(o_kept, u - 1)
                for c in range(VC):
                    pe.matmul(ops[:, us, 0:P], vb[:, s, c, h * HD:(h + 1) * HD], pT[:, us, c * P:(c + 1) * P],
                              start=(c == 0), stop=False)
                pe.matmul(ops[:, us, 0:P], vb[0:NS, s, VC, h * HD:(h + 1) * HD], pT[0:NS, us, VC * P:],
                          start=False, stop=True).then_inc(pv_done, 1)

            def body(i, first):
                for m in range(NU):
                    u = i * NU + m
                    scores(i, m, first)
                    if not (first and m < 2):
                        turn((m - 2) % NU, u - 2)
                    if not (first and m < 3):
                        values(i if m >= 3 else i - 1, (m - 3) % NU, u - 3)
            pe.wait_ge(mask_ready, 1)
            peeled(pe, NB // 2, body)
            U = NB * HH
            turn(NU - 2, U - 2)
            values(NB // 2 - 1, NU - 3, U - 3)
            turn(NU - 1, U - 1)
            values(NB // 2 - 1, NU - 2, U - 2)
            values(NB // 2 - 1, NU - 1, U - 1)

        @block.scalar
        def _(act):
            def keep(m, u):
                us = m % 2
                act.wait_ge(t_done, u + 1)
                if not isinstance(u, int) or u >= 2:
                    act.wait_ge(pv_done, u - 1)
                act.copy(pT[:, us, 0:CL], tps[:, 0, :])
                act.copy(pT[0:NS, us, CL:], tps[0:NS, 1, 0:P]).then_inc(pT_kept, 1)

            def fetch(b, s, upto=PA):
                if not isinstance(b, int) or b >= 2:
                    act.wait_ge(qk_done, (b - 1) * HH)
                for j in range(PG, upto):
                    load_page(act, b, s, j)

            fetch(0, 0, PA0)

            def body(i, first, last):
                for m in range(NU):
                    us, u = m % 2, i * NU + m
                    if m % HH == 1 and not (last and m > HH):
                        fetch(i * 2 + m // HH + 1, 1 - m // HH)
                    if not (first and m < 2):
                        keep((m - 2) % NU, u - 2)
                        act.wait_ge(rv_ready, u - 1)
                    act.wait_ge(nmx_ready, u + 1)
                    if not (first and m < 4):
                        act.wait_ge(t_done, u - 3)
                    act.activation(pm[:, m % 4, :], sm[:, us, :], ACT.Exp, bias=nmx[:, us:us + 1], scale=SCALE,
                                   accum_out=rs[:, us:us + 1]).then_inc(exp_done, 1)
            body(0, True, False)
            with act.Fori(1, NB // 2 - 1) as i:
                body(i, False, False)
            body(NB // 2 - 1, False, True)
            keep(NU - 2, NB * HH - 2)
            keep(NU - 1, NB * HH - 1)

        @block.vector
        def _(dve):
            dve.memset(mask[:], 0.0).then_inc(mask_ready, 1)
            dve.wait_ge(mask_ready, 1)

            def fetch(b, s):
                if not isinstance(b, int) or b >= 2:
                    dve.wait_ge(qk_done, (b - 1) * HH)
                dve.tensor_copy(kqb[:, s, NPP * HH:, :], k.qkT[:, bass.ds(b, 1)].rearrange("p o h n -> p (o h) n"))\
                    .then_inc(kq_ready, 1)
            fetch(0, 0)

            def body(i, first, last):
                for m in range(NU):
                    s, h, us = m // HH, m % HH, m % 2
                    u, b = i * NU + m, i * 2 + s
                    if h == 1 and not (last and s == 1):
                        fetch(b + 1, 1 - s)
                    if h == 0:
                        if not first:
                            dve.wait_ge(max_done, (b - 1) * HH)
                        dve.tensor_scalar(mask[:, s, 0:CL], k.c("iota512"), k.klen[:, bass.ds(b, 1)], NEG,
                                          ALU.is_ge, ALU.mult).then_inc(mask_ready, 1)
                        dve.wait_ge(mask_ready, b + 2)
                    dve.wait_ge(qk_done, u + 1)
                    if not (first and m < 2):
                        lone_wait(dve, exp_done, u - 1, passed)
                    dve.tensor_tensor_reduce(out=sm[:, us, 0:CA], in0=sps[:, us, 0, 0:CA], in1=mask[:, s, 0:CA], scale=1.0,
                                             scalar=-3e38, op0=ALU.add, op1=ALU.max, accum_out=mxs[:, us, 0:1]).then_inc(max_a, 1)
                    lone_wait(dve, max_a, u + 1, passed)
                    dve.tensor_tensor_reduce(out=sm[:, us, CA:KL], in0=sps[:, us, 1, 0:CB], in1=mask[:, s, CA:KL], scale=1.0,
                                             scalar=mxs[:, us, 0:1], op0=ALU.add, op1=ALU.max,
                                             accum_out=mxs[:, us, 1:2]).then_inc(max_done, 1)
                    dve.wait_ge(max_done, u + 1)
                    dve.tensor_scalar(nmx[:, us:us + 1], mxs[:, us, 1:2], -SCALE, None, ALU.mult).then_inc(nmx_ready, 1)
                    if not (first and m < 1):
                        scale((m - 1) % NU, u - 1)
                    if not (first and m < 3):
                        out(i if m >= 3 else i - 1, (m - 3) % NU, u - 3)

            def scale(m, u):
                us = m % 2
                dve.wait_ge(exp_done, u + 1)
                dve.reciprocal(rv[:, us:us + 1], rs[:, us:us + 1]).then_inc(rv_ready, 1)
                dve.wait_ge(rv_ready, u + 1)
                dve.tensor_scalar(pm[:, m % 4, :], pm[:, m % 4, :], rv[:, us:us + 1], None, ALU.mult).then_inc(p_ready, 1)

            def out(i, m, u):
                s, h, us = m // HH, m % HH, m % 2
                dve.wait_ge(pv_done, u + 1)
                dve.tensor_copy(k.qkT[:, bass.ds(i * 2 + s, 1), HH + G * h:HH + G * (h + 1), :].rearrange("p o g n -> p (o g n)"),
                                ops[:, us, 0:P]).then_inc(o_kept, 1)
            body(0, True, False)
            with dve.Fori(1, NB // 2 - 1) as i:
                body(i, False, False)
            body(NB // 2 - 1, False, True)
            scale(NU - 1, NB * HH - 1)
            for m in (NU - 3, NU - 2, NU - 1):
                out(NB // 2 - 1, m, NB * HH - NU + m)
    k.end_phase(ctx)


def output_phase(k, hh):
    nc, dram = k.nc, k.dram
    ctx = ExitStack()
    sb = lambda name, shape, dt=F32: k.sb(f"{name}{hh}", shape, dt, ctx)
    n = lambda name: k.sem(f"{name}{hh}")
    NH = HH * G
    worw = sb("worw", [P, 2, D])
    woh = sb("woh", [P, 2, D], F32R)
    wol = sb("wol", [P, 2, D], F32R)
    oh = sb("ohi", [P, 2, TOK], F32R)
    ol = sb("olo", [P, 2, TOK], F32R)
    if hh == 1:
        araw = sb("araw", [P, KC, E3 * R3])
    acc = ctx.enter_context(nc.psum_tensor(f"acc{hh}", [P, TILES, 512], F32))
    wo_in = [n("wo_in_a"), n("wo_in_b")]
    wo_high, wo_low, o_high, o_low, head_done, tile_done, y3_kept = (
        n(x) for x in ("wo_high", "wo_low", "o_high", "o_low", "head_done", "tile_done", "y3_kept"))
    wo = dram["wo"][hh]
    head_of = lambda h: k.qkT[:, :, bass.ds(h + HH, 1), :].rearrange("p b o n -> p b (o n)")

    if hh == 1:
        ex_high, wr_in, ex_low = n("ex_high"), n("wr_in"), n("ex_low")
        a_in = [n(f"a_in{c}_") for c in range(KC)]

    with nc.Block() as block:
        @block.sync
        def _(sp):
            def body(i, first):
                for s in range(2):
                    h = i * 2 + s
                    if not first:
                        sp.wait_ge(wo_low, h - 1)
                    sp.dma_start(worw[:, s, :], wo[bass.ds(h, 1)].rearrange("o p n -> (o p) n")).then_inc(wo_in[s], 16)
                if first and hh == 1:
                    for c in range(KC):
                        sp.dma_start(araw[:, c, :], dram["a3"][:, c, :]).then_inc(a_in[c], 16)
            peeled(sp, NH // 2, body)
            if hh == 1:
                sp.dma_start(k.wr[:], dram["wr"]).then_inc(wr_in, 16)
                sp.wait_ge(wr_in, 16)

        @block.scalar
        def _(act):
            def body(i, first):
                for s in range(2):
                    h = i * 2 + s
                    if not first:
                        act.wait_ge(head_done, h - 1)
                    act.copy(oh[:, s, :].rearrange("p (b n) -> p b n", n=NS), head_of(h)).then_inc(o_high, 1)
            peeled(act, NH // 2, body)
            if hh == 1:
                for c in range(KC):
                    act.wait_ge(a_in[c], 16)
                    act.copy(k.x3h[:, c, :], araw[:, c, :]).then_inc(ex_high, 1)

        @block.vector
        def _(dve):
            def body(i, first):
                for s in range(2):
                    h = i * 2 + s
                    dve.wait_ge(o_high, h + 1)
                    dve.tensor_tensor(ol[:, s, :].rearrange("p (b n) -> p b n", n=NS), head_of(h),
                                      oh[:, s, :].bitcast(F32).rearrange("p (b n) -> p b n", n=NS), ALU.subtract).then_inc(o_low, 1)
                    dve.wait_ge(wo_in[s], i * 16 + 16)
                    if not first:
                        dve.wait_ge(head_done, h - 1)
                    dve.tensor_copy(woh[:, s, :], worw[:, s, :]).then_inc(wo_high, 1)
                    dve.wait_ge(wo_high, h + 1)
                    dve.tensor_tensor(wol[:, s, :], worw[:, s, :], woh[:, s, :].bitcast(F32), ALU.subtract).then_inc(wo_low, 1)
            peeled(dve, NH // 2, body)
            if hh == 1:
                for c in range(KC):
                    dve.wait_ge(ex_high, c + 1)
                    dve.tensor_tensor(k.x3l[:, c, :], araw[:, c, :], k.x3h[:, c, :].bitcast(F32), ALU.subtract)\
                        .then_inc(ex_low, 1)
            for t in range(TILES):
                dve.wait_ge(tile_done, t + 1)
                if hh == 0:
                    dve.tensor_copy(k.y3[:, t, :], acc[:, t, :]).then_inc(y3_kept, 1)
                else:
                    dve.tensor_tensor(k.y3[:, t, :], k.y3[:, t, :], acc[:, t, :], ALU.add).then_inc(y3_kept, 1)

        @block.tensor
        def _(pe):
            def head(h, s, first, last_head):
                pe.wait_ge(o_low, h + 1)
                pe.wait_ge(wo_low, h + 1)
                for t in range(TILES):
                    cols = slice(t * P, (t + 1) * P)
                    for j, (o, w) in enumerate(((oh, woh), (oh, wol), (ol, woh))):
                        last = pe.matmul(acc[:, t, :], o[:, s, cols], w[:, s, :], start=(first and j == 0),
                                         stop=(last_head and j == 2))
                    if last_head:
                        last.then_inc(tile_done, 1)
                if not last_head:
                    last.then_inc(head_done, 1)
            head(0, 0, True, False)
            head(1, 1, False, False)
            with pe.Fori(1, NH // 2 - 1) as i:
                for s in range(2):
                    head(i * 2 + s, s, False, False)
            head(NH - 2, 0, False, False)
            head(NH - 1, 1, False, True)
    k.end_phase(ctx)


def expert_phase(k):
    nc, dram = k.nc, k.dram
    ctx = ExitStack()
    sb = lambda name, shape, dt=F32: k.sb(name, shape, dt, ctx)
    S2 = (0, 1)
    NRK = E3 * R3
    EC = NRK // P
    wr = k.wr
    ah, al = k.x3h, k.x3l
    bh, bl = (sb(x, [P, EC, D], F32R) for x in ("bh", "bl"))
    spare, at = k.qkT[:].rearrange("p b h n -> p (b h n)"), 0

    def over(pattern, columns, **sizes):
        nonlocal at
        at += columns
        return spare[:, at - columns:at].rearrange(pattern, **sizes)

    braw = over("p (c n) -> p c n", EC * D, n=D)
    hg = over("p (s n) -> p s n", 2 * NRK, s=2)
    y3T = over("p (s c t) -> p s c t", 2 * D, s=2, c=KC)
    yt, xres, fin = (over("p (s n) -> p s n", 2 * D, s=2) for _ in range(3))
    yh = sb("yh", [P, 2, KC, P], F32R)
    yl = sb("yl", [P, 2, KC, P], F32R)
    sc = sb("sc3", [P, 2, E3])
    m1 = sb("m1", [P, 2, 8])
    m2 = sb("m2", [P, 2, 8])
    r1 = sb("r1", [P, 2, E3])
    r2 = sb("r2", [P, 2, E3])
    pick = sb("pick", [P, 2, E3])
    nm = sb("nm3", [P, 2, 1])
    ex = sb("ex3", [P, 2, E3])
    gate = sb("gate", [P, 2, E3])
    sr = sb("sr3", [P, 2, 2])
    hgh = sb("hgh", [P, 2, EC, P], F32R)
    hgl = sb("hgl", [P, 2, EC, P], F32R)
    pa = ctx.enter_context(nc.psum_tensor("pa3", [P, 2, 512], F32))
    psc = ctx.enter_context(nc.psum_tensor("psc3", [P, 2, 512], F32))
    pr = ctx.enter_context(nc.psum_tensor("pr3", [P, 2, 2, 512], F32))
    b_high, b_low, yh_kept, yl_kept = (k.sem(x) for x in ("b_high", "b_low", "yh_kept", "yl_kept"))
    b_in = [k.sem("b_in0"), k.sem("b_in1")]
    half_high = [k.sem("half_high0"), k.sem("half_high1")]
    yt_ready, y3T_done, y3T_kept, sc_done, rank_done, nm3_ready, ex3_done, hg_ready = (
        k.sem(n) for n in ("yt_ready", "y3T_done", "y3T_kept", "sc_done", "rank_done", "nm3_ready", "ex3_done", "hg_ready"))
    fin_done, fin_ready, e_steps = (k.sem(n) for n in ("fin_done", "fin_ready", "e_steps"))
    half_done = [k.sem("half_done0"), k.sem("half_done1")]
    half_kept = [k.sem("half_kept0"), k.sem("half_kept1")]
    res_in = [k.sem("res_in0"), k.sem("res_in1")]
    out_done = [k.sem("out_done0"), k.sem("out_done1")]
    x3res = dram["x3res"].rearrange("(t p) d -> t p d", p=P)
    out = dram["out"].rearrange("(t p) d -> t p d", p=P)

    passed = k.sem("passed_expert")
    with nc.Block() as block:
        @block.sync
        def _(sp):
            for j in range(2):
                half = slice(j * EC // 2, (j + 1) * EC // 2)
                sp.dma_start(braw[:, half, :], dram["b3"][:, half, :]).then_inc(b_in[j], 16)

            def body(it, first):
                for s in S2:
                    t = it * 2 + s
                    if not first:
                        sp.wait_ge(fin_ready, t - 1)
                    sp.dma_start(xres[:, s, :], x3res[bass.ds(t, 1)].rearrange("o p d -> (o p) d")).then_inc(res_in[s], 16)
                for s in S2:
                    t = it * 2 + s
                    sp.wait_ge(fin_ready, t + 1)
                    sp.dma_start(out[bass.ds(t, 1)].rearrange("o p d -> (o p) d"), fin[:, s, :]).then_inc(out_done[s], 16)
            peeled(sp, TILES // 2, body)
            for s in S2:
                sp.wait_ge(out_done[s], 16 * TILES // 2)

        @block.gpsimd
        def _(pool):
            for c in range(EC):
                pool.wait_ge(b_high, c + 1)
                pool.tensor_tensor(bl[:, c, :], braw[:, c, :], bh[:, c, :].bitcast(F32), ALU.subtract).then_inc(b_low, 1)
            pool.wait_ge(yt_ready, 2)
            with pool.Fori(1, TILES // 2) as it:
                for s in S2:
                    t = it * 2 + s
                    pool.wait_ge(y3T_done, t - 1)
                    pool.tensor_copy(yt[:, s, :], k.y3[:].rearrange("p t d -> p (t d)")[:, bass.ds(t * D, D)]).then_inc(yt_ready, 1)

        @block.tensor
        def _(pe):
            def body(it, first):
                for s in S2:
                    at = it * 2 + s + 1
                    pe.wait_ge(yt_ready, at)
                    if not first:
                        pe.wait_ge(fin_ready, at - 2)
                    for c in range(KC):
                        last = pe.transpose(pa[:, s, c * P:(c + 1) * P], yt[:, s, c * P:(c + 1) * P], k.c("ident"))
                    last.then_inc(y3T_done, 1)
                for s in S2:
                    pe.wait_ge(y3T_kept, it * 2 + s + 1)
                    for c in range(KC):
                        last = pe.matmul(psc[:, s, 0:E3], y3T[:, s, c, :], wr[:, c, :], start=(c == 0), stop=(c == KC - 1))
                    last.then_inc(sc_done, 1)
                for s in S2:
                    pe.wait_ge(yl_kept, it * 2 + s + 1)
                    for j in range(2):
                        cols = slice(j * 512, (j + 1) * 512)
                        for c in range(KC):
                            for n, (y, a) in enumerate(((yh, ah), (yh, al), (yl, ah))):
                                last = pe.matmul(pr[:, s, j, :], y[:, s, c, :], a[:, c, cols], start=(c == 0 and n == 0),
                                                 stop=(c == KC - 1 and n == 2))
                    last.then_inc(rank_done, 1)
                for s in S2:
                    pe.wait_ge(hg_ready, it * 2 + s + 1)
                    for half in range(2):
                        for c in range(KC):
                            last = pe.transpose(pr[:, s, half, c * P:(c + 1) * P], hg[:, s, (half * KC + c) * P:(half * KC + c + 1) * P],
                                                k.c("ident"))
                        last.then_inc(half_done[s], 1)
                for s in S2:
                    for c in range(EC):
                        if first and s == 0:
                            pe.wait_ge(b_low, c + 1)
                        if c % KC == 0:
                            pe.wait_ge(half_kept[s], it * 2 + 1 + c // KC)
                        for n, (g, b) in enumerate(((hgh, bh), (hgh, bl), (hgl, bh))):
                            last = pe.matmul(pa[:, s, :], g[:, s, c, :], b[:, c, :], start=(c == 0 and n == 0),
                                             stop=(c == EC - 1 and n == 2))
                    last.then_inc(fin_done, 1)
            peeled(pe, TILES // 2, body)

        @block.scalar
        def _(act):
            for s in S2:
                act.copy(yt[:, s, :], k.y3[:, s, :]).then_inc(yt_ready, 1)

            def body(it, first):
                for s in S2:
                    act.wait_ge(y3T_done, it * 2 + s + 1)
                    act.copy(y3T[:, s].rearrange("p c t -> p (c t)"), pa[:, s, :]).then_inc(y3T_kept, 1)
                    act.copy(yh[:, s].rearrange("p c t -> p (c t)"), pa[:, s, :]).then_inc(yh_kept, 1)
                for s in S2:
                    act.wait_ge(nm3_ready, it * 2 + s + 1)
                    act.activation(ex[:, s, :], sc[:, s, :], ACT.Exp, bias=nm[:, s, :]).then_inc(ex3_done, 1)
                if first:
                    for c in range(EC):
                        if c % KC == 0:
                            act.wait_ge(b_in[c // KC], 16)
                        act.copy(bh[:, c, :], braw[:, c, :]).then_inc(b_high, 1)
                for s in S2:
                    for half in range(2):
                        act.wait_ge(half_done[s], it * 2 + half + 1)
                        act.copy(hgh[:, s, half * KC:(half + 1) * KC].rearrange("p c t -> p (c t)"), pr[:, s, half, :])\
                            .then_inc(half_high[s], 1)
            peeled(act, TILES // 2, body)

        @block.vector
        def _(dve):
            TS, TT = dve.tensor_scalar, dve.tensor_tensor
            PER = 20

            def parts(it):
                for s in S2:
                    dve.wait_ge(yh_kept, it * 2 + s + 1)
                    TT(yl[:, s], y3T[:, s], yh[:, s].bitcast(F32), ALU.subtract).then_inc(yl_kept, 1)

            def body(it, first):
                link = Link(dve, e_steps, it * PER)
                parts(it)
                for s in S2:
                    at = it * 2 + s + 1
                    dve.wait_ge(sc_done, at)
                    link(dve.tensor_copy(sc[:, s, :], psc[:, s, 0:E3]), passed)
                    link(dve.max(m1[:, s, :], sc[:, s, :]))
                    TS(nm[:, s, :], m1[:, s, 0:1], -1.0, None, ALU.mult).then_inc(nm3_ready, 1)
                    link(dve.match_replace(r1[:, s, :], m1[:, s, :], sc[:, s, :], NEG), passed)
                    link(dve.max(m2[:, s, :], r1[:, s, :]), passed)
                    link(dve.match_replace(r2[:, s, :], m2[:, s, :], r1[:, s, :], NEG))
                    link(TT(pick[:, s, :], r2[:, s, :], sc[:, s, :], ALU.not_equal))
                    dve.wait_ge(ex3_done, at)
                    link(TT(gate[:, s, :], ex[:, s, :], pick[:, s, :], ALU.mult))
                    link(dve.tensor_reduce(sr[:, s, 0:1], gate[:, s, :], AX.X, ALU.add))
                    link(dve.reciprocal(sr[:, s, 1:2], sr[:, s, 0:1]))
                    link(TS(gate[:, s, :], gate[:, s, :], sr[:, s, 1:2], 2.0, ALU.mult, ALU.mult))
                    dve.wait_ge(rank_done, at)
                    for j in range(2):
                        last = TT(hg[:, s, j * 512:(j + 1) * 512].rearrange("p (e r) -> p e r", r=R3),
                                  pr[:, s, j, :].rearrange("p (e r) -> p e r", r=R3),
                                  bc(gate[:, s, j * 32:(j + 1) * 32], 2, R3), ALU.mult)
                    last.then_inc(hg_ready, 1)
                for s in S2:
                    for half in range(2):
                        dve.wait_ge(half_high[s], it * 2 + half + 1)
                        chunks = slice(half * KC, (half + 1) * KC)
                        TT(hgl[:, s, chunks].rearrange("p c t -> p (c t)"), pr[:, s, half, :],
                           hgh[:, s, chunks].bitcast(F32).rearrange("p c t -> p (c t)"), ALU.subtract).then_inc(half_kept[s], 1)
                for s in S2:
                    at = it * 2 + s + 1
                    dve.wait_ge(fin_done, at)
                    dve.wait_ge(res_in[s], it * 16 + 16)
                    if not first:
                        dve.wait_ge(out_done[s], it * 16)
                    TT(fin[:, s, :], pa[:, s, :], xres[:, s, :], ALU.add).then_inc(fin_ready, 1)
                assert link.n == PER, link.n
            peeled(dve, TILES // 2, body)
    k.end_phase(ctx)


def build(nc, dram):
    with ExitStack() as ctx:
        k = Core(nc, ctx, dram)
        kpad = dram["kpad"]
        dram["toeplitz"] = lambda h: overlapped(kpad, h)
        k.cst = k.sb("cst", [P, CONST_N])
        k.x3h = k.sb("x3h", [P, KC, TOK], F32R)
        k.x3l = k.sb("x3l", [P, KC, TOK], F32R)
        k.table = k.sb("table", [1, NB * NPP], I32)
        k.kpage = k.sb("kpage", [P, NB * PG], I32)
        k.vrow = k.sb("vrow", [P, NB * VC], I32)
        k.klen = k.sb("klen", [P, NB])
        low = ExitStack()
        k.y0T = k.sb("y0T", [P, KC, TOK], F32, low)
        k.early = {"wup": k.sb("wup", [P, KC, D], F32, low), "gzw": k.sb("gzw", [P, KC, E0 + E0 * R0], F32, low),
                   "bias0": k.sb("bias0", [P, E0], F32, low), "lb0": k.sb("lb0", [E0 * R0, D], F32, low)}
        k.high, k.low = ({"wup": k.sb(f"wup_{x}", [P, KC, D], F32R, low),
                          "gzw": k.sb(f"gzw_{x}", [P, KC, E0 + E0 * R0], F32R, low)} for x in ("high", "low"))
        k.cond = k.sb("cond", [P, TILES], I32, low)
        k.wg = k.sb("wg", [P, TILES, NS], F32, low)
        s4_phase(k)
        k.hx = k.sb("hx", [P, TILES * D], F32, low)
        k.z1 = k.sb("z1", [P, TILES * R1], F32, low)
        k.hs1 = k.sb("hs1", [P, TILES * E1], F32, low)
        k.ds1 = k.sb("dl1", [P, TILES * E1], F32, low)
        mix_phase(k)
        route_phase(k)
        low.close()
        k.qkT = k.sb("qkT", [P, NB, HH + HH * G, NS])
        for hh in range(2):
            project_phase(k, hh)
            attend_phase(k, hh)
            if hh == 0:
                k.y3 = k.sb("y3", [P, TILES, D])
            else:
                k.wr = k.sb("wr", [P, KC, E3])
            output_phase(k, hh)
        expert_phase(k)
    return nc


def overlapped(kpad, h):
    return bass.AP(kpad.tensor, h * KPAD + 1, [[1, P], [KPAD, 2], [1, D]])


def layouts(i):
    a = np.ascontiguousarray
    rep = lambda v: np.broadcast_to(v, (P,) + v.shape)
    f = {n: np.asarray(v) for n, v in i.items()}
    d = {"cst": constants()}
    dup = lambda v: np.concatenate([v.T, v.T], 0)
    d["s4in"] = a(np.stack([rep(f["L0_cond_log_dt"]), dup(f["L0_cond_log_A_real"]), dup(f["L0_cond_A_imag"]),
                            dup(f["L0_cond_C"][:, :, 0]), dup(f["L0_cond_C"][:, :, 1])], 1))
    d["L0_cond_D"] = f["L0_cond_D"]
    d["len_b"] = a(rep(f["itok_B_78_3631"]))
    x = f["x"]
    d["x_rev"] = a(x.reshape(NB, NS, KC, P)[..., ::-1].transpose(3, 2, 1, 0))
    chunks = lambda m: a(m.reshape(-1, P, m.shape[1]).transpose(1, 0, 2))
    d["xtok"] = chunks(x.reshape(TOK, D))
    d["wup"] = chunks(f["L0_ffn_W_up"].T)
    d["gzw"] = chunks(np.concatenate([f["L0_ffn_gate_w"].T, f["L0_ffn_lora_A"].reshape(E0 * R0, D).T], 1))
    d["bias0"] = a(rep(f["L0_ffn_expert_bias"]))
    d["lb0"] = a(f["L0_ffn_lora_B"].transpose(0, 2, 1).reshape(E0 * R0, D))
    d["cond_b"] = a(np.repeat(f["itok_B_0_15"], NS).reshape(TILES, P).T)
    d["l1w"] = a(f["L1_cond_weights"].reshape(-1, NS))
    d["w1t"] = chunks(f["L1_ffn_W"].T)
    d["a1w"] = chunks(f["L1_ffn_A"])
    d["a1h"] = chunks(np.concatenate([f["L1_ffn_W"].T[:, :E1], f["L1_ffn_A"]], 1))
    d["b1"] = a(rep(f["L1_ffn_b"]))
    d["lime"] = a(rep(f["L1_ffn_LiMEs"]))
    d["lime_re"] = a(rep(f["L1_ffn_LiMEs"].T))
    d["bmat"] = f["L1_ffn_Bmat"]
    d["ids_b"] = a(rep(np.repeat(f["itok_B_3_7"], NS)))
    d["b2t"] = chunks(f["L2_cond_B"].reshape(AD2 * RC2, D).T)
    d["a2"] = a(f["L2_cond_A"].transpose(0, 2, 1).reshape(AD2 * RC2, D))
    d["rw2"] = chunks(np.concatenate([f["L2_ffn_W_router"].T, f["L2_ffn_lora_A"].reshape(E2 * R2, D).T], 1))
    d["w2t"] = chunks(f["L2_ffn_W_base"].T)
    d["lb2"] = a(f["L2_ffn_lora_B"].transpose(0, 2, 1).reshape(E2 * R2, D))
    d["bb2"] = a(rep(f["L2_ffn_b_base"]))
    d["start_b"] = a(np.repeat(f["itok_B_207_1644"], NS).reshape(TILES, P).T)
    swap = lambda v: np.concatenate([v[HD // 2:], v[:HD // 2]])
    qw, kw = f["L3_cond_q_norm_w"], f["L3_cond_k_norm_w"]
    d["norm_w"] = a(rep(np.stack([qw, swap(qw), kw, swap(kw)])))
    halves = lambda w: w.T.reshape(KC, P, 2, -1, HH * HD).transpose(2, 3, 1, 0, 4)
    d["wqkv"] = a(np.concatenate([halves(f["L3_cond_Wv"]), halves(f["L3_cond_Wk"]), halves(f["L3_cond_Wq"])], 1))
    d["table"] = a(f["itok_Bx16_0_63"].reshape(1, -1))
    d["table_b"] = a(np.repeat(f["itok_Bx16_0_63"].reshape(NB * CL // P, P // PS).T, PS, 0))
    d["pages_b"] = a(rep(f["itok_Bx16_0_63"][:, :PG].reshape(-1)))
    d["start_rep"] = a(rep(f["itok_B_207_1644"]))
    kc, vc = f["L3_cond_k_cache"], f["L3_cond_v_cache"]
    for hh in range(2):
        d[f"kpages{hh}"] = a(kc.reshape(PAGES, PS, 2, HH, HD)[:, :, hh].transpose(0, 3, 2, 1).reshape(PAGES, HD, HH * PS))
        d[f"vrows{hh}"] = a(vc.reshape(PAGES * PS, 2, HH * HD)[:, hh])
    d["wo"] = a(f["L3_cond_Wo"].T.reshape(2, HH * G, HD, D))
    d["wr"] = chunks(f["L3_ffn_Wr"].T)
    d["a3"] = chunks(f["L3_ffn_A"].reshape(E3 * R3, D).T)
    d["b3"] = chunks(f["L3_ffn_B"].transpose(0, 2, 1).reshape(E3 * R3, D))
    return d


SCRATCH = {"kpad": (NS, KPAD), "x3res": (TOK, D), "ropetab": (P, 4 * TILES * HD), "vnew": (2, TOK, HH * HD)}


def kernel(**inputs):
    import concourse.bacc as bacc
    from concourse.bass_utils import run_bass_kernel_spmd

    arrays = layouts(inputs)
    nc = bacc.Bacc("TRN2", target_bir_lowering=False, num_devices=1)
    dram = {n: nc.dram_tensor(f"in_{n}", v.shape, mybir.dt.from_np(v.dtype), kind="ExternalInput").ap()
            for n, v in arrays.items()}
    for n, shape in SCRATCH.items():
        dram[n] = nc.dram_tensor(f"scratch_{n}", shape, F32, kind="Internal").ap()
    dram["out"] = nc.dram_tensor("out", (TOK, D), F32, kind="ExternalOutput").ap()
    build(nc, dram)
    r = run_bass_kernel_spmd(nc, [{f"in_{n}": v for n, v in arrays.items()}], core_ids=[0])
    return r.results[0]["out"].reshape(NB, NS, D)
```
